# Optimizing a Trainium2 kernel written in Bass

```python
import numpy as np
import jax
import jax.numpy as jnp

def _softmax(x, axis=-1):
    return jax.nn.softmax(x, axis=axis)

def _gelu(x):
    return jax.nn.gelu(x, approximate=True)

def _silu(x):
    return jax.nn.silu(x)

def _sigmoid(x):
    return jax.nn.sigmoid(x)

def _layernorm(x, axis=-1, eps=1e-05):
    m = jnp.mean(x, axis=axis, keepdims=True)
    v = jnp.var(x, axis=axis, keepdims=True)
    return (x - m) / jnp.sqrt(v + eps)

def _scatter_add(tgt, idx, src, axis=0):
    return tgt.at[idx].add(src)

def _segment_sum(src, seg, n):
    return jax.ops.segment_sum(src, seg, n)
kernel_name = 'mk_seq_preln_d4_jaxref_r8_15c01c'

def setup_inputs(seed: int=0):
    np.random.seed(seed)
    _w = jnp.asarray

    def _L0_attn_setup():
        import jax, jax.numpy as jnp
        import numpy as np
        from jax import lax
        B, L, D_MODEL = (2, 512, 128)
        D_STATE, D_CONV, EXPAND = (16, 4, 2)
        D_INNER = D_MODEL * EXPAND
        DT_RANK = (D_MODEL + 15) // 16
        EPS = 1e-05

        def _dt_bias(k):
            u = jax.random.uniform(k, (D_INNER,), dtype=jnp.float32)
            dt = jnp.exp(u * (np.log(0.1) - np.log(0.001)) + np.log(0.001))
            dt = jnp.clip(dt, 0.0001)
            return dt + jnp.log(-jnp.expm1(-dt))

        def _init_A_log():
            a = jnp.arange(1, D_STATE + 1, dtype=jnp.float32)
            return jnp.log(jnp.broadcast_to(a[None, :], (D_INNER, D_STATE)))

        def _causal_dwconv(x, w, b):
            xc = lax.conv_general_dilated(x.transpose(0, 2, 1), w, (1,), [(D_CONV - 1, 0)], dimension_numbers=('NCH', 'OIH', 'NCH'), feature_group_count=D_INNER)
            return (xc + b[None, :, None]).transpose(0, 2, 1)

        def _mamba_dir(xi, z, conv_w, conv_b, xproj_w, dtproj_w, dtproj_b, A_log, Dp):
            xc = jax.nn.silu(_causal_dwconv(xi, conv_w, conv_b))
            x_dbl = jnp.einsum('bld,ed->ble', xc, xproj_w)
            dt = x_dbl[..., :DT_RANK]
            Bm = x_dbl[..., DT_RANK:DT_RANK + D_STATE]
            Cm = x_dbl[..., DT_RANK + D_STATE:]
            delta = jax.nn.softplus(jnp.einsum('blr,dr->bld', dt, dtproj_w) + dtproj_b)
            A = -jnp.exp(A_log)

            def step(h, inp):
                xt, dlt, bt, ct = inp
                h = jnp.exp(dlt[:, :, None] * A) * h + (dlt * xt)[:, :, None] * bt[:, None, :]
                return (h, jnp.einsum('bdn,bn->bd', h, ct))
            h0 = jnp.zeros((xc.shape[0], D_INNER, D_STATE), xc.dtype)
            xs = (xc.transpose(1, 0, 2), delta.transpose(1, 0, 2), Bm.transpose(1, 0, 2), Cm.transpose(1, 0, 2))
            _, ys = lax.scan(step, h0, xs)
            y = ys.transpose(1, 0, 2) + Dp * xc
            return y * jax.nn.silu(z)
        key = jax.random.key(seed)
        ks = jax.random.split(key, 16)

        def g(i, shape, scale=0.02):
            return jax.random.normal(ks[i], shape, dtype=jnp.float32) * scale
        return {'x': jax.random.normal(ks[0], (B, L, D_MODEL), dtype=jnp.float32), 'norm_w': jnp.ones((D_MODEL,), jnp.float32), 'in_proj_w': g(1, (2 * D_INNER, D_MODEL)), 'out_proj_w': g(2, (D_MODEL, D_INNER)), 'conv_w_f': g(3, (D_INNER, 1, D_CONV), 0.1), 'conv_b_f': jnp.zeros((D_INNER,), jnp.float32), 'xproj_w_f': g(4, (DT_RANK + 2 * D_STATE, D_INNER)), 'dtproj_w_f': g(5, (D_INNER, DT_RANK), 0.1), 'dtproj_b_f': _dt_bias(ks[6]), 'A_log_f': _init_A_log(), 'D_f': jnp.ones((D_INNER,), jnp.float32), 'conv_w_b': g(7, (D_INNER, 1, D_CONV), 0.1), 'conv_b_b': jnp.zeros((D_INNER,), jnp.float32), 'xproj_w_b': g(8, (DT_RANK + 2 * D_STATE, D_INNER)), 'dtproj_w_b': g(9, (D_INNER, DT_RANK), 0.1), 'dtproj_b_b': _dt_bias(ks[10]), 'A_log_b': _init_A_log(), 'D_b': jnp.ones((D_INNER,), jnp.float32)}
    _L0_attn_in = _L0_attn_setup()

    def _L0_ffn_setup():
        import jax, jax.numpy as jnp
        import numpy as np
        DIM = 128
        E = 16
        TOPK = 2
        G = 4
        TOPK_G = 2
        INTER = 64
        N_SHARED = 2
        ROUTE_SCALE = 1.0

        def _gate(xf, gate_w, gate_b):
            scores = xf @ gate_w.T
            scores = jax.nn.softmax(scores.astype(jnp.float32), axis=-1)
            orig = scores
            scores = scores + gate_b
            T = xf.shape[0]
            sg = scores.reshape(T, G, E // G)
            group_scores = jax.lax.top_k(sg, 2)[0].sum(-1)
            _, gidx = jax.lax.top_k(group_scores, TOPK_G)
            keep = jax.nn.one_hot(gidx, G).sum(axis=1) > 0
            sg = jnp.where(keep[:, :, None], sg, -jnp.inf)
            scores = sg.reshape(T, E)
            _, idx = jax.lax.top_k(scores, TOPK)
            weights = jnp.take_along_axis(orig, idx, axis=1)
            weights = (weights * ROUTE_SCALE).astype(xf.dtype)
            return (weights, idx)
        key = jax.random.key(seed)
        ks = jax.random.split(key, 16)
        s = lambda fan_in: 1.0 / np.sqrt(fan_in)
        inp = {'x': jax.random.normal(ks[0], (4, 128, DIM), dtype=jnp.float32), 'gate_w': jax.random.normal(ks[1], (E, DIM), dtype=jnp.float32) * s(DIM), 'gate_b': jnp.zeros((E,), dtype=jnp.float32), 'We1': jax.random.normal(ks[2], (E, DIM, INTER), dtype=jnp.float32) * s(DIM), 'be1': jnp.zeros((E, INTER), dtype=jnp.float32), 'We2': jax.random.normal(ks[3], (E, INTER, DIM), dtype=jnp.float32) * s(INTER), 'be2': jnp.zeros((E, DIM), dtype=jnp.float32), 'We3': jax.random.normal(ks[4], (E, DIM, INTER), dtype=jnp.float32) * s(DIM), 'be3': jnp.zeros((E, INTER), dtype=jnp.float32), 'ws1': jax.random.normal(ks[5], (DIM, N_SHARED * INTER), dtype=jnp.float32) * s(DIM), 'bs1': jnp.zeros((N_SHARED * INTER,), dtype=jnp.float32), 'ws2': jax.random.normal(ks[6], (N_SHARED * INTER, DIM), dtype=jnp.float32) * s(N_SHARED * INTER), 'bs2': jnp.zeros((DIM,), dtype=jnp.float32), 'ws3': jax.random.normal(ks[7], (DIM, N_SHARED * INTER), dtype=jnp.float32) * s(DIM), 'bs3': jnp.zeros((N_SHARED * INTER,), dtype=jnp.float32)}
        return inp
    _L0_ffn_in = _L0_ffn_setup()

    def _L1_attn_setup():
        import jax, jax.numpy as jnp
        import numpy as np
        import math
        B, S, D, H, DK = (4, 256, 128, 16, 64)
        NUM_BUCKETS, MAX_DISTANCE = (32, 128)

        def _relative_position_bucket(relative_position, num_buckets=NUM_BUCKETS, max_distance=MAX_DISTANCE):
            num_buckets //= 2
            buckets = (relative_position > 0).astype(jnp.int32) * num_buckets
            rp = jnp.abs(relative_position)
            max_exact = num_buckets // 2
            is_small = rp < max_exact
            rp_large = max_exact + (jnp.log(jnp.maximum(rp, 1).astype(jnp.float32) / max_exact) / math.log(max_distance / max_exact) * (num_buckets - max_exact)).astype(jnp.int32)
            rp_large = jnp.minimum(rp_large, num_buckets - 1)
            return buckets + jnp.where(is_small, rp, rp_large)

        def compute_bias(query_length, key_length, rel_bias_table):
            ctx = jnp.arange(query_length)[:, None]
            mem = jnp.arange(key_length)[None, :]
            buckets = _relative_position_bucket(mem - ctx)
            values = rel_bias_table[buckets]
            return jnp.transpose(values, (2, 0, 1))[None]
        key = jax.random.key(seed)
        ks = jax.random.split(key, 6)
        return {'hidden_states': jax.random.normal(ks[0], (B, S, D), dtype=jnp.float32), 'Wq': jax.random.normal(ks[1], (D, H * DK), dtype=jnp.float32) * (D * DK) ** (-0.5), 'Wk': jax.random.normal(ks[2], (D, H * DK), dtype=jnp.float32) * D ** (-0.5), 'Wv': jax.random.normal(ks[3], (D, H * DK), dtype=jnp.float32) * D ** (-0.5), 'Wo': jax.random.normal(ks[4], (H * DK, D), dtype=jnp.float32) * (H * DK) ** (-0.5), 'rel_bias_table': jax.random.normal(ks[5], (NUM_BUCKETS, H), dtype=jnp.float32) * (H * DK) ** (-0.5)}
    _L1_attn_in = _L1_attn_setup()

    def _L1_ffn_setup():
        import jax, jax.numpy as jnp
        import numpy as np
        TOP_K = 2
        EPS = 1e-06
        key = jax.random.key(seed)
        ks = jax.random.split(key, 6)
        B_, T, D = (8, 256, 128)
        E, R_ = (8, 16)
        scale = 1.0 / np.sqrt(D)
        x = jax.random.normal(ks[0], (B_, T, D), dtype=jnp.float32)
        W = jax.random.normal(ks[1], (D, D), dtype=jnp.float32) * scale
        b = jax.random.normal(ks[2], (D,), dtype=jnp.float32)
        R = jax.random.normal(ks[3], (E, D), dtype=jnp.float32) * scale
        A = jax.random.normal(ks[4], (E, R_, D), dtype=jnp.float32) * scale
        B = jax.random.normal(ks[5], (D, R_), dtype=jnp.float32)[None] * jnp.ones((E, 1, 1), jnp.float32)
        B = jax.random.normal(ks[5], (E, D, R_), dtype=jnp.float32) * (1.0 / np.sqrt(R_))
        return {'x': x, 'W': W, 'b': b, 'R': R, 'A': A, 'B': B}
    _L1_ffn_in = _L1_ffn_setup()

    def _L2_attn_setup():
        import jax, jax.numpy as jnp
        import numpy as np
        D_MODEL = 128
        NUM_HEADS = 16
        D_K = D_MODEL // NUM_HEADS
        THETA = 10000.0

        def _rope(x, positions):
            d = x.shape[-1]
            inv_freq = THETA ** (-jnp.arange(0, d, 2, dtype=jnp.float32) / d)
            ang = positions[:, :, None].astype(jnp.float32) * inv_freq[None, None, :]
            cos = jnp.cos(ang)[:, None, :, :]
            sin = jnp.sin(ang)[:, None, :, :]
            x1 = x[..., 0::2]
            x2 = x[..., 1::2]
            r1 = x1 * cos - x2 * sin
            r2 = x1 * sin + x2 * cos
            out = jnp.stack([r1, r2], axis=-1).reshape(x.shape)
            return out
        key = jax.random.key(seed)
        k1, k2, k3 = jax.random.split(key, 3)
        B, S = (4, 256)
        x = jax.random.normal(k1, (B, S, D_MODEL), dtype=jnp.float32)
        W_qkv = jax.random.normal(k2, (3 * D_MODEL, D_MODEL), dtype=jnp.float32) * (1.0 / np.sqrt(D_MODEL))
        W_o = jax.random.normal(k3, (D_MODEL, D_MODEL), dtype=jnp.float32) * (1.0 / np.sqrt(D_MODEL))
        return {'x': x, 'W_qkv': W_qkv, 'W_o': W_o}
    _L2_attn_in = _L2_attn_setup()

    def _L2_ffn_setup():
        import jax, jax.numpy as jnp
        import numpy as np
        from math import sqrt
        B, S, D, H, E, K, FF = (2, 128, 128, 16, 8, 2, 512)
        HD = D // H
        EPS = 1e-05

        def _rope_cache(seq_len, hd):
            inv_freq = 1.0 / 10000.0 ** (jnp.arange(0, hd, 2, dtype=jnp.float32) / hd)
            t = jnp.arange(seq_len, dtype=jnp.float32)
            freqs = t[:, None] * inv_freq[None, :]
            emb = jnp.concatenate([freqs, freqs], axis=-1)
            return (jnp.cos(emb), jnp.sin(emb))

        def _rotate_half(x):
            x1, x2 = jnp.split(x, 2, axis=-1)
            return jnp.concatenate([-x2, x1], axis=-1)

        def _layernorm(x, g, b):
            m = jnp.mean(x, axis=-1, keepdims=True)
            v = jnp.var(x, axis=-1, keepdims=True)
            return (x - m) * jax.lax.rsqrt(v + EPS) * g + b

        def _forward(x, Wq, bq, Wk, bk, Wv, bv, Wo, bo, Wg, bg, W1, b1, W2, b2, g1, be1, g2, be2):
            bsz, seq, d = x.shape
            q = (x @ Wq + bq).reshape(bsz, seq, H, HD).transpose(0, 2, 1, 3)
            k = (x @ Wk + bk).reshape(bsz, seq, H, HD).transpose(0, 2, 1, 3)
            v = (x @ Wv + bv).reshape(bsz, seq, H, HD).transpose(0, 2, 1, 3)
            cos, sin = _rope_cache(seq, HD)
            cos = cos[None, None]
            sin = sin[None, None]
            q = q * cos + _rotate_half(q) * sin
            k = k * cos + _rotate_half(k) * sin
            scores = jnp.einsum('bhqd,bhkd->bhqk', q, k) / sqrt(HD)
            attn = jax.nn.softmax(scores, axis=-1)
            ao = jnp.einsum('bhqk,bhkd->bhqd', attn, v)
            ao = ao.transpose(0, 2, 1, 3).reshape(bsz, seq, d)
            attn_out = ao @ Wo + bo
            x1 = _layernorm(x + attn_out, g1, be1)
            gate_logits = x1 @ Wg + bg
            gate_probs = jax.nn.softmax(gate_logits, axis=-1)
            topk_p, topk_i = jax.lax.top_k(gate_probs, K)
            topk_p = topk_p / jnp.sum(topk_p, axis=-1, keepdims=True)
            comb = jnp.sum(jax.nn.one_hot(topk_i, E, dtype=x.dtype) * topk_p[..., None], axis=-2)
            h = jax.nn.gelu(jnp.einsum('bsd,edf->bsef', x1, W1) + b1, approximate=False)
            y = jnp.einsum('bsef,efd->bsed', h, W2) + b2
            moe_out = jnp.einsum('bse,bsed->bsd', comb, y)
            return _layernorm(x1 + moe_out, g2, be2)
        key = jax.random.key(seed)
        ks = jax.random.split(key, 20)
        std = 0.02
        p = lambda k, sh: jax.random.normal(k, sh, dtype=jnp.float32) * std
        return {'x': jax.random.normal(ks[0], (B, S, D), dtype=jnp.float32), 'Wq': p(ks[1], (D, D)), 'bq': jnp.zeros((D,), jnp.float32), 'Wk': p(ks[2], (D, D)), 'bk': jnp.zeros((D,), jnp.float32), 'Wv': p(ks[3], (D, D)), 'bv': jnp.zeros((D,), jnp.float32), 'Wo': p(ks[4], (D, D)), 'bo': jnp.zeros((D,), jnp.float32), 'Wg': p(ks[5], (D, E)), 'bg': jnp.zeros((E,), jnp.float32), 'W1': p(ks[6], (E, D, FF)), 'b1': jnp.zeros((E, FF), jnp.float32), 'W2': p(ks[7], (E, FF, D)), 'b2': jnp.zeros((E, D), jnp.float32), 'g1': jnp.ones((D,), jnp.float32), 'be1': jnp.zeros((D,), jnp.float32), 'g2': jnp.ones((D,), jnp.float32), 'be2': jnp.zeros((D,), jnp.float32)}
    _L2_ffn_in = _L2_ffn_setup()

    def _L3_attn_setup():
        import jax, jax.numpy as jnp
        import numpy as np
        LN_EPS = 1e-05
        U_T = 1.0
        key = jax.random.key(seed)
        B, L, D, H = (2, 256, 128, 16)
        dk = D // H
        ks = jax.random.split(key, 4)
        x = jax.random.normal(ks[0], (B, L, D), jnp.float32)
        W_qkv = jax.random.normal(ks[1], (3 * D, D), jnp.float32) / np.sqrt(D)
        W_o = jax.random.normal(ks[2], (D, D), jnp.float32) / np.sqrt(D)
        W_LTM = jax.random.normal(ks[3], (H, dk, dk), jnp.float32) * 0.5
        return {'x': x, 'W_qkv': W_qkv, 'W_o': W_o, 'W_LTM': W_LTM, 'V_gs': jnp.zeros((H,), jnp.float32), 'V_T0': jnp.zeros((H,), jnp.float32), 'beta_tau': jnp.ones((H,), jnp.float32), 'beta_gm': jnp.ones((H,), jnp.float32) * 0.1, 'C_ch': jnp.ones((H,), jnp.float32), 'gamma': jnp.ones((H,), jnp.float32) * 0.1, 'alpha_ppd': jnp.ones((1,), jnp.float32), 'IC_threshold': jnp.ones((1,), jnp.float32)}
    _L3_attn_in = _L3_attn_setup()

    def _L3_ffn_setup():
        import jax, jax.numpy as jnp
        import numpy as np
        DIM = 128
        HID = 256
        E = 8
        K = 2
        R = 16
        B_, S_ = (2, 128)

        def _lora_in(xf, W, b, A, B):
            base = jnp.einsum('td,ehd->teh', xf, W)
            low = jnp.einsum('ter,ehr->teh', jnp.einsum('td,erd->ter', xf, A), B)
            return base + low + b

        def _lora_out(g, W, b, A, B):
            base = jnp.einsum('teh,edh->ted', g, W)
            low = jnp.einsum('ter,edr->ted', jnp.einsum('teh,erh->ter', g, A), B)
            return base + low + b
        key = jax.random.key(seed)
        ks = jax.random.split(key, 14)
        n = lambda k, shape, scale: jax.random.normal(k, shape, jnp.float32) * scale
        inp = {'x': jax.random.normal(ks[0], (B_, S_, DIM), jnp.float32), 'Wg': n(ks[1], (E, DIM), DIM ** (-0.5)), 'W1': n(ks[2], (E, HID, DIM), DIM ** (-0.5)), 'b1': jnp.zeros((E, HID), jnp.float32), 'A1': n(ks[3], (E, R, DIM), DIM ** (-0.5)), 'B1': n(ks[4], (E, HID, R), 0.01), 'W2': n(ks[5], (E, DIM, HID), HID ** (-0.5)), 'b2': jnp.zeros((E, DIM), jnp.float32), 'A2': n(ks[6], (E, R, HID), HID ** (-0.5)), 'B2': n(ks[7], (E, DIM, R), 0.01), 'W3': n(ks[8], (E, HID, DIM), DIM ** (-0.5)), 'b3': jnp.zeros((E, HID), jnp.float32), 'A3': n(ks[9], (E, R, DIM), DIM ** (-0.5)), 'B3': n(ks[10], (E, HID, R), 0.01)}
        return inp
    _L3_ffn_in = _L3_ffn_setup()
    _d = {'L0_attn_x': _L0_attn_in['x'], 'L0_attn_norm_w': _L0_attn_in['norm_w'], 'L0_attn_in_proj_w': _L0_attn_in['in_proj_w'], 'L0_attn_out_proj_w': _L0_attn_in['out_proj_w'], 'L0_attn_conv_w_f': _L0_attn_in['conv_w_f'], 'L0_attn_conv_b_f': _L0_attn_in['conv_b_f'], 'L0_attn_xproj_w_f': _L0_attn_in['xproj_w_f'], 'L0_attn_dtproj_w_f': _L0_attn_in['dtproj_w_f'], 'L0_attn_dtproj_b_f': _L0_attn_in['dtproj_b_f'], 'L0_attn_A_log_f': _L0_attn_in['A_log_f'], 'L0_attn_D_f': _L0_attn_in['D_f'], 'L0_attn_conv_w_b': _L0_attn_in['conv_w_b'], 'L0_attn_conv_b_b': _L0_attn_in['conv_b_b'], 'L0_attn_xproj_w_b': _L0_attn_in['xproj_w_b'], 'L0_attn_dtproj_w_b': _L0_attn_in['dtproj_w_b'], 'L0_attn_dtproj_b_b': _L0_attn_in['dtproj_b_b'], 'L0_attn_A_log_b': _L0_attn_in['A_log_b'], 'L0_attn_D_b': _L0_attn_in['D_b'], 'L0_ffn_gate_w': _L0_ffn_in['gate_w'], 'L0_ffn_gate_b': _L0_ffn_in['gate_b'], 'L0_ffn_We1': _L0_ffn_in['We1'], 'L0_ffn_be1': _L0_ffn_in['be1'], 'L0_ffn_We2': _L0_ffn_in['We2'], 'L0_ffn_be2': _L0_ffn_in['be2'], 'L0_ffn_We3': _L0_ffn_in['We3'], 'L0_ffn_be3': _L0_ffn_in['be3'], 'L0_ffn_ws1': _L0_ffn_in['ws1'], 'L0_ffn_bs1': _L0_ffn_in['bs1'], 'L0_ffn_ws2': _L0_ffn_in['ws2'], 'L0_ffn_bs2': _L0_ffn_in['bs2'], 'L0_ffn_ws3': _L0_ffn_in['ws3'], 'L0_ffn_bs3': _L0_ffn_in['bs3'], 'L1_attn_Wq': _L1_attn_in['Wq'], 'L1_attn_Wk': _L1_attn_in['Wk'], 'L1_attn_Wv': _L1_attn_in['Wv'], 'L1_attn_Wo': _L1_attn_in['Wo'], 'L1_attn_rel_bias_table': _L1_attn_in['rel_bias_table'], 'L1_ffn_W': _L1_ffn_in['W'], 'L1_ffn_b': _L1_ffn_in['b'], 'L1_ffn_R': _L1_ffn_in['R'], 'L1_ffn_A': _L1_ffn_in['A'], 'L1_ffn_B': _L1_ffn_in['B'], 'L2_attn_W_qkv': _L2_attn_in['W_qkv'], 'L2_attn_W_o': _L2_attn_in['W_o'], 'L2_ffn_Wq': _L2_ffn_in['Wq'], 'L2_ffn_bq': _L2_ffn_in['bq'], 'L2_ffn_Wk': _L2_ffn_in['Wk'], 'L2_ffn_bk': _L2_ffn_in['bk'], 'L2_ffn_Wv': _L2_ffn_in['Wv'], 'L2_ffn_bv': _L2_ffn_in['bv'], 'L2_ffn_Wo': _L2_ffn_in['Wo'], 'L2_ffn_bo': _L2_ffn_in['bo'], 'L2_ffn_Wg': _L2_ffn_in['Wg'], 'L2_ffn_bg': _L2_ffn_in['bg'], 'L2_ffn_W1': _L2_ffn_in['W1'], 'L2_ffn_b1': _L2_ffn_in['b1'], 'L2_ffn_W2': _L2_ffn_in['W2'], 'L2_ffn_b2': _L2_ffn_in['b2'], 'L2_ffn_g1': _L2_ffn_in['g1'], 'L2_ffn_be1': _L2_ffn_in['be1'], 'L2_ffn_g2': _L2_ffn_in['g2'], 'L2_ffn_be2': _L2_ffn_in['be2'], 'L3_attn_W_qkv': _L3_attn_in['W_qkv'], 'L3_attn_W_o': _L3_attn_in['W_o'], 'L3_attn_W_LTM': _L3_attn_in['W_LTM'], 'L3_attn_V_gs': _L3_attn_in['V_gs'], 'L3_attn_V_T0': _L3_attn_in['V_T0'], 'L3_attn_beta_tau': _L3_attn_in['beta_tau'], 'L3_attn_beta_gm': _L3_attn_in['beta_gm'], 'L3_attn_C_ch': _L3_attn_in['C_ch'], 'L3_attn_gamma': _L3_attn_in['gamma'], 'L3_attn_alpha_ppd': _L3_attn_in['alpha_ppd'], 'L3_attn_IC_threshold': _L3_attn_in['IC_threshold'], 'L3_ffn_Wg': _L3_ffn_in['Wg'], 'L3_ffn_W1': _L3_ffn_in['W1'], 'L3_ffn_b1': _L3_ffn_in['b1'], 'L3_ffn_A1': _L3_ffn_in['A1'], 'L3_ffn_B1': _L3_ffn_in['B1'], 'L3_ffn_W2': _L3_ffn_in['W2'], 'L3_ffn_b2': _L3_ffn_in['b2'], 'L3_ffn_A2': _L3_ffn_in['A2'], 'L3_ffn_B2': _L3_ffn_in['B2'], 'L3_ffn_W3': _L3_ffn_in['W3'], 'L3_ffn_b3': _L3_ffn_in['b3'], 'L3_ffn_A3': _L3_ffn_in['A3'], 'L3_ffn_B3': _L3_ffn_in['B3']}
    _x0 = _d['L0_attn_x']
    _d['L0_attn_x'] = jax.random.normal(jax.random.fold_in(jax.random.key(seed), 1), (8, 512, 128), dtype=_x0.dtype)
    del _x0
    return _d

def reference(L0_attn_x, L0_attn_norm_w, L0_attn_in_proj_w, L0_attn_out_proj_w, L0_attn_conv_w_f, L0_attn_conv_b_f, L0_attn_xproj_w_f, L0_attn_dtproj_w_f, L0_attn_dtproj_b_f, L0_attn_A_log_f, L0_attn_D_f, L0_attn_conv_w_b, L0_attn_conv_b_b, L0_attn_xproj_w_b, L0_attn_dtproj_w_b, L0_attn_dtproj_b_b, L0_attn_A_log_b, L0_attn_D_b, L0_ffn_gate_w, L0_ffn_gate_b, L0_ffn_We1, L0_ffn_be1, L0_ffn_We2, L0_ffn_be2, L0_ffn_We3, L0_ffn_be3, L0_ffn_ws1, L0_ffn_bs1, L0_ffn_ws2, L0_ffn_bs2, L0_ffn_ws3, L0_ffn_bs3, L1_attn_Wq, L1_attn_Wk, L1_attn_Wv, L1_attn_Wo, L1_attn_rel_bias_table, L1_ffn_W, L1_ffn_b, L1_ffn_R, L1_ffn_A, L1_ffn_B, L2_attn_W_qkv, L2_attn_W_o, L2_ffn_Wq, L2_ffn_bq, L2_ffn_Wk, L2_ffn_bk, L2_ffn_Wv, L2_ffn_bv, L2_ffn_Wo, L2_ffn_bo, L2_ffn_Wg, L2_ffn_bg, L2_ffn_W1, L2_ffn_b1, L2_ffn_W2, L2_ffn_b2, L2_ffn_g1, L2_ffn_be1, L2_ffn_g2, L2_ffn_be2, L3_attn_W_qkv, L3_attn_W_o, L3_attn_W_LTM, L3_attn_V_gs, L3_attn_V_T0, L3_attn_beta_tau, L3_attn_beta_gm, L3_attn_C_ch, L3_attn_gamma, L3_attn_alpha_ppd, L3_attn_IC_threshold, L3_ffn_Wg, L3_ffn_W1, L3_ffn_b1, L3_ffn_A1, L3_ffn_B1, L3_ffn_W2, L3_ffn_b2, L3_ffn_A2, L3_ffn_B2, L3_ffn_W3, L3_ffn_b3, L3_ffn_A3, L3_ffn_B3):

    def _L0_attn_ref(x, norm_w, in_proj_w, out_proj_w, conv_w_f, conv_b_f, xproj_w_f, dtproj_w_f, dtproj_b_f, A_log_f, D_f, conv_w_b, conv_b_b, xproj_w_b, dtproj_w_b, dtproj_b_b, A_log_b, D_b):
        import jax, jax.numpy as jnp
        import numpy as np
        from jax import lax
        B, L, D_MODEL = (2, 512, 128)
        D_STATE, D_CONV, EXPAND = (16, 4, 2)
        D_INNER = D_MODEL * EXPAND
        DT_RANK = (D_MODEL + 15) // 16
        EPS = 1e-05

        def _dt_bias(k):
            u = jax.random.uniform(k, (D_INNER,), dtype=jnp.float32)
            dt = jnp.exp(u * (np.log(0.1) - np.log(0.001)) + np.log(0.001))
            dt = jnp.clip(dt, 0.0001)
            return dt + jnp.log(-jnp.expm1(-dt))

        def _init_A_log():
            a = jnp.arange(1, D_STATE + 1, dtype=jnp.float32)
            return jnp.log(jnp.broadcast_to(a[None, :], (D_INNER, D_STATE)))

        def _causal_dwconv(x, w, b):
            xc = lax.conv_general_dilated(x.transpose(0, 2, 1), w, (1,), [(D_CONV - 1, 0)], dimension_numbers=('NCH', 'OIH', 'NCH'), feature_group_count=D_INNER)
            return (xc + b[None, :, None]).transpose(0, 2, 1)

        def _mamba_dir(xi, z, conv_w, conv_b, xproj_w, dtproj_w, dtproj_b, A_log, Dp):
            xc = jax.nn.silu(_causal_dwconv(xi, conv_w, conv_b))
            x_dbl = jnp.einsum('bld,ed->ble', xc, xproj_w)
            dt = x_dbl[..., :DT_RANK]
            Bm = x_dbl[..., DT_RANK:DT_RANK + D_STATE]
            Cm = x_dbl[..., DT_RANK + D_STATE:]
            delta = jax.nn.softplus(jnp.einsum('blr,dr->bld', dt, dtproj_w) + dtproj_b)
            A = -jnp.exp(A_log)

            def step(h, inp):
                xt, dlt, bt, ct = inp
                h = jnp.exp(dlt[:, :, None] * A) * h + (dlt * xt)[:, :, None] * bt[:, None, :]
                return (h, jnp.einsum('bdn,bn->bd', h, ct))
            h0 = jnp.zeros((xc.shape[0], D_INNER, D_STATE), xc.dtype)
            xs = (xc.transpose(1, 0, 2), delta.transpose(1, 0, 2), Bm.transpose(1, 0, 2), Cm.transpose(1, 0, 2))
            _, ys = lax.scan(step, h0, xs)
            y = ys.transpose(1, 0, 2) + Dp * xc
            return y * jax.nn.silu(z)
        residual = x
        xn = x * lax.rsqrt(jnp.mean(x * x, axis=-1, keepdims=True) + EPS) * norm_w
        xz = jnp.einsum('bld,ed->ble', xn, in_proj_w)
        xi, z = (xz[..., :D_INNER], xz[..., D_INNER:])
        y_f = _mamba_dir(xi, z, conv_w_f, conv_b_f, xproj_w_f, dtproj_w_f, dtproj_b_f, A_log_f, D_f)
        y_b = _mamba_dir(xi[:, ::-1], z[:, ::-1], conv_w_b, conv_b_b, xproj_w_b, dtproj_w_b, dtproj_b_b, A_log_b, D_b)
        y = 0.5 * y_f + 0.5 * y_b[:, ::-1]
        return jnp.einsum('bld,ed->ble', y, out_proj_w) + residual

    def _L0_ffn_ref(x, gate_w, gate_b, We1, be1, We2, be2, We3, be3, ws1, bs1, ws2, bs2, ws3, bs3):
        import jax, jax.numpy as jnp
        import numpy as np
        DIM = 128
        E = 16
        TOPK = 2
        G = 4
        TOPK_G = 2
        INTER = 64
        N_SHARED = 2
        ROUTE_SCALE = 1.0

        def _gate(xf, gate_w, gate_b):
            scores = xf @ gate_w.T
            scores = jax.nn.softmax(scores.astype(jnp.float32), axis=-1)
            orig = scores
            scores = scores + gate_b
            T = xf.shape[0]
            sg = scores.reshape(T, G, E // G)
            group_scores = jax.lax.top_k(sg, 2)[0].sum(-1)
            _, gidx = jax.lax.top_k(group_scores, TOPK_G)
            keep = jax.nn.one_hot(gidx, G).sum(axis=1) > 0
            sg = jnp.where(keep[:, :, None], sg, -jnp.inf)
            scores = sg.reshape(T, E)
            _, idx = jax.lax.top_k(scores, TOPK)
            weights = jnp.take_along_axis(orig, idx, axis=1)
            weights = (weights * ROUTE_SCALE).astype(xf.dtype)
            return (weights, idx)
        shape = x.shape
        xf = x.reshape(-1, DIM)
        weights, idx = _gate(xf, gate_w, gate_b)
        combine = (jax.nn.one_hot(idx, E, dtype=xf.dtype) * weights[..., None]).sum(1)
        h1 = jnp.einsum('td,edi->tei', xf, We1) + be1
        h3 = jnp.einsum('td,edi->tei', xf, We3) + be3
        h = jax.nn.silu(h1) * h3
        yo = jnp.einsum('tei,eid->ted', h, We2) + be2
        y = jnp.einsum('te,ted->td', combine, yo)
        z = jax.nn.silu(xf @ ws1 + bs1) * (xf @ ws3 + bs3) @ ws2 + bs2
        return (y + z).reshape(shape)

    def _L1_attn_ref(hidden_states, Wq, Wk, Wv, Wo, rel_bias_table):
        import jax, jax.numpy as jnp
        import numpy as np
        import math
        B, S, D, H, DK = (4, 256, 128, 16, 64)
        NUM_BUCKETS, MAX_DISTANCE = (32, 128)

        def _relative_position_bucket(relative_position, num_buckets=NUM_BUCKETS, max_distance=MAX_DISTANCE):
            num_buckets //= 2
            buckets = (relative_position > 0).astype(jnp.int32) * num_buckets
            rp = jnp.abs(relative_position)
            max_exact = num_buckets // 2
            is_small = rp < max_exact
            rp_large = max_exact + (jnp.log(jnp.maximum(rp, 1).astype(jnp.float32) / max_exact) / math.log(max_distance / max_exact) * (num_buckets - max_exact)).astype(jnp.int32)
            rp_large = jnp.minimum(rp_large, num_buckets - 1)
            return buckets + jnp.where(is_small, rp, rp_large)

        def compute_bias(query_length, key_length, rel_bias_table):
            ctx = jnp.arange(query_length)[:, None]
            mem = jnp.arange(key_length)[None, :]
            buckets = _relative_position_bucket(mem - ctx)
            values = rel_bias_table[buckets]
            return jnp.transpose(values, (2, 0, 1))[None]
        b, s, _ = hidden_states.shape

        def shape(x):
            return jnp.transpose(x.reshape(b, s, H, DK), (0, 2, 1, 3))
        q = shape(hidden_states @ Wq)
        k = shape(hidden_states @ Wk)
        v = shape(hidden_states @ Wv)
        scores = jnp.einsum('bhqd,bhkd->bhqk', q, k)
        position_bias = compute_bias(s, s, rel_bias_table)
        scores = scores + position_bias
        attn = jax.nn.softmax(scores, axis=-1)
        out = jnp.einsum('bhqk,bhkd->bhqd', attn, v)
        out = jnp.transpose(out, (0, 2, 1, 3)).reshape(b, s, H * DK)
        return out @ Wo

    def _L1_ffn_ref(x, W, b, R, A, B):
        import jax, jax.numpy as jnp
        import numpy as np
        TOP_K = 2
        EPS = 1e-06
        base_out = jnp.einsum('btd,od->bto', x, W) + b
        logits = jnp.einsum('btd,ed->bte', x, R)
        gate = jax.nn.softmax(logits, axis=-1)
        E = gate.shape[-1]
        _, idx = jax.lax.top_k(gate, TOP_K)
        mask = jax.nn.one_hot(idx, E, dtype=gate.dtype).sum(axis=-2)
        gate = gate * mask
        gate = gate / (gate.sum(axis=-1, keepdims=True) + EPS)
        h = jnp.einsum('btd,erd->bter', x, A)
        gh = gate[..., None] * h
        lora_out = jnp.einsum('bter,eor->bto', gh, B)
        return base_out + lora_out

    def _L2_attn_ref(x, W_qkv, W_o):
        import jax, jax.numpy as jnp
        import numpy as np
        D_MODEL = 128
        NUM_HEADS = 16
        D_K = D_MODEL // NUM_HEADS
        THETA = 10000.0

        def _rope(x, positions):
            d = x.shape[-1]
            inv_freq = THETA ** (-jnp.arange(0, d, 2, dtype=jnp.float32) / d)
            ang = positions[:, :, None].astype(jnp.float32) * inv_freq[None, None, :]
            cos = jnp.cos(ang)[:, None, :, :]
            sin = jnp.sin(ang)[:, None, :, :]
            x1 = x[..., 0::2]
            x2 = x[..., 1::2]
            r1 = x1 * cos - x2 * sin
            r2 = x1 * sin + x2 * cos
            out = jnp.stack([r1, r2], axis=-1).reshape(x.shape)
            return out
        B, S, _ = x.shape
        H, dk = (NUM_HEADS, D_K)
        qkv = jnp.einsum('bsd,ed->bse', x, W_qkv)
        qkv = qkv.reshape(B, S, 3, H, dk).transpose(2, 0, 3, 1, 4)
        q, k, v = (qkv[0], qkv[1], qkv[2])
        positions = jnp.broadcast_to(jnp.arange(S)[None, :], (B, S))
        q = _rope(q, positions)
        k = _rope(k, positions)
        scores = jnp.einsum('bhqd,bhkd->bhqk', q, k) / jnp.sqrt(jnp.float32(dk))
        causal = jnp.tril(jnp.ones((S, S), dtype=bool))
        scores = jnp.where(causal[None, None, :, :], scores, -jnp.inf)
        attn = jax.nn.softmax(scores, axis=-1)
        out = jnp.einsum('bhqk,bhkd->bhqd', attn, v)
        out = out.transpose(0, 2, 1, 3).reshape(B, S, H * dk)
        return jnp.einsum('bsd,ed->bse', out, W_o)

    def _L2_ffn_ref(x, Wq, bq, Wk, bk, Wv, bv, Wo, bo, Wg, bg, W1, b1, W2, b2, g1, be1, g2, be2):
        import jax, jax.numpy as jnp
        import numpy as np
        from math import sqrt
        B, S, D, H, E, K, FF = (2, 128, 128, 16, 8, 2, 512)
        HD = D // H
        EPS = 1e-05

        def _rope_cache(seq_len, hd):
            inv_freq = 1.0 / 10000.0 ** (jnp.arange(0, hd, 2, dtype=jnp.float32) / hd)
            t = jnp.arange(seq_len, dtype=jnp.float32)
            freqs = t[:, None] * inv_freq[None, :]
            emb = jnp.concatenate([freqs, freqs], axis=-1)
            return (jnp.cos(emb), jnp.sin(emb))

        def _rotate_half(x):
            x1, x2 = jnp.split(x, 2, axis=-1)
            return jnp.concatenate([-x2, x1], axis=-1)

        def _layernorm(x, g, b):
            m = jnp.mean(x, axis=-1, keepdims=True)
            v = jnp.var(x, axis=-1, keepdims=True)
            return (x - m) * jax.lax.rsqrt(v + EPS) * g + b

        def _forward(x, Wq, bq, Wk, bk, Wv, bv, Wo, bo, Wg, bg, W1, b1, W2, b2, g1, be1, g2, be2):
            bsz, seq, d = x.shape
            q = (x @ Wq + bq).reshape(bsz, seq, H, HD).transpose(0, 2, 1, 3)
            k = (x @ Wk + bk).reshape(bsz, seq, H, HD).transpose(0, 2, 1, 3)
            v = (x @ Wv + bv).reshape(bsz, seq, H, HD).transpose(0, 2, 1, 3)
            cos, sin = _rope_cache(seq, HD)
            cos = cos[None, None]
            sin = sin[None, None]
            q = q * cos + _rotate_half(q) * sin
            k = k * cos + _rotate_half(k) * sin
            scores = jnp.einsum('bhqd,bhkd->bhqk', q, k) / sqrt(HD)
            attn = jax.nn.softmax(scores, axis=-1)
            ao = jnp.einsum('bhqk,bhkd->bhqd', attn, v)
            ao = ao.transpose(0, 2, 1, 3).reshape(bsz, seq, d)
            attn_out = ao @ Wo + bo
            x1 = _layernorm(x + attn_out, g1, be1)
            gate_logits = x1 @ Wg + bg
            gate_probs = jax.nn.softmax(gate_logits, axis=-1)
            topk_p, topk_i = jax.lax.top_k(gate_probs, K)
            topk_p = topk_p / jnp.sum(topk_p, axis=-1, keepdims=True)
            comb = jnp.sum(jax.nn.one_hot(topk_i, E, dtype=x.dtype) * topk_p[..., None], axis=-2)
            h = jax.nn.gelu(jnp.einsum('bsd,edf->bsef', x1, W1) + b1, approximate=False)
            y = jnp.einsum('bsef,efd->bsed', h, W2) + b2
            moe_out = jnp.einsum('bse,bsed->bsd', comb, y)
            return _layernorm(x1 + moe_out, g2, be2)
        return _forward(x, Wq, bq, Wk, bk, Wv, bv, Wo, bo, Wg, bg, W1, b1, W2, b2, g1, be1, g2, be2)

    def _L3_attn_ref(x, W_qkv, W_o, W_LTM, V_gs, V_T0, beta_tau, beta_gm, C_ch, gamma, alpha_ppd, IC_threshold):
        import jax, jax.numpy as jnp
        import numpy as np
        LN_EPS = 1e-05
        U_T = 1.0
        B, L, D = x.shape
        H, dk, _ = W_LTM.shape
        qkv = (x @ W_qkv.T).reshape(B, L, 3, H, dk)
        q, k, v = (qkv[:, :, 0], qkv[:, :, 1], qkv[:, :, 2])
        mu = k.mean(-1, keepdims=True)
        var = ((k - mu) ** 2).mean(-1, keepdims=True)
        k = (k - mu) / jnp.sqrt(var + LN_EPS)
        V_norm = (V_gs[:, None, None] - V_T0[:, None, None] + W_LTM) / U_T
        sp = jax.nn.softplus(V_norm)
        g_ch = beta_tau[:, None, None] * sp
        retention = jnp.exp(-g_ch / C_ch[:, None, None])
        G = beta_gm[:, None, None] * sp * jax.nn.sigmoid(V_norm)
        sign_mask = jnp.tanh(alpha_ppd * (g_ch - IC_threshold))
        coef = gamma[:, None, None] * sign_mask * G
        qL = jnp.moveaxis(q, 1, 0)
        kL = jnp.moveaxis(k, 1, 0)
        vL = jnp.moveaxis(v, 1, 0)

        def step(F, qkv_t):
            q_t, k_t, v_t = qkv_t
            hebbian = jnp.einsum('bhd,bhe->bhde', v_t, k_t)
            F = retention * F + coef * hebbian
            y_t = jnp.einsum('bhde,bhe->bhd', W_LTM + F, q_t)
            return (F, y_t)
        F0 = jnp.zeros((B, H, dk, dk), x.dtype)
        _, yL = jax.lax.scan(step, F0, (qL, kL, vL))
        y = jnp.moveaxis(yL, 0, 1).reshape(B, L, D)
        return y @ W_o.T

    def _L3_ffn_ref(x, Wg, W1, b1, A1, B1, W2, b2, A2, B2, W3, b3, A3, B3):
        import jax, jax.numpy as jnp
        import numpy as np
        DIM = 128
        HID = 256
        E = 8
        K = 2
        R = 16
        B_, S_ = (2, 128)

        def _lora_in(xf, W, b, A, B):
            base = jnp.einsum('td,ehd->teh', xf, W)
            low = jnp.einsum('ter,ehr->teh', jnp.einsum('td,erd->ter', xf, A), B)
            return base + low + b

        def _lora_out(g, W, b, A, B):
            base = jnp.einsum('teh,edh->ted', g, W)
            low = jnp.einsum('ter,edr->ted', jnp.einsum('teh,erh->ter', g, A), B)
            return base + low + b
        orig_shape = x.shape
        xf = x.reshape(-1, x.shape[-1])
        scores = jax.nn.softmax(xf @ Wg.T, axis=-1)
        expert_weights, expert_indices = jax.lax.top_k(scores, K)
        expert_weights = expert_weights / expert_weights.sum(-1, keepdims=True)
        gates = (jax.nn.one_hot(expert_indices, E, dtype=xf.dtype) * expert_weights[..., None]).sum(axis=1)
        h1 = _lora_in(xf, W1, b1, A1, B1)
        h3 = _lora_in(xf, W3, b3, A3, B3)
        g = jax.nn.silu(h1) * h3
        y_e = _lora_out(g, W2, b2, A2, B2)
        y = jnp.einsum('te,ted->td', gates, y_e)
        return y.reshape(orig_shape)
    x = L0_attn_x
    x = x + _L0_attn_ref(_layernorm(x, axis=-1), L0_attn_norm_w, L0_attn_in_proj_w, L0_attn_out_proj_w, L0_attn_conv_w_f, L0_attn_conv_b_f, L0_attn_xproj_w_f, L0_attn_dtproj_w_f, L0_attn_dtproj_b_f, L0_attn_A_log_f, L0_attn_D_f, L0_attn_conv_w_b, L0_attn_conv_b_b, L0_attn_xproj_w_b, L0_attn_dtproj_w_b, L0_attn_dtproj_b_b, L0_attn_A_log_b, L0_attn_D_b)
    x = x + _L0_ffn_ref(_layernorm(x, axis=-1), L0_ffn_gate_w, L0_ffn_gate_b, L0_ffn_We1, L0_ffn_be1, L0_ffn_We2, L0_ffn_be2, L0_ffn_We3, L0_ffn_be3, L0_ffn_ws1, L0_ffn_bs1, L0_ffn_ws2, L0_ffn_bs2, L0_ffn_ws3, L0_ffn_bs3)
    x = x + _L1_attn_ref(_layernorm(x, axis=-1), L1_attn_Wq, L1_attn_Wk, L1_attn_Wv, L1_attn_Wo, L1_attn_rel_bias_table)
    x = x + _L1_ffn_ref(_layernorm(x, axis=-1), L1_ffn_W, L1_ffn_b, L1_ffn_R, L1_ffn_A, L1_ffn_B)
    x = x + _L2_attn_ref(_layernorm(x, axis=-1), L2_attn_W_qkv, L2_attn_W_o)
    x = x + _L2_ffn_ref(_layernorm(x, axis=-1), L2_ffn_Wq, L2_ffn_bq, L2_ffn_Wk, L2_ffn_bk, L2_ffn_Wv, L2_ffn_bv, L2_ffn_Wo, L2_ffn_bo, L2_ffn_Wg, L2_ffn_bg, L2_ffn_W1, L2_ffn_b1, L2_ffn_W2, L2_ffn_b2, L2_ffn_g1, L2_ffn_be1, L2_ffn_g2, L2_ffn_be2)
    x = x + _L3_attn_ref(_layernorm(x, axis=-1), L3_attn_W_qkv, L3_attn_W_o, L3_attn_W_LTM, L3_attn_V_gs, L3_attn_V_T0, L3_attn_beta_tau, L3_attn_beta_gm, L3_attn_C_ch, L3_attn_gamma, L3_attn_alpha_ppd, L3_attn_IC_threshold)
    x = x + _L3_ffn_ref(_layernorm(x, axis=-1), L3_ffn_Wg, L3_ffn_W1, L3_ffn_b1, L3_ffn_A1, L3_ffn_B1, L3_ffn_W2, L3_ffn_b2, L3_ffn_A2, L3_ffn_B2, L3_ffn_W3, L3_ffn_b3, L3_ffn_A3, L3_ffn_B3)
    return x

_drawn_inputs = setup_inputs


def setup_inputs(seed=0):
    import zlib

    import numpy as np

    out = dict(_drawn_inputs(seed))
    spreads = {'L0_attn_norm_w': (1.0, 0.2),
     'L0_attn_conv_b_f': (0.0, 0.1),
     'L0_attn_D_f': (1.0, 0.2),
     'L0_attn_conv_b_b': (0.0, 0.1),
     'L0_attn_D_b': (1.0, 0.2),
     'L0_ffn_gate_b': (0.0, 0.1),
     'L0_ffn_be1': (0.0, 0.1),
     'L0_ffn_be2': (0.0, 0.1),
     'L0_ffn_be3': (0.0, 0.1),
     'L0_ffn_bs1': (0.0, 0.1),
     'L0_ffn_bs2': (0.0, 0.1),
     'L0_ffn_bs3': (0.0, 0.1),
     'L2_ffn_bq': (0.0, 0.1),
     'L2_ffn_bk': (0.0, 0.1),
     'L2_ffn_bv': (0.0, 0.1),
     'L2_ffn_bo': (0.0, 0.1),
     'L2_ffn_bg': (0.0, 0.1),
     'L2_ffn_b1': (0.0, 0.1),
     'L2_ffn_b2': (0.0, 0.1),
     'L2_ffn_g1': (1.0, 0.2),
     'L2_ffn_be1': (0.0, 0.1),
     'L2_ffn_g2': (1.0, 0.2),
     'L2_ffn_be2': (0.0, 0.1),
     'L3_attn_V_gs': (0.0, 0.1),
     'L3_attn_V_T0': (0.0, 0.1),
     'L3_attn_beta_tau': (1.0, 0.2),
     'L3_attn_beta_gm': (0.10000000149011612, 0.2),
     'L3_attn_C_ch': (1.0, 0.2),
     'L3_attn_gamma': (0.10000000149011612, 0.2),
     'L3_ffn_b1': (0.0, 0.1),
     'L3_ffn_b2': (0.0, 0.1),
     'L3_ffn_b3': (0.0, 0.1)}
    factors = {}
    for name, (base, spread) in spreads.items():
        noise = np.random.default_rng([zlib.crc32(name.encode()), seed]).standard_normal(out[name].shape)
        drawn = base * np.exp(spread * noise) if base else spread * noise
        out[name] = jnp.asarray(drawn.astype(out[name].dtype))
    for name, factor in factors.items():
        out[name] = (out[name] * factor).astype(out[name].dtype)
    return out
```

```python
from contextlib import ExitStack

import numpy as np

import concourse.bass as bass
from concourse import mybir

ALU = mybir.AluOpType
ACT = mybir.ActivationFunctionType
F32 = mybir.dt.float32
BF16 = mybir.dt.bfloat16
AX = mybir.AxisListType

P = 128
D = 128
SEQ = 512
NJ = SEQ // P
BIG = 3.0e38
EPS = 1e-5

DI = 256
ND = DI // P
NS = 16
DTR = 8
KC = 4
PAD = KC - 1

H = 16
DK = 64
TW = SEQ + P * (NJ - 1)
HD = 8
HS = 64
SPLITS = 6
SK = SPLITS * HD
E0, INTER = 16, 64
E1, R1 = 8, 16
E2, FF = 8, 512
E3, HID = 8, 256
NG = H * HD * HD // P


class Chain:

    def __init__(self, eng, sem):
        self.eng, self.sem, self.n = eng, sem, 0

    def __call__(self, ins):
        self.n += 1
        ins.then_inc(self.sem, 1)
        self.eng.wait_ge(self.sem, self.n)


def bass_mk_seq(nc, x, cols_f, cols_b, wf, wb, lora, lora_cols, onehot, table, out):
    top = ExitStack()

    def sbt(c, name, shape, dt=F32):
        return c.enter_context(nc.sbuf_tensor(name, shape, dt))

    WF = sbt(top, "WF", [P, wf.shape[1]])
    WB = sbt(top, "WB", [P, wb.shape[1]], BF16)

    def W(name, p=P):
        o, n = cols_f[name]
        return WF[0:p, o:o + n]

    def WBF(name, p=P):
        o, n = cols_b[name]
        return WB[0:p, o:o + n]

    X = sbt(top, "X", [P, NJ, D])
    XN = sbt(top, "XN", [P, NJ, D])
    XT = sbt(top, "XT", [P, SEQ])
    stats = sbt(top, "stats", [P, NJ, 6])
    mv = sbt(top, "mv", [P, NJ, 2])
    rstd = sbt(top, "rstd", [P, NJ])
    PS = [top.enter_context(nc.psum_tensor(f"PS{i}", [P, 512], F32)) for i in range(8)]
    ident = W("ident")
    ident_b = WBF("ident_b")
    bias_dram = nc.dram_tensor("bias_line", [H, 1024], F32, kind="Internal").ap()

    tiles = "p (j d) -> p j d"

    class Stage:

        def __init__(self, name):
            self.name, self.ctx, self.sems = name, ExitStack(), {}

        def __enter__(self):
            return self

        def sb(self, name, shape, dt=F32, scope=None):
            return sbt(scope or self.ctx, f"{self.name}_{name}", shape, dt)

        def sem(self, name):
            s = self.ctx.enter_context(nc.semaphore(f"{self.name}_{name}"))
            self.sems[name] = s
            return s

        def __exit__(self, *_):
            sems = list(self.sems.values())
            with nc.Block() as block:
                @block.sync
                def _(sp):
                    for s in sems:
                        sp.sem_clear(s)
            self.ctx.close()

    def bc(ap, shape):
        return ap.to_broadcast(shape)

    def norm_tiles(st, tag, src, dst, dst_t, rms=False, gain_t=None, gain=None, shift=None, extra=None,
                   transposed=True):
        ch, normed = st.sem(f"{tag}_chain"), st.sem(f"{tag}_normed")
        turned, evac = st.sem(f"{tag}_turned"), st.sem(f"{tag}_evac")
        shifted, rooted = st.sem(f"{tag}_shifted"), st.sem(f"{tag}_rooted")
        sq = XT if rms else None
        with nc.Block() as block:
            @block.gpsimd
            def _(pool):
                pool.wait_ge(shifted, 1)
                nc.gpsimd.tensor_tensor(rstd[:, :], rstd[:, :], W("minus_half")[:, 0:NJ], ALU.pow).then_inc(rooted, 1)

            @block.vector
            def _(dve):
                link = Chain(dve, ch)
                if rms:
                    for j in range(NJ):
                        last = nc.vector.tensor_tensor_reduce(sq[:, j * D:(j + 1) * D], src[:, j, :], src[:, j, :], 1.0 / D, 0.0,
                                                              ALU.mult, ALU.add, rstd[:, j:j + 1])
                    link(last)
                    nc.vector.tensor_scalar(rstd[:, :], rstd[:, :], EPS, None, ALU.add).then_inc(shifted, 1)
                else:
                    for j in range(NJ):
                        last = nc.vector.bn_stats(stats[:, j, :], src[:, j, :])
                    link(last)
                    for j in range(NJ):
                        last = nc.vector.bn_aggr(mv[:, j, :], stats[:, j, :])
                    link(last)
                    nc.vector.tensor_scalar(rstd[:, :], mv[:, :, 1], EPS, None, ALU.add).then_inc(shifted, 1)
                dve.wait_ge(rooted, 1)
                for j in range(NJ):
                    if rms:
                        ins = nc.vector.tensor_scalar(dst[:, j, :], src[:, j, :], rstd[:, j:j + 1], None, ALU.mult)
                    else:
                        ins = nc.vector.tensor_scalar(dst[:, j, :], src[:, j, :], mv[:, j, 0:1], rstd[:, j:j + 1],
                                                      ALU.subtract, ALU.mult)
                    if gain is not None:
                        link(ins)
                        link(nc.vector.tensor_tensor(dst[:, j, :], dst[:, j, :], gain, ALU.mult))
                        ins = nc.vector.tensor_tensor(dst[:, j, :], dst[:, j, :], shift, ALU.add)
                    ins.then_inc(normed, 1)
                if extra is not None:
                    dve.wait_ge(normed, NJ)
                    extra(link)

            if transposed:
                @block.tensor
                def _(pe):
                    for j in range(NJ):
                        pe.wait_ge(normed, j + 1)
                        nc.tensor.transpose(PS[7][:, j * P:(j + 1) * P], dst[:, j, :], ident).then_inc(turned, 1)

                @block.scalar
                def _(act):
                    act.wait_ge(turned, NJ)
                    if gain_t is not None:
                        nc.scalar.activation(dst_t[:, :], PS[7][:, :], ACT.Copy, scale=gain_t).then_inc(evac, 1)
                    else:
                        nc.scalar.copy(dst_t[:, :], PS[7][:, :]).then_inc(evac, 1)

    def top2_mask(link, s, mask, E, big1, big2, rank):
        n = NJ * E * E
        a = big1[:, 0:n].rearrange("p (j g o) -> p j g o", j=NJ, g=E)
        b = big2[:, 0:n].rearrange("p (j g o) -> p j g o", j=NJ, g=E)
        other = bc(s.unsqueeze(2), [P, NJ, E, E])
        own = bc(s.unsqueeze(3), [P, NJ, E, E])
        tri = W(f"tri{E}").rearrange("p (g o) -> p g o", g=E)
        nc.vector.tensor_tensor(a, other, own, ALU.is_gt)
        link(nc.vector.tensor_tensor(b, other, own, ALU.is_equal))
        link(nc.vector.tensor_tensor(b, b, bc(tri.unsqueeze(1), [P, NJ, E, E]), ALU.mult))
        link(nc.vector.tensor_tensor(a, a, b, ALU.add))
        link(nc.vector.tensor_reduce(rank, a, AX.X, ALU.add))
        link(nc.vector.tensor_scalar(mask, rank, 2.0, None, ALU.is_lt))

    def gates(st, src_t, w_gate, E, comb, comb_t, bias=None, grouped_bias=None, eps=None):
        lg, ex, mask = st.sb("lg", [P, NJ, E]), st.sb("ex", [P, NJ, E]), st.sb("mask", [P, NJ, E])
        m1, t4 = st.sb("m1", [P, NJ]), st.sb("t4", [P, 6, NJ, 4])
        big1, big2 = st.sb("cmp1", [P, NJ * E * E]), st.sb("cmp2", [P, NJ * E * E])
        rank = st.sb("rank", [P, NJ, E])
        ch, logits, shifted = st.sem("gchain"), st.sem("logits"), st.sem("shifted")
        exped, combed, turned, evac = st.sem("exped"), st.sem("combed"), st.sem("gturned"), st.sem("gevac")
        with nc.Block() as block:
            @block.tensor
            def _(pe):
                for j in range(NJ):
                    last = nc.tensor.matmul(PS[0][:, j * E:(j + 1) * E], src_t[:, j * P:(j + 1) * P], w_gate,
                                            start=True, stop=True)
                last.then_inc(logits, 1)
                pe.wait_ge(combed, 1)
                for j in range(NJ):
                    last = nc.tensor.transpose(PS[1][0:E, j * P:(j + 1) * P], comb[:, j, :], ident)
                last.then_inc(turned, 1)

            @block.scalar
            def _(act):
                act.wait_ge(shifted, 1)
                nc.scalar.activation(ex[:, :, :], lg[:, :, :], ACT.Exp).then_inc(exped, 1)
                act.wait_ge(turned, 1)
                nc.scalar.copy(comb_t[0:E, :], PS[1][0:E, :]).then_inc(evac, 1)

            @block.vector
            def _(dve):
                link = Chain(dve, ch)
                V = nc.vector
                raw = PS[0][:, 0:NJ * E].rearrange("p (j e) -> p j e", e=E)
                dve.wait_ge(logits, 1)
                if bias is not None:
                    link(V.tensor_tensor(lg[:, :, :], raw, bc(bias.unsqueeze(1), [P, NJ, E]), ALU.add))
                    raw = lg[:, :, :]
                link(V.tensor_reduce(m1[:, :], raw, AX.X, ALU.max))
                V.tensor_tensor(lg[:, :, :], raw, bc(m1[:, :].unsqueeze(2), [P, NJ, E]),
                                ALU.subtract).then_inc(shifted, 1)
                dve.wait_ge(exped, 1)
                link(V.tensor_reduce(m1[:, :], ex[:, :, :], AX.X, ALU.add))
                link(V.reciprocal(m1[:, :], m1[:, :]))
                link(V.tensor_tensor(ex[:, :, :], ex[:, :, :], bc(m1[:, :].unsqueeze(2), [P, NJ, E]), ALU.mult))
                score = ex
                if grouped_bias is not None:
                    link(V.tensor_tensor(lg[:, :, :], ex[:, :, :], bc(grouped_bias.unsqueeze(1), [P, NJ, E]), ALU.add))
                    q = lg[:, :, :].rearrange("p j (g k) -> p j g k", k=4)
                    t = [t4[:, i, :, :] for i in range(6)]
                    V.tensor_tensor(t[0], q[:, :, :, 0], q[:, :, :, 1], ALU.max)
                    V.tensor_tensor(t[1], q[:, :, :, 0], q[:, :, :, 1], ALU.min)
                    V.tensor_tensor(t[2], q[:, :, :, 2], q[:, :, :, 3], ALU.max)
                    link(V.tensor_tensor(t[3], q[:, :, :, 2], q[:, :, :, 3], ALU.min))
                    V.tensor_tensor(t[4], t[0], t[2], ALU.max)
                    V.tensor_tensor(t[5], t[0], t[2], ALU.min)
                    link(V.tensor_tensor(t[1], t[1], t[3], ALU.max))
                    link(V.tensor_tensor(t[5], t[5], t[1], ALU.max))
                    link(V.tensor_tensor(t[4], t[4], t[5], ALU.add))
                    top2_mask(link, t[4], t[0], 4, big1, big2, rank[:, :, 0:4])
                    link(V.tensor_scalar(t[1], t[0], 1.0, BIG, ALU.subtract, ALU.mult))
                    link(V.tensor_tensor(q, q, bc(t[1].unsqueeze(3), [P, NJ, 4, 4]), ALU.add))
                    score = lg
                top2_mask(link, score[:, :, :], mask[:, :, :], E, big1, big2, rank[:, :, :])
                if eps is None:
                    V.tensor_tensor(comb[:, :, :], ex[:, :, :], mask[:, :, :], ALU.mult).then_inc(combed, 1)
                else:
                    link(V.tensor_tensor(ex[:, :, :], ex[:, :, :], mask[:, :, :], ALU.mult))
                    link(V.tensor_reduce(m1[:, :], ex[:, :, :], AX.X, ALU.add))
                    if eps:
                        link(V.tensor_scalar(m1[:, :], m1[:, :], eps, None, ALU.add))
                    link(V.reciprocal(m1[:, :], m1[:, :]))
                    V.tensor_tensor(comb[:, :, :], ex[:, :, :], bc(m1[:, :].unsqueeze(2), [P, NJ, E]),
                                    ALU.mult).then_inc(combed, 1)

    def attention(st, scores, vals, dv, O, causal=False, bias_of=None, evac_act=lambda u: u % 2,
                  loads=None, pe_ahead=None, act_ahead=None):
        U = H * NJ
        NS_, NP_, NT_ = 3, 3, 2
        prob = st.sb("prob", [P, NP_, SEQ])
        probt = st.sb("probt", [P, NT_, SEQ])
        biased = st.sb("biased", [P, NS_, SEQ]) if bias_of else None
        nmax = st.sb("nmax", [P, U])
        rden = st.sb("rden", [P, 2, NJ])
        scored, maxed, exped = st.sem("scored"), st.sem("maxed"), st.sem("exped_p")
        turned, evac_d, evac_a = st.sem("turned_p"), st.sem("evac_d"), st.sem("evac_a")
        weighed, normed, ch = st.sem("weighed"), st.sem("head_normed"), st.sem("achain")
        n_act = [0]
        n_dve = [0]
        for u in range(U):
            n_act.append(n_act[-1] + bool(evac_act(u)))
            n_dve.append(n_dve[-1] + (not evac_act(u)))

        def keys(u):
            return P * (u % NJ + 1) if causal else SEQ

        def evacuated(eng, u):
            if evac_act(u):
                eng.wait_ge(evac_a, n_act[u + 1])
            else:
                eng.wait_ge(evac_d, n_dve[u + 1])

        def out_ps(h):
            return PS[5 + h % 2][:, 0:NJ * (dv + 1)].rearrange("p (j v) -> p j v", j=NJ)

        with nc.Block() as block:
            if loads is not None:
                loads(block)

            @block.tensor
            def _(pe):
                for s in range(U + 3):
                    if pe_ahead is not None and s < U:
                        pe_ahead(pe, s)
                    if s < U:
                        if s >= NS_:
                            pe.wait_ge(maxed if bias_of else exped, s - NS_ + 1)
                        scores(pe, s, PS[s % NS_][:, 0:keys(s)]).then_inc(scored, 1)
                    u = s - 2
                    if 0 <= u < U:
                        pe.wait_ge(exped, u + 1)
                        if u >= NT_:
                            evacuated(pe, u - NT_)
                        for kt in range(keys(u) // P):
                            last = nc.tensor.transpose(PS[3 + u % NT_][:, kt * P:(kt + 1) * P],
                                                       prob[:, u % NP_, kt * P:(kt + 1) * P], ident)
                        last.then_inc(turned, 1)
                    u = s - 3
                    if 0 <= u < U:
                        h, j = u // NJ, u % NJ
                        evacuated(pe, u)
                        if j == 0 and h >= 2:
                            pe.wait_ge(normed, h - 1)
                        n = keys(u) // P
                        for kt in range(n):
                            last = nc.tensor.matmul(out_ps(h)[:, j, :], probt[:, u % NT_, kt * P:(kt + 1) * P],
                                                    vals[:, kt, h, :], start=(kt == 0), stop=(kt == n - 1))
                        last.then_inc(weighed, 1)

            def evac(eng, copy, sem, u):
                eng.wait_ge(turned, u + 1)
                if u >= NT_:
                    eng.wait_ge(weighed, u - NT_ + 1)
                copy(probt[:, u % NT_, 0:keys(u)], PS[3 + u % NT_][:, 0:keys(u)]).then_inc(sem, 1)

            @block.vector
            def _(dve):
                link = Chain(dve, ch)
                for s in range(U + 5):
                    if s < U:
                        dve.wait_ge(scored, s + 1)
                        if bias_of:
                            if s >= NS_:
                                dve.wait_ge(exped, s - NS_ + 1)
                            nc.vector.tensor_tensor_reduce(
                                biased[:, s % NS_, :], PS[s % NS_][:, :], bias_of(dve, s), -1.0, BIG,
                                ALU.add, ALU.min, nmax[:, s:s + 1]).then_inc(maxed, 1)
                        else:
                            nc.vector.tensor_reduce(nmax[:, s:s + 1], PS[s % NS_][:, 0:keys(s)], AX.X, ALU.max,
                                                    negate=True).then_inc(maxed, 1)
                    u = s - 2
                    if 0 <= u < U and not evac_act(u):
                        evac(dve, nc.vector.tensor_copy, evac_d, u)
                    u = s - 4
                    if u >= 0 and u % NJ == NJ - 1:
                        h = u // NJ
                        dve.wait_ge(weighed, u + 1)
                        r = rden[:, h % 2, :]
                        link(nc.vector.reciprocal(r, out_ps(h)[:, :, dv]))
                        nc.vector.tensor_tensor(O[:, :, h * dv:(h + 1) * dv], out_ps(h)[:, :, 0:dv],
                                                bc(r.unsqueeze(2), [P, NJ, dv]), ALU.mult).then_inc(normed, 1)

            @block.scalar
            def _(act):
                for s in range(U + 3):
                    if act_ahead is not None and s < U:
                        act_ahead(act, s)
                    if s < U:
                        act.wait_ge(maxed, s + 1)
                        if s >= NP_:
                            act.wait_ge(turned, s - NP_ + 1)
                        src = biased[:, s % NS_, :] if bias_of else PS[s % NS_][:, 0:keys(s)]
                        nc.scalar.activation(prob[:, s % NP_, 0:keys(s)], src, ACT.Exp, bias=nmax[:, s:s + 1],
                                             scale=-1.0 if bias_of else 1.0).then_inc(exped, 1)
                    u = s - 2
                    if 0 <= u < U and evac_act(u):
                        evac(act, nc.scalar.copy, evac_a, u)

    with Stage("init") as st:
        ld, ld_b, ld_x, ch = st.sem("ld"), st.sem("ld_b"), st.sem("ld_x"), st.sem("ch")
        fold, folded = st.sem("fold"), st.sem("folded")
        ach, line, lined, stored = st.sem("ach"), st.sem("line"), st.sem("lined"), st.sem("stored")
        LO = st.sb("LO", [R1, lora.shape[1]])
        OH = st.sb("OH", [32, 1024])
        TB = st.sb("TB", [32, H])
        LN = st.sb("LN", [H, 1024])

        def lo(name):
            o, n = lora_cols[name]
            return LO[:, o:o + n]

        with nc.Block() as block:
            @block.sync
            def _(sp):
                n = wf.shape[1]
                step = -(-n // 8)
                for c in range(0, n, step):
                    e = min(n, c + step)
                    sp.dma_start(WF[:, c:e], wf[:, c:e]).then_inc(ld, 16)
                sp.dma_start(WB[:, :], wb).then_inc(ld_b, 16)
                sp.dma_start(LO[:, :], lora).then_inc(ld_x, 16)
                sp.dma_start(OH[:, :], onehot).then_inc(ld_x, 16)
                sp.dma_start(TB[:, :], table).then_inc(ld_x, 16)
                sp.wait_ge(ld, 128)
                sp.wait_ge(ld_b, 16)
                sp.wait_ge(lined, 2)
                sp.dma_start(bias_dram, LN[:, :]).then_inc(stored, 16)
                sp.wait_ge(stored, 16)

            def jobs():
                for w, a, b in (("W1_3", "A1", "B1T"), ("W3_3", "A3", "B3T")):
                    for e in range(E3):
                        yield (lo(a)[:, e * D:(e + 1) * D], lo(b)[:, e * HID:(e + 1) * HID],
                               W(w)[:, e * HID:(e + 1) * HID])
                for e in range(E3):
                    for t in range(HID // P):
                        yield (lo("A2")[:, e * HID + t * P:e * HID + (t + 1) * P], lo("B2T")[:, e * D:(e + 1) * D],
                               W("W2_3")[:, (2 * e + t) * D:(2 * e + t + 1) * D])

            @block.tensor
            def _(pe):
                pe.wait_ge(ld_x, 48)
                for i in range(2):
                    nc.tensor.matmul(PS[6 + i][0:H, :], TB[:, :], OH[:, i * 512:(i + 1) * 512],
                                     start=True, stop=True).then_inc(line, 1)
                for i, (a, b, w) in enumerate(jobs()):
                    if i >= 4:
                        pe.wait_ge(folded, i - 3)
                    nc.tensor.matmul(PS[i % 4][:, 0:w.shape[1]], a, b, start=True, stop=True).then_inc(fold, 1)

            @block.vector
            def _(dve):
                link = Chain(dve, ch)
                V = nc.vector
                for i in range(2):
                    dve.wait_ge(line, i + 1)
                    V.tensor_copy(LN[:, i * 512:(i + 1) * 512], PS[6 + i][0:H, :]).then_inc(lined, 1)
                dve.wait_ge(ld, 128)
                for i, (a, b, w) in enumerate(jobs()):
                    dve.wait_ge(fold, i + 1)
                    V.tensor_tensor(w, w, PS[i % 4][:, 0:w.shape[1]], ALU.add).then_inc(folded, 1)
                dve.wait_ge(ach, 1)
                link(V.tensor_scalar(W("A"), W("A"), -1.0, None, ALU.mult))

            @block.scalar
            def _(act):
                act.wait_ge(ld, 128)
                nc.scalar.activation(W("A"), W("A"), ACT.Exp).then_inc(ach, 1)

        T = {n: st.sb(f"m_{n}", [P, NG]) for n in ("v", "a", "e", "l", "sp", "g", "t", "c", "u")}
        dv, da = st.sem("dv"), st.sem("da")
        with nc.Block() as block:
            @block.vector
            def _(dve):
                V = nc.vector
                n = [0]

                def link(ins):
                    ins.then_inc(dv, 1)
                    n[0] += 1
                    dve.wait_ge(dv, n[0])

                t = {k: v[:, :] for k, v in T.items()}
                link(V.tensor_tensor(t["v"], W("Vgs"), W("VT0"), ALU.subtract))
                link(V.tensor_tensor(t["v"], t["v"], W("LTM"), ALU.add))
                link(V.scalar_tensor_tensor(t["a"], t["v"], -1.0, t["v"], ALU.mult, ALU.max))
                dve.wait_ge(da, 2)
                link(V.tensor_scalar(t["u"], t["e"], 1.0, -1.0, ALU.add, ALU.add))
                link(V.tensor_tensor(t["l"], t["l"], t["u"], ALU.subtract))
                link(V.tensor_tensor(t["l"], t["l"], t["e"], ALU.add))
                link(V.tensor_scalar(t["u"], t["v"], 0.0, None, ALU.max))
                link(V.tensor_tensor(t["sp"], t["l"], t["u"], ALU.add))
                link(V.tensor_tensor(t["g"], t["sp"], W("btau"), ALU.mult))
                link(V.reciprocal(t["c"], W("Cch")))
                link(V.tensor_tensor(t["c"], t["c"], t["g"], ALU.mult))
                link(V.tensor_scalar(t["t"], t["g"], W("ICt"), W("ppd"), ALU.subtract, ALU.mult))
                dve.wait_ge(da, 5)
                link(V.tensor_scalar(t["u"], t["u"], 1.0, None, ALU.add))
                link(V.reciprocal(t["u"], t["u"]))
                link(V.tensor_tensor(t["u"], t["u"], t["sp"], ALU.mult))
                link(V.tensor_tensor(t["u"], t["u"], W("bgm"), ALU.mult))
                link(V.tensor_tensor(t["u"], t["u"], t["t"], ALU.mult))
                link(V.tensor_tensor(W("coef"), t["u"], W("gam"), ALU.mult))

            @block.scalar
            def _(act):
                t = {k: v[:, :] for k, v in T.items()}
                act.wait_ge(dv, 3)
                nc.scalar.activation(t["e"], t["a"], ACT.Exp, scale=-1.0).then_inc(da, 1)
                act.wait_ge(da, 1)
                nc.scalar.activation(t["l"], t["e"], ACT.Ln, bias=1.0).then_inc(da, 1)
                act.wait_ge(dv, 12)
                nc.scalar.activation(t["u"], t["v"], ACT.Exp, scale=-1.0).then_inc(da, 1)
                nc.scalar.activation(W("ret"), t["c"], ACT.Exp, scale=-1.0).then_inc(da, 1)
                nc.scalar.activation(t["t"], t["t"], ACT.Tanh).then_inc(da, 1)

    xs = x.rearrange("b (j p) d -> b p j d", p=P)
    ys = out.rearrange("b (j p) d -> b p j d", p=P)

    def one(v, b):
        return v[bass.ds(b, 1)].rearrange("o p j d -> (o p) j d")

    with nc.Fori(0, x.shape[0]) as b:
        with Stage("mamba") as st:
            got = st.sem("got")
            with nc.Block() as block:
                @block.sync
                def _(sp):
                    sp.dma_start(X[:, :, :], one(xs, b)).then_inc(got, 16)
                    sp.wait_ge(got, 16)

            norm_tiles(st, "outer", X, XN, None, transposed=False)

            def keep_residual(link):
                nc.vector.tensor_tensor(X[:, :, :], X[:, :, :], XN[:, :, :], ALU.add)

            zs = st.sb("zs", [P, ND, SEQ])
            xc = st.sb("xc", [P, 2, ND, SEQ])
            delta = st.sb("delta", [P, 2, ND, SEQ])
            du = st.sb("du", [P, 2, ND, SEQ])
            ysum = st.sb("ysum", [P, ND, SEQ])
            bcs = st.sb("bcs", [96, 2, SEQ], BF16)
            dts = st.sb("dts", [DTR + 1, 2, SEQ])
            short = ExitStack()
            XR = st.sb("XR", [P, NJ, D], scope=short)
            norm_tiles(st, "inner", XN, XR, XT, rms=True, gain_t=W("norm_w"), extra=keep_residual)

            xi = st.sb("xi", [P, 2, ND, SEQ + PAD], scope=short)
            pr, zr, conv, conved = st.sem("projected"), st.sem("padded"), st.sem("conv"), st.sem("conved")
            zed, xid, rch, silu = st.sem("zed"), st.sem("xid"), st.sem("reversed"), st.sem("silu")
            with nc.Block() as block:
                @block.tensor
                def _(pe):
                    for e in range(2 * ND):
                        nc.tensor.matmul(PS[e][:, :], W("in_T")[:, e * P:(e + 1) * P], XT[:, :],
                                         start=True, stop=True).then_inc(pr, 1)

                @block.scalar
                def _(act):
                    for t in range(ND):
                        act.wait_ge(pr, t + 1)
                        nc.scalar.copy(xi[:, 0, t, PAD:], PS[t][:, :]).then_inc(xid, 1)
                    for t in range(ND):
                        act.wait_ge(pr, ND + t + 1)
                        nc.scalar.activation(zs[:, t, :], PS[ND + t][:, :], ACT.Silu).then_inc(zed, 1)
                    for i in range(2 * ND):
                        act.wait_ge(conved, i + 1)
                        nc.scalar.activation(xc[:, i // ND, i % ND, :], xc[:, i // ND, i % ND, :],
                                             ACT.Silu).then_inc(silu, 1)

                @block.gpsimd
                def _(pool):
                    nc.gpsimd.memset(xi[:, :, :, 0:PAD], 0.0).then_inc(zr, 1)
                    nc.gpsimd.memset(dts[:, :, :], 1.0).then_inc(zr, 1)
                    for t in range(ND):
                        pool.wait_ge(xid, t + 1)
                        nc.gpsimd.tensor_copy(xi[:, 1, t, PAD:], xi[:, 0, t, SEQ + PAD - 1:PAD - 1:-1]).then_inc(rch, 1)

                @block.vector
                def _(dve):
                    link = Chain(dve, conv)
                    dve.wait_ge(zr, 2)
                    for i in range(2 * ND):
                        d, t = i // ND, i % ND
                        if d:
                            dve.wait_ge(rch, t + 1)
                        else:
                            dve.wait_ge(xid, t + 1)
                        cw = W("conv_w")[:, i * KC:(i + 1) * KC]
                        acc = xc[:, d, t, :]
                        link(nc.vector.tensor_scalar(acc, xi[:, d, t, 0:SEQ], cw[:, 0:1], W("conv_b")[:, i:i + 1],
                                                     ALU.mult, ALU.add))
                        for k in range(1, KC):
                            ins = nc.vector.scalar_tensor_tensor(acc, xi[:, d, t, k:k + SEQ], cw[:, k:k + 1], acc,
                                                                 ALU.mult, ALU.add)
                            if k < KC - 1:
                                link(ins)
                        ins.then_inc(conved, 1)

            short.close()
            short = ExitStack()
            rem = st.sb("rem", [96, SEQ], scope=short)
            soft = st.sb("soft", [P, 3, SEQ], scope=short)

            xp, sc, dtd, dpr = st.sem("xp"), st.sem("sc"), st.sem("dtd"), st.sem("dpr")
            sa, dd, dud = st.sem("sa"), st.sem("dd"), st.sem("dud")
            with nc.Block() as block:
                @block.tensor
                def _(pe):
                    for d in range(2):
                        for t in range(ND):
                            last = nc.tensor.matmul(PS[d][0:96, :], W("xp_bc")[:, (d * ND + t) * 96:(d * ND + t + 1) * 96],
                                                    xc[:, d, t, :], start=(t == 0), stop=(t == ND - 1))
                        for t in range(ND):
                            last = nc.tensor.matmul(PS[2 + d][0:DTR, :],
                                                    W("xp_dt")[:, (d * ND + t) * DTR:(d * ND + t + 1) * DTR],
                                                    xc[:, d, t, :], start=(t == 0), stop=(t == ND - 1))
                        last.then_inc(xp, 1)
                    for d in range(2):
                        pe.wait_ge(dtd, d + 1)
                        for t in range(ND):
                            i = d * ND + t
                            nc.tensor.matmul(PS[4 + i][:, :], W("dt_T", DTR + 1)[:, i * P:(i + 1) * P],
                                             dts[:, d, :], start=True, stop=True).then_inc(dpr, 1)

                @block.scalar
                def _(act):
                    for d in range(2):
                        act.wait_ge(xp, d + 1)
                        nc.scalar.copy(dts[0:DTR, d, :], PS[2 + d][0:DTR, :]).then_inc(dtd, 1)
                    n = 0
                    for i in range(2 * ND):
                        act.wait_ge(dpr, i + 1)
                        if i:
                            act.wait_ge(dd, i)
                        nc.scalar.activation(soft[:, 0, :], PS[4 + i][:, :], ACT.Abs).then_inc(sa, 1)
                        act.wait_ge(sa, 3 * i + 1)
                        nc.scalar.activation(soft[:, 1, :], soft[:, 0, :], ACT.Exp, scale=-1.0).then_inc(sa, 1)
                        act.wait_ge(sa, 3 * i + 2)
                        nc.scalar.activation(soft[:, 2, :], soft[:, 1, :], ACT.Ln, bias=1.0).then_inc(sa, 1)

                @block.vector
                def _(dve):
                    link = Chain(dve, sc)
                    V = nc.vector
                    for d in range(2):
                        dve.wait_ge(xp, d + 1)
                        src = PS[d]
                        link(V.tensor_copy(bcs[:, d, :], src[0:96, :]))
                        link(V.tensor_tensor(rem[:, :], src[0:96, :], bcs[:, d, :], ALU.subtract))
                        link(V.tensor_copy(bcs[32:64, d, :], rem[32:64, :]))
                        link(V.tensor_copy(bcs[64:96, d, :], rem[64:96, :]))
                        link(V.tensor_tensor(rem[64:96, :], rem[64:96, :], bcs[64:96, d, :], ALU.subtract))
                        link(V.tensor_copy(bcs[64:96, d, :], rem[64:96, :]))
                    for i in range(2 * ND):
                        d, t = i // ND, i % ND
                        dve.wait_ge(sa, 3 * i + 3)
                        link(V.tensor_scalar(soft[:, 0, :], soft[:, 1, :], 1.0, -1.0, ALU.add, ALU.add))
                        link(V.tensor_tensor(soft[:, 2, :], soft[:, 2, :], soft[:, 0, :], ALU.subtract))
                        link(V.tensor_tensor(soft[:, 2, :], soft[:, 2, :], soft[:, 1, :], ALU.add))
                        V.scalar_tensor_tensor(delta[:, d, t, :], PS[4 + i][:, :], 0.0, soft[:, 2, :],
                                               ALU.max, ALU.add).then_inc(dd, 1)

                @block.gpsimd
                def _(pool):
                    for i in range(2 * ND):
                        pool.wait_ge(dd, i + 1)
                        nc.gpsimd.tensor_tensor(du[:, i // ND, i % ND, :], delta[:, i // ND, i % ND, :],
                                                xc[:, i // ND, i % ND, :], ALU.mult).then_inc(dud, 1)

            short.close()

            UN = 2 * NS * ND
            R = 2
            decay = st.sb("decay", [P, R, SEQ])
            drive = st.sb("drive", [P, R, SEQ])
            state = st.sb("state", [P, R, SEQ])
            read = st.sb("read", [P, R, SEQ])
            c_all = st.sb("c_all", [P, 2, SEQ])
            bcast, c_cp, dec, drv = st.sem("bcast"), st.sem("c_cp"), st.sem("dec"), st.sem("drv")
            scn, rd, acc, yev = st.sem("scn"), st.sem("rd"), st.sem("acc"), st.sem("yev")
            ych, outp = st.sem("ych"), st.sem("outp")
            with nc.Block() as block:
                @block.tensor
                def _(pe):
                    def spread(m):
                        d, n = m // NS, m % NS
                        if m >= 2:
                            pe.wait_ge(drv, ND * (m - 1))
                            pe.wait_ge(c_cp, m - 1)
                        nc.tensor.matmul(PS[m % 2][:, :], WBF("sel_bc", 96)[:, n * P:(n + 1) * P],
                                         bcs[:, d, :], start=True, stop=True)
                        nc.tensor.matmul(PS[2 + m % 2][:, :], WBF("sel_bc", 96)[:, (NS + n) * P:(NS + n + 1) * P],
                                         bcs[:, d, :], start=True, stop=True).then_inc(bcast, 1)

                    spread(0)
                    for m in range(2 * NS):
                        if m + 1 < 2 * NS:
                            spread(m + 1)
                        d, n = m // NS, m % NS
                        for t in range(ND):
                            u = m * ND + t
                            pe.wait_ge(rd, u + 1)
                            nc.tensor.matmul(PS[4 + 2 * d + t][:, :], ident, read[:, u % R, :],
                                             start=(n == 0), stop=(n == NS - 1)).then_inc(acc, 1)
                    pe.wait_ge(yev, 1)
                    for j in range(NJ):
                        for t in range(ND):
                            last = nc.tensor.matmul(PS[0][:, j * D:(j + 1) * D], ysum[:, t, j * P:(j + 1) * P],
                                                    W("out_T")[:, t * D:(t + 1) * D], start=(t == 0), stop=(t == ND - 1))
                    last.then_inc(outp, 1)

                @block.scalar
                def _(act):
                    for m in range(2 * NS):
                        d, n = m // NS, m % NS
                        act.wait_ge(bcast, m + 1)
                        if m >= 2:
                            act.wait_ge(rd, ND * (m - 1))
                        nc.scalar.copy(c_all[:, m % 2, :], PS[2 + m % 2][:, :]).then_inc(c_cp, 1)
                        for t in range(ND):
                            u = m * ND + t
                            if u >= R:
                                act.wait_ge(scn, u - R + 1)
                            a = (d * ND + t) * NS + n
                            nc.scalar.activation(decay[:, u % R, :], delta[:, d, t, :], ACT.Exp,
                                                 scale=W("A")[:, a:a + 1]).then_inc(dec, 1)

                @block.vector
                def _(dve):
                    V = nc.vector

                    def drive_unit(u):
                        m, t = u // ND, u % ND
                        dve.wait_ge(bcast, m + 1)
                        if u >= R:
                            dve.wait_ge(scn, u - R + 1)
                        V.tensor_tensor(drive[:, u % R, :], PS[m % 2][:, :], du[:, m // NS, t, :],
                                        ALU.mult).then_inc(drv, 1)

                    drive_unit(0)
                    for u in range(UN):
                        if u + 1 < UN:
                            drive_unit(u + 1)
                        dve.wait_ge(dec, u + 1)
                        dve.wait_ge(drv, u + 1)
                        if u >= R:
                            dve.wait_ge(rd, u - R + 1)
                        V.tensor_tensor_scan(state[:, u % R, :], decay[:, u % R, :], drive[:, u % R, :], 0.0,
                                             ALU.mult, ALU.add).then_inc(scn, 1)
                    link = Chain(dve, ych)
                    dve.wait_ge(acc, UN)
                    for t in range(ND):
                        V.scalar_tensor_tensor(ysum[:, t, :], xc[:, 0, t, :], W("D")[:, t:t + 1], PS[4 + t][:, :],
                                               ALU.mult, ALU.add)
                        link(V.scalar_tensor_tensor(xc[:, 1, t, :], xc[:, 1, t, :], W("D")[:, ND + t:ND + t + 1],
                                                    PS[6 + t][:, :], ALU.mult, ALU.add))
                        link(V.tensor_tensor(ysum[:, t, :], ysum[:, t, :], xc[:, 1, t, ::-1], ALU.add))
                        ins = V.scalar_tensor_tensor(ysum[:, t, :], ysum[:, t, :], 0.5, zs[:, t, :], ALU.mult, ALU.mult)
                    ins.then_inc(yev, 1)
                    dve.wait_ge(outp, 1)
                    V.tensor_tensor(X[:, :, :], X[:, :, :], PS[0][:, :].rearrange(tiles, j=NJ), ALU.add)

                @block.gpsimd
                def _(pool):
                    for u in range(UN):
                        m = u // ND
                        pool.wait_ge(scn, u + 1)
                        pool.wait_ge(c_cp, m + 1)
                        if u >= R:
                            pool.wait_ge(acc, u - R + 1)
                        nc.gpsimd.tensor_tensor(read[:, u % R, :], state[:, u % R, :], c_all[:, m % 2, :],
                                                ALU.mult).then_inc(rd, 1)

        with Stage("moe0") as st:
            norm_tiles(st, "ln", X, XN, XT)
            comb, comb_t = st.sb("comb", [P, NJ, E0]), st.sb("comb_t", [E0, SEQ])
            gates(st, XT, W("gate_T"), E0, comb, comb_t, grouped_bias=W("gate_b"))
            NP0 = E0 * INTER // P + 1
            s1 = st.sb("s1", [P, 2, SEQ])
            g = st.sb("g", [P, 2, SEQ])
            hid, act1, gated, used, ch = st.sem("hid"), st.sem("act1"), st.sem("gated"), st.sem("used"), st.sem("ch")
            with nc.Block() as block:
                @block.tensor
                def _(pe):
                    def down(r):
                        pe.wait_ge(gated, r + 1)
                        for j in range(NJ):
                            last = nc.tensor.matmul(PS[6][:, j * D:(j + 1) * D], g[:, r % 2, j * P:(j + 1) * P],
                                                    W("We2")[:, r * D:(r + 1) * D], start=(r == 0 and j == 0), stop=False,
                                                    skip_group_check=True)
                        last.then_inc(used, 1)

                    for r in range(NP0):
                        if r >= 2:
                            pe.wait_ge(gated, r - 1)
                        k = 3 * (r % 2)
                        nc.tensor.matmul(PS[k][:, :], W("We1")[:, r * P:(r + 1) * P], XT[:, :], start=True, stop=True)
                        last = nc.tensor.matmul(PS[k + 1][:, :], W("We3")[:, r * P:(r + 1) * P], XT[:, :],
                                                start=True, stop=True)
                        if r < NP0 - 1:
                            last = nc.tensor.matmul(PS[k + 2][:, :], W("sel_e0", E0)[:, r * P:(r + 1) * P], comb_t[:, :],
                                                    start=True, stop=True)
                        last.then_inc(hid, 1)
                        if r:
                            down(r - 1)
                    down(NP0 - 1)
                    for j in range(NJ):
                        last = nc.tensor.matmul(PS[6][:, j * D:(j + 1) * D], comb_t[:, j * P:(j + 1) * P],
                                                W("be2", E0), start=False, stop=(j == NJ - 1), skip_group_check=True)
                    last.then_inc(used, 1)

                @block.scalar
                def _(act):
                    for r in range(NP0):
                        act.wait_ge(hid, r + 1)
                        if r >= 2:
                            act.wait_ge(gated, r - 1)
                        nc.scalar.activation(s1[:, r % 2, :], PS[3 * (r % 2)][:, :], ACT.Silu,
                                             bias=W("be1")[:, r:r + 1]).then_inc(act1, 1)

                @block.vector
                def _(dve):
                    link = Chain(dve, ch)
                    V = nc.vector
                    for r in range(NP0):
                        dve.wait_ge(act1, r + 1)
                        if r >= 2:
                            dve.wait_ge(used, r - 1)
                        k = 3 * (r % 2)
                        ins = V.scalar_tensor_tensor(g[:, r % 2, :], PS[k + 1][:, :], W("be3")[:, r:r + 1],
                                                     s1[:, r % 2, :], ALU.add, ALU.mult)
                        if r < NP0 - 1:
                            link(ins)
                            ins = V.tensor_tensor(g[:, r % 2, :], g[:, r % 2, :], PS[k + 2][:, :], ALU.mult)
                        ins.then_inc(gated, 1)
                    link(V.tensor_tensor(X[:, :, :], X[:, :, :], bc(W("bs2").unsqueeze(1), [P, NJ, D]), ALU.add))
                    dve.wait_ge(used, NP0 + 1)
                    V.tensor_tensor(X[:, :, :], X[:, :, :], PS[6][:, :].rearrange(tiles, j=NJ), ALU.add)

        with Stage("attn1") as st:
            norm_tiles(st, "ln", X, XN, XT)
            vals = st.sb("vals", [P, NJ, H, DK + 1])
            O = st.sb("O", [P, NJ, H * DK])
            qk = st.sb("qk", [P, 2, 2, SEQ])
            toep = st.sb("toep", [P, 2, TW])
            vp, vc = st.sem("vp"), st.sem("vc")
            with nc.Block() as block:
                @block.tensor
                def _(pe):
                    for i in range(2 * NJ):
                        j, c = i // 2, i % 2
                        if i >= 4:
                            pe.wait_ge(vc, i - 3)
                        nc.tensor.matmul(PS[i % 4][:, :], XT[:, j * P:(j + 1) * P], W("Wv")[:, c * 512:(c + 1) * 512],
                                         start=True, stop=True).then_inc(vp, 1)

                @block.gpsimd
                def _(pool):
                    nc.gpsimd.memset(vals[:, :, :, DK], 1.0)

                @block.scalar
                def _(act):
                    for i in range(2 * NJ):
                        j, c = i // 2, i % 2
                        act.wait_ge(vp, i + 1)
                        nc.scalar.copy(vals[:, j, c * 8:(c + 1) * 8, 0:DK],
                                       PS[i % 4][:, :].rearrange("p (h v) -> p h v", v=DK)).then_inc(vc, 1)

            toep_ld = [st.sem(f"toep_ld{i}") for i in range(2)]
            qk_ps, qk_cp = st.sem("qk_ps"), st.sem("qk_cp")

            def load_bias(block):
                @block.sync
                def _(sp):
                    for h in range(H):
                        if h >= 2:
                            sp.wait_ge(st.sems["maxed"], NJ * (h - 1))
                        line = bias_dram[h:h + 1, :]
                        src = bass.AP(line.tensor, line.offset, [[1, P], [1, TW]])
                        sp.dma_start(toep[:, h % 2, :], src).then_inc(toep_ld[h % 2], 16)

            def copies(s):
                if s == 0:
                    return [(0, 0), (0, 1)]
                at = {4: 0, 6: 1}.get(s % (2 * NJ))
                return [(s // (2 * NJ) + 1, at)] if at is not None and s // (2 * NJ) + 1 < H // 2 else []

            def project_ahead(pe, s):
                for r, i in copies(s + 1) if s else copies(0):
                    if 2 * r + i:
                        pe.wait_ge(qk_cp, 2 * r + i)
                    nc.tensor.matmul(PS[7][:, :], W(("Wq", "Wk")[i])[:, r * P:(r + 1) * P], XT[:, :],
                                     start=True, stop=True).then_inc(qk_ps, 1)

            def copy_ahead(act, s):
                for r, i in copies(s):
                    act.wait_ge(qk_ps, 2 * r + i + 1)
                    dst = qk[:, r % 2, i, :].rearrange("p (j t) -> p j t", j=NJ)
                    nc.scalar.copy(dst if i else dst[:, :, ::-1],
                                   PS[7][:, :].rearrange("p (j t) -> p j t", j=NJ)).then_inc(qk_cp, 1)

            def scores1(pe, u, ps):
                h, j = u // NJ, u % NJ
                if j == 0 and h % 2 == 0:
                    pe.wait_ge(qk_cp, h + 2)
                o = DK * (h % 2)
                q, k = qk[o:o + DK, (h // 2) % 2, 0, :], qk[o:o + DK, (h // 2) % 2, 1, :]
                return nc.tensor.matmul(ps, q[:, j * P:(j + 1) * P], k, start=True, stop=True)

            def bias_of(dve, u):
                h, j = u // NJ, u % NJ
                if j == 0:
                    dve.wait_ge(toep_ld[h % 2], 16 * (h // 2 + 1))
                c = P * (NJ - 1 - j)
                return toep[:, h % 2, c:c + SEQ]

            attention(st, scores1, vals, DK, O, bias_of=bias_of, loads=load_bias, pe_ahead=project_ahead,
                      act_ahead=copy_ahead)

            ot = st.sb("ot", [P, 2, SEQ])
            tn, ev, dn, ad = st.sem("tn"), st.sem("ev"), st.sem("dn"), st.sem("ad")
            NC1 = H * DK // P
            with nc.Block() as block:
                @block.tensor
                def _(pe):
                    def project(c):
                        pe.wait_ge(ev, c + 1)
                        for j in range(NJ):
                            last = nc.tensor.matmul(PS[4][:, j * D:(j + 1) * D], ot[:, c % 2, j * P:(j + 1) * P],
                                                    W("Wo")[:, c * D:(c + 1) * D], start=(c == 0 and j == 0),
                                                    stop=(c == NC1 - 1 and j == NJ - 1), skip_group_check=True)
                        last.then_inc(dn, 1)

                    for c in range(NC1):
                        if c >= 2:
                            pe.wait_ge(ev, c - 1)
                        for j in range(NJ):
                            last = nc.tensor.transpose(PS[c % 2][:, j * P:(j + 1) * P], O[:, j, c * P:(c + 1) * P], ident)
                        last.then_inc(tn, 1)
                        if c:
                            project(c - 1)
                    project(NC1 - 1)

                @block.scalar
                def _(act):
                    for c in range(NC1):
                        act.wait_ge(tn, c + 1)
                        if c >= 2:
                            act.wait_ge(dn, c - 1)
                        nc.scalar.copy(ot[:, c % 2, :].rearrange("p (j t) -> p j t", j=NJ)[:, :, ::-1],
                                       PS[c % 2][:, :].rearrange("p (j t) -> p j t", j=NJ)).then_inc(ev, 1)

                @block.vector
                def _(dve):
                    dve.wait_ge(dn, NC1)
                    nc.vector.tensor_tensor(X[:, :, :], X[:, :, :], PS[4][:, :].rearrange(tiles, j=NJ), ALU.add)

        with Stage("lora1") as st:
            norm_tiles(st, "ln", X, XN, XT)
            comb, comb_t = st.sb("comb", [P, NJ, E1]), st.sb("comb_t", [E1, SEQ])
            gates(st, XT, W("R_T"), E1, comb, comb_t, eps=1e-6)
            gh, gh_t = st.sb("gh", [P, NJ, E1 * R1]), st.sb("gh_t", [P, SEQ])
            low, gated, tn, ev, dn, ch = (st.sem(n) for n in ("low", "gated", "tn", "ev", "dn", "ch"))
            with nc.Block() as block:
                @block.tensor
                def _(pe):
                    for j in range(NJ):
                        last = nc.tensor.matmul(PS[0][:, j * P:(j + 1) * P], XT[:, j * P:(j + 1) * P], W("A1_T"),
                                                start=True, stop=True)
                    last.then_inc(low, 1)
                    pe.wait_ge(gated, 1)
                    for j in range(NJ):
                        last = nc.tensor.transpose(PS[1][:, j * P:(j + 1) * P], gh[:, j, :], ident)
                    last.then_inc(tn, 1)
                    pe.wait_ge(ev, 1)
                    for j in range(NJ):
                        nc.tensor.matmul(PS[2][:, j * P:(j + 1) * P], XT[:, j * P:(j + 1) * P], W("W_T"),
                                         start=True, stop=False)
                        last = nc.tensor.matmul(PS[2][:, j * P:(j + 1) * P], gh_t[:, j * P:(j + 1) * P], W("B1"),
                                                start=False, stop=True)
                    last.then_inc(dn, 1)

                @block.vector
                def _(dve):
                    link = Chain(dve, ch)
                    dve.wait_ge(low, 1)
                    for j in range(NJ):
                        last = nc.vector.tensor_tensor(
                            gh[:, j, :].rearrange("p (e r) -> p e r", r=R1),
                            PS[0][:, j * P:(j + 1) * P].rearrange("p (e r) -> p e r", r=R1),
                            bc(comb[:, j, :].unsqueeze(2), [P, E1, R1]), ALU.mult)
                    last.then_inc(gated, 1)
                    link(nc.vector.tensor_tensor(X[:, :, :], X[:, :, :], bc(W("b_1").unsqueeze(1), [P, NJ, D]), ALU.add))
                    dve.wait_ge(dn, 1)
                    nc.vector.tensor_tensor(X[:, :, :], X[:, :, :], PS[2][:, :].rearrange(tiles, j=NJ), ALU.add)

                @block.scalar
                def _(act):
                    act.wait_ge(tn, 1)
                    nc.scalar.copy(gh_t[:, :], PS[1][:, :]).then_inc(ev, 1)

        def rope_attention(st, w_qkv, bias, half, causal, O):
            qkv = st.sb("qkv", [P, NJ, 2 * D])
            rot = st.sb("rot", [P, NJ, 2 * D])
            vals = st.sb("vals", [P, NJ, H, HD + 1])
            tmp = st.sb("tmp", [P, 2, NJ, D])
            parts = [st.sb(f"parts_{n}", [P, NJ * H, HS], BF16) for n in "qk"]
            turned = [st.sb(f"parts_{n}T", [P, H // 2, SEQ], BF16) for n in "qk"]
            pj, one_, vcp, qcp, ch = (st.sem(n) for n in ("pj", "one", "vcp", "qcp", "rchain"))
            ready, tn, ev, zero = (st.sem(n) for n in ("ready", "ttn", "tev", "zero"))
            with nc.Block() as block:
                @block.gpsimd
                def _(pool):
                    nc.gpsimd.memset(vals[:, :, :, HD], 1.0)
                    for i in range(2):
                        nc.gpsimd.memset(parts[i][:, :, SK:], 0.0).then_inc(zero, 1)

                @block.tensor
                def _(pe):
                    for j in range(NJ):
                        nc.tensor.matmul(PS[j][:, 0:3 * D], XT[:, j * P:(j + 1) * P], w_qkv,
                                         start=True, stop=True).then_inc(pj, 1)
                    pe.wait_ge(zero, 2)
                    n = 0
                    for i in range(2):
                        pe.wait_ge(ready, i + 1)
                        view = parts[i][:, :, :].rearrange("p (j r) s -> p j (r s)", j=NJ)
                        for r in range(H // 2):
                            if n >= 4:
                                pe.wait_ge(ev, n - 3)
                            bank = PS[4 + n % 4][:, :].bitcast(BF16)
                            for j in range(NJ):
                                last = nc.tensor.transpose(bank[:, j * P:(j + 1) * P],
                                                           view[:, j, r * P:(r + 1) * P], ident_b)
                            last.then_inc(tn, 1)
                            n += 1

                @block.scalar
                def _(act):
                    for j in range(NJ if bias is None else 0):
                        act.wait_ge(pj, j + 1)
                        nc.scalar.copy(qkv[:, j, :], PS[j][:, 0:2 * D]).then_inc(qcp, 1)
                        nc.scalar.copy(vals[:, j, :, 0:HD],
                                       PS[j][:, 2 * D:3 * D].rearrange("p (h v) -> p h v", v=HD)).then_inc(vcp, 1)
                    n = 0
                    for i in range(2):
                        for r in range(H // 2):
                            act.wait_ge(tn, n + 1)
                            nc.scalar.copy(turned[i][:, r, :], PS[4 + n % 4][:, 0:SEQ // 2].bitcast(BF16)).then_inc(ev, 1)
                            n += 1

                @block.vector
                def _(dve):
                    V = nc.vector
                    link = Chain(dve, ch)
                    if bias is None:
                        dve.wait_ge(qcp, NJ)
                    else:
                        for j in range(NJ):
                            dve.wait_ge(pj, j + 1)
                            V.tensor_tensor(vals[:, j, :, 0:HD], PS[j][:, 2 * D:3 * D].rearrange("p (h v) -> p h v", v=HD),
                                            bias[:, 2 * D:3 * D].rearrange("p (h v) -> p h v", v=HD), ALU.add)
                            last = V.tensor_tensor(qkv[:, j, :], PS[j][:, 0:2 * D], bias[:, 0:2 * D], ALU.add)
                        link(last)

                    def ends(t):
                        if half:
                            v = t[:, :, :].rearrange("p j (h a f) -> p j h a f", a=2, f=HD // 2)
                            return v[:, :, :, 0, :], v[:, :, :, 1, :]
                        v = t[:, :, :].rearrange("p j (h f a) -> p j h f a", a=2, f=HD // 2)
                        return v[:, :, :, :, 0], v[:, :, :, :, 1]

                    x1, x2 = ends(qkv)
                    r1, r2 = ends(rot)
                    shape = [P, NJ, 2 * H, HD // 2]
                    f = "p (j f) -> p j f"
                    cos = bc(W("cos").rearrange(f, j=NJ).unsqueeze(2), shape)
                    sin = bc(W("sin").rearrange(f, j=NJ).unsqueeze(2), shape)
                    t1, t2 = (tmp[:, i, :, :].rearrange("p j (h f) -> p j h f", f=HD // 2) for i in range(2))
                    V.tensor_tensor(t1, x1, cos, ALU.mult)
                    link(V.tensor_tensor(t2, x2, sin, ALU.mult))
                    link(V.tensor_tensor(r1, t1, t2, ALU.subtract))
                    V.tensor_tensor(t1, x1, sin, ALU.mult)
                    link(V.tensor_tensor(t2, x2, cos, ALU.mult))
                    link(V.tensor_tensor(r2, t1, t2, ALU.add))
                    link(V.tensor_scalar(rot[:, :, 0:D], rot[:, :, 0:D], float(HD) ** -0.5, None, ALU.mult))
                    for i, slots in enumerate((((0, 1, 2), (3, 4), (5,)), ((0, 3, 5), (1, 4), (2,)))):
                        left = rot[:, :, i * D:(i + 1) * D]
                        flat = left.rearrange("p j (h f) -> p j h f", f=HD)
                        part = parts[i][:, :, :].rearrange("p (j h) s -> p j h s", j=NJ)
                        for lvl, where in enumerate(slots):
                            first = part[:, :, :, where[0] * HD:(where[0] + 1) * HD]
                            if lvl == 2:
                                V.tensor_copy(first, flat).then_inc(ready, 1)
                                continue
                            link(V.tensor_copy(first, flat))
                            for w in where[1:]:
                                V.tensor_copy(part[:, :, :, w * HD:(w + 1) * HD], first)
                            link(V.tensor_tensor(flat, flat, first, ALU.subtract))

            def scores(pe, u, ps):
                h, j = u // NJ, u % NJ
                o = HS * (h % 2)
                q = turned[0][o:o + SK, h // 2, j * P:(j + 1) * P]
                k = turned[1][o:o + SK, h // 2, 0:ps.shape[1]]
                if not causal:
                    return nc.tensor.matmul(ps, q, k, start=True, stop=True)
                nc.tensor.matmul(ps, q, k, start=True, stop=False)
                return nc.tensor.matmul(ps[:, j * P:(j + 1) * P], ident_b, WBF("later"), start=False, stop=True)

            attention(st, scores, vals, HD, O, causal=causal)

        def project_back(st, tag, O, w_o, add_to, bias=None):
            tn, ev, dn, ch = (st.sem(f"{tag}_{n}") for n in ("tn", "ev", "dn", "ch"))
            ot = st.sb(f"{tag}_ot", [P, SEQ])
            with nc.Block() as block:
                @block.tensor
                def _(pe):
                    for j in range(NJ):
                        last = nc.tensor.transpose(PS[0][:, j * P:(j + 1) * P], O[:, j, :], ident)
                    last.then_inc(tn, 1)
                    pe.wait_ge(ev, 1)
                    for j in range(NJ):
                        last = nc.tensor.matmul(PS[1][:, j * P:(j + 1) * P], ot[:, j * P:(j + 1) * P], w_o,
                                                start=True, stop=True)
                    last.then_inc(dn, 1)

                @block.scalar
                def _(act):
                    act.wait_ge(tn, 1)
                    nc.scalar.copy(ot[:, :], PS[0][:, :]).then_inc(ev, 1)

                @block.vector
                def _(dve):
                    link = Chain(dve, ch)
                    if bias is not None:
                        link(nc.vector.tensor_tensor(add_to[:, :, :], add_to[:, :, :], bc(bias.unsqueeze(1), [P, NJ, D]), ALU.add))
                    dve.wait_ge(dn, 1)
                    nc.vector.tensor_tensor(add_to[:, :, :], add_to[:, :, :], PS[1][:, :].rearrange(tiles, j=NJ), ALU.add)

        with Stage("attn2") as st:
            norm_tiles(st, "ln", X, XN, XT)
            O = st.sb("O", [P, NJ, D])
            rope_attention(st, W("qkv2"), None, False, True, O)
            project_back(st, "pb", O, W("o2"), X)

        def experts(st, w_up, w_gate, b_up, b_gate, w_down, b_down, E, tiles_per, func, comb, comb_t, acc):
            n = E * tiles_per
            NB = 2 if w_gate is not None else 4
            a1 = st.sb("a1", [P, 3, SEQ])
            s1 = st.sb("s1", [P, 2, SEQ]) if w_gate is not None else None
            hid, acted, gated, used, weighed, ch = (st.sem(f"x_{k}") for k in ("hid", "acted", "gated", "used", "weighed", "ch"))
            hidden_done = gated if w_gate is not None else acted
            with nc.Block() as block:
                @block.tensor
                def _(pe):
                    def down(i):
                        e, t = i // tiles_per, i % tiles_per
                        pe.wait_ge(hidden_done, i + 1)
                        if t == 0 and e >= 2:
                            pe.wait_ge(weighed, e - 1)
                        for j in range(NJ):
                            last = nc.tensor.matmul(PS[4 + e % 2][:, j * D:(j + 1) * D], a1[:, i % 3, j * P:(j + 1) * P],
                                                    w_down[:, i * D:(i + 1) * D], start=(t == 0 and j == 0),
                                                    stop=(t == tiles_per - 1 and j == NJ - 1), skip_group_check=True)
                        last.then_inc(used, 1)

                    for j in range(NJ):
                        nc.tensor.matmul(PS[6][:, j * D:(j + 1) * D], comb_t[:, j * P:(j + 1) * P], b_down,
                                         start=True, stop=True)
                    for i in range(n):
                        if i >= NB:
                            pe.wait_ge(hidden_done, i - NB + 1)
                        last = nc.tensor.matmul(PS[i % NB][:, :], w_up[:, i * P:(i + 1) * P], XT[:, :], start=True, stop=True)
                        if w_gate is not None:
                            last = nc.tensor.matmul(PS[2 + i % NB][:, :], w_gate[:, i * P:(i + 1) * P], XT[:, :],
                                                    start=True, stop=True)
                        last.then_inc(hid, 1)
                        if i >= 1:
                            down(i - 1)
                    down(n - 1)

                @block.scalar
                def _(act):
                    for i in range(n):
                        act.wait_ge(hid, i + 1)
                        if w_gate is None:
                            if i >= 3:
                                act.wait_ge(used, i - 2)
                            nc.scalar.activation(a1[:, i % 3, :], PS[i % NB][:, :], func, bias=b_up[:, i:i + 1]).then_inc(acted, 1)
                        else:
                            if i >= 2:
                                act.wait_ge(gated, i - 1)
                            nc.scalar.activation(s1[:, i % 2, :], PS[i % NB][:, :], func, bias=b_up[:, i:i + 1]).then_inc(acted, 1)

                @block.vector
                def _(dve):
                    V = nc.vector
                    link = Chain(dve, ch)

                    def weigh(e):
                        dve.wait_ge(used, (e + 1) * tiles_per)
                        for j in range(NJ):
                            last = V.scalar_tensor_tensor(acc[:, j, :], PS[4 + e % 2][:, j * D:(j + 1) * D],
                                                          comb[:, j, e:e + 1], acc[:, j, :], ALU.mult, ALU.add)
                        last.then_inc(weighed, 1)
                        dve.wait_ge(weighed, e + 1)

                    for i in range(n):
                        if w_gate is not None:
                            dve.wait_ge(acted, i + 1)
                            if i >= 3:
                                dve.wait_ge(used, i - 2)
                            V.scalar_tensor_tensor(a1[:, i % 3, :], PS[2 + i % NB][:, :], b_gate[:, i:i + 1], s1[:, i % 2, :],
                                                   ALU.add, ALU.mult).then_inc(gated, 1)
                        if i % tiles_per == 1 and i >= tiles_per:
                            weigh(i // tiles_per - 1)
                    weigh(E - 1)
                    V.tensor_tensor(acc[:, :, :], acc[:, :, :], PS[6][:, :].rearrange(tiles, j=NJ), ALU.add)

        with Stage("block2") as st0:
            Y = st0.sb("Y", [P, NJ, D])
            with Stage("inner2") as st:
                norm_tiles(st, "ln", X, XN, XT)
                O = st.sb("O", [P, NJ, D])
                rope_attention(st, W("qkv3"), W("bqkv3"), True, False, O)
                project_back(st, "pb", O, W("o3"), XN, bias=W("bo3"))
            norm_tiles(st0, "ln1", XN, Y, XT, gain=W("g1"), shift=W("be1_2"))
            comb, comb_t = st0.sb("comb", [P, NJ, E2]), st0.sb("comb_t", [E2, SEQ])
            gates(st0, XT, W("Wg2"), E2, comb, comb_t, bias=W("bg2"), eps=0.0)
            experts(st0, W("W1_2"), None, W("b1_2"), None, W("W2_2"), W("b2_2", E2), E2, FF // P, ACT.Gelu, comb, comb_t, Y)

            def add_back(link):
                nc.vector.tensor_tensor(X[:, :, :], X[:, :, :], XN[:, :, :], ALU.add)

            norm_tiles(st0, "ln2", Y, XN, None, gain=W("g2"), shift=W("be2_2"), extra=add_back, transposed=False)

        with Stage("memory") as st:
            norm_tiles(st, "ln", X, XN, XT)
            qkv = st.sb("qkv", [P, NJ, 3 * D])
            sq = st.sb("sq", [P, NJ, D])
            mu = st.sb("mu", [P, NJ * H])
            var = st.sb("var", [P, NJ * H])
            qkv_t = st.sb("qkv_t", [P, 3, SEQ])
            pj, cp, ch, kn, tn, ev, vsh, vrt = (st.sem(n) for n in ("pj", "cp", "ch", "kn", "tn", "ev", "vsh", "vrt"))
            with nc.Block() as block:
                @block.gpsimd
                def _(pool):
                    pool.wait_ge(vsh, 1)
                    nc.gpsimd.tensor_tensor(var[:, :], var[:, :], W("minus_half"), ALU.pow).then_inc(vrt, 1)

                @block.tensor
                def _(pe):
                    for j in range(NJ):
                        nc.tensor.matmul(PS[j][:, 0:3 * D], XT[:, j * P:(j + 1) * P], W("qkv4"),
                                         start=True, stop=True).then_inc(pj, 1)
                    for n, i in enumerate((0, 2, 1)):
                        if i == 1:
                            pe.wait_ge(kn, 1)
                        else:
                            pe.wait_ge(cp, NJ)
                        for j in range(NJ):
                            last = nc.tensor.transpose(PS[4 + n][:, j * P:(j + 1) * P], qkv[:, j, i * D:(i + 1) * D], ident)
                        last.then_inc(tn, 1)

                @block.scalar
                def _(act):
                    for j in range(NJ):
                        act.wait_ge(pj, j + 1)
                        nc.scalar.copy(qkv[:, j, :], PS[j][:, 0:3 * D]).then_inc(cp, 1)
                    for n, i in enumerate((0, 2, 1)):
                        act.wait_ge(tn, n + 1)
                        nc.scalar.copy(qkv_t[:, i, :], PS[4 + n][:, :]).then_inc(ev, 1)

                @block.vector
                def _(dve):
                    link = Chain(dve, ch)
                    V = nc.vector
                    dve.wait_ge(cp, NJ)
                    k = qkv[:, :, D:2 * D].rearrange("p j (h f) -> p j h f", f=HD)
                    s4 = sq[:, :, :].rearrange("p j (h f) -> p j h f", f=HD)
                    shape = [P, NJ, H, HD]
                    mu_v = mu[:, :].rearrange("p (j h) -> p j h", j=NJ)
                    var_v = var[:, :].rearrange("p (j h) -> p j h", j=NJ)
                    link(V.tensor_reduce(mu_v, k, AX.X, ALU.add))
                    link(V.tensor_scalar(mu[:, :], mu[:, :], 1.0 / HD, None, ALU.mult))
                    link(V.tensor_tensor(k, k, bc(mu_v.unsqueeze(3), shape), ALU.subtract))
                    link(V.tensor_tensor(s4, k, k, ALU.mult))
                    link(V.tensor_reduce(var_v, s4, AX.X, ALU.add))
                    V.tensor_scalar(var[:, :], var[:, :], 1.0 / HD, EPS, ALU.mult, ALU.add).then_inc(vsh, 1)
                    dve.wait_ge(vrt, 1)
                    V.tensor_tensor(k, k, bc(var_v.unsqueeze(3), shape), ALU.mult).then_inc(kn, 1)

            vrc = st.sb("vrc", [P, 2, SEQ])
            heb = st.sb("heb", [P, 2, SEQ])
            mem = st.sb("mem", [P, 2, SEQ])
            red = st.sb("red", [P, 2, SEQ])
            yt = st.sb("yt", [P, SEQ])
            reps, vd, hd, sd, gd, summed, yev, dn = (st.sem(n) for n in ("reps", "vd", "hd", "sd", "gd", "summed", "yev", "dn"))
            with nc.Block() as block:
                @block.tensor
                def _(pe):
                    def total(g):
                        pe.wait_ge(gd, g + 1)
                        nc.tensor.matmul(PS[6][:, :], W("sel_sum")[:, g * P:(g + 1) * P], red[:, g % 2, :],
                                         start=(g == 0), stop=(g == NG - 1)).then_inc(summed, 1)

                    for g in range(NG):
                        if g >= 2:
                            pe.wait_ge(gd, g - 1)
                        k = 3 * (g % 2)
                        nc.tensor.matmul(PS[k][:, :], W("sel_d")[:, g * P:(g + 1) * P], qkv_t[:, 2, :], start=True, stop=True)
                        nc.tensor.matmul(PS[k + 1][:, :], W("sel_e")[:, g * P:(g + 1) * P], qkv_t[:, 1, :], start=True, stop=True)
                        nc.tensor.matmul(PS[k + 2][:, :], W("sel_e")[:, g * P:(g + 1) * P], qkv_t[:, 0, :],
                                         start=True, stop=True).then_inc(reps, 1)
                        if g:
                            total(g - 1)
                    total(NG - 1)
                    pe.wait_ge(yev, 1)
                    for j in range(NJ):
                        last = nc.tensor.matmul(PS[7][:, j * D:(j + 1) * D], yt[:, j * P:(j + 1) * P], W("o4"), start=True, stop=True)
                    last.then_inc(dn, 1)

                @block.scalar
                def _(act):
                    for g in range(NG):
                        act.wait_ge(reps, g + 1)
                        if g >= 2:
                            act.wait_ge(hd, g - 1)
                        nc.scalar.activation(vrc[:, g % 2, :], PS[3 * (g % 2)][:, :], ACT.Copy,
                                             scale=W("coef")[:, g:g + 1]).then_inc(vd, 1)
                    act.wait_ge(summed, NG)
                    nc.scalar.copy(yt[:, :], PS[6][:, :]).then_inc(yev, 1)

                @block.vector
                def _(dve):
                    V = nc.vector
                    for g in range(NG):
                        k = 3 * (g % 2)
                        dve.wait_ge(vd, g + 1)
                        V.tensor_tensor(heb[:, g % 2, :], PS[k + 1][:, :], vrc[:, g % 2, :], ALU.mult).then_inc(hd, 1)
                        dve.wait_ge(hd, g + 1)
                        V.tensor_tensor_scan(mem[:, g % 2, :], bc(W("ret")[:, g:g + 1], [P, SEQ]), heb[:, g % 2, :], 0.0,
                                             ALU.mult, ALU.add).then_inc(sd, 1)
                        dve.wait_ge(sd, g + 1)
                        if g >= 2:
                            dve.wait_ge(summed, g - 1)
                        V.scalar_tensor_tensor(red[:, g % 2, :], mem[:, g % 2, :], W("LTM")[:, g:g + 1], PS[k + 2][:, :],
                                               ALU.add, ALU.mult).then_inc(gd, 1)
                    dve.wait_ge(dn, 1)
                    V.tensor_tensor(X[:, :, :], X[:, :, :], PS[7][:, :].rearrange(tiles, j=NJ), ALU.add)

        with Stage("moe3") as st:
            norm_tiles(st, "ln", X, XN, XT)
            comb, comb_t = st.sb("comb", [P, NJ, E3]), st.sb("comb_t", [E3, SEQ])
            gates(st, XT, W("Wg3"), E3, comb, comb_t, eps=0.0)
            experts(st, W("W1_3"), W("W3_3"), W("b1_3"), W("b3_3"), W("W2_3"), W("b2_3", E3), E3, HID // P, ACT.Silu,
                    comb, comb_t, X)
            written = st.sem("written")
            with nc.Block() as block:
                @block.sync
                def _(sp):
                    sp.dma_start(one(ys, b), X[:, :, :]).then_inc(written, 16)
                    sp.wait_ge(written, 16)
    top.close()


def constants():
    c = {"ident": np.eye(P), "minus_half": np.full((P, NJ * H), -0.5)}
    for E in (4, E1, E0):
        c[f"tri{E}"] = np.broadcast_to(np.tril(np.ones((E, E)), -1).ravel(), (P, E * E))
    sel = np.zeros((E0, E0 * INTER))
    for e in range(E0):
        sel[e, e * INTER:(e + 1) * INTER] = 1
    c["sel_e0"] = sel
    inv = (1.0 / (np.float32(10000.0) ** (np.arange(0, HD, 2, dtype=np.float32) / np.float32(HD)))).astype(np.float32)
    ang = (np.arange(SEQ, dtype=np.float32)[:, None] * inv[None]).astype(np.float32)
    for n, f in (("cos", np.cos), ("sin", np.sin)):
        c[n] = f(ang.astype(np.float64)).reshape(NJ, P, HD // 2).transpose(1, 0, 2).reshape(P, -1)
    ch = np.arange(H * HD * HD)
    h, d, e = ch // 64, ch // 8 % 8, ch % 8
    sd, se = np.zeros((P, ch.size)), np.zeros((P, ch.size))
    sd[h * 8 + d, ch] = 1
    se[h * 8 + e, ch] = 1
    c["sel_d"], c["sel_e"] = sd, se
    c["sel_sum"] = sd.T.reshape(NG, P, P).transpose(1, 0, 2).reshape(P, -1)
    b = {"ident_b": np.eye(P), "later": np.triu(np.full((P, P), -1e30), 1)}
    s = np.zeros((96, 2 * NS, P))
    for n in range(2 * NS):
        for part in range(3):
            s[32 * part + n, n] = 1
    b["sel_bc"] = s.reshape(96, -1)
    return c, b


def relative_buckets():
    rel = np.arange(1024) - (SEQ - 1)
    nb = 16
    out = (rel > 0).astype(np.int32) * nb
    rp = np.abs(rel)
    large = 8 + (np.log(np.maximum(rp, 1).astype(np.float32) / np.float32(8)) / np.float32(np.log(128 / 8)) * np.float32(8)).astype(np.int32)
    out = out + np.where(rp < 8, rp, np.minimum(large, nb - 1))
    return (np.arange(32)[:, None] == out[None]).astype(np.float32)


def kernel(**inputs):
    import ml_dtypes
    import concourse.bacc as _bacc
    from concourse.bass_utils import run_bass_kernel_spmd as _run

    g = {k: np.asarray(v) for k, v in inputs.items()}
    consts, consts_b = constants()
    cols, cols_b, lora_cols = {}, {}, {}

    def pack(items, index, rows, dtype=np.float32):
        at, parts = 0, []
        for name, a in items:
            a = np.asarray(a)
            a = a.reshape(a.shape[0], -1)
            full = np.zeros((rows, a.shape[1]), dtype)
            full[:a.shape[0]] = a
            index[name] = (at, a.shape[1])
            at += a.shape[1]
            parts.append(full)
        return np.ascontiguousarray(np.concatenate(parts, 1))

    def rows(v):
        return np.broadcast_to(v.reshape(1, -1), (P, v.size))

    def feat(v):
        return v.reshape(-1, P).T

    def down(w):
        return w.reshape(-1, P, w.shape[-1]).transpose(1, 0, 2)

    a, f, q, l, m, n_, t, k = ("L0_attn_", "L0_ffn_", "L1_attn_", "L1_ffn_", "L2_attn_", "L2_ffn_", "L3_attn_", "L3_ffn_")
    both = ("_f", "_b")
    items = list(consts.items())
    items += [
        ("norm_w", g[a + "norm_w"][:, None]), ("in_T", g[a + "in_proj_w"].T), ("out_T", down(g[a + "out_proj_w"].T)),
        ("conv_w", np.stack([g[a + "conv_w" + s].reshape(ND, P, KC) for s in both]).transpose(2, 0, 1, 3)),
        ("conv_b", np.stack([g[a + "conv_b" + s].reshape(ND, P) for s in both]).transpose(2, 0, 1)),
        ("xp_bc", np.stack([np.tile(g[a + "xproj_w" + s][DTR:].T.reshape(ND, P, 2 * NS), (1, 1, 3)) for s in both]).transpose(2, 0, 1, 3)),
        ("xp_dt", np.stack([g[a + "xproj_w" + s][:DTR].T.reshape(ND, P, DTR) for s in both]).transpose(2, 0, 1, 3)),
        ("dt_T", np.concatenate([np.concatenate([g[a + "dtproj_w" + s].T, g[a + "dtproj_b" + s][None]], 0) for s in both], 1)),
        ("A", np.stack([g[a + "A_log" + s].reshape(ND, P, NS) for s in both]).transpose(2, 0, 1, 3)),
        ("D", np.stack([g[a + "D" + s].reshape(ND, P) for s in both]).transpose(2, 0, 1)),
        ("gate_T", g[f + "gate_w"].T), ("gate_b", rows(g[f + "gate_b"])),
        ("We1", np.concatenate([g[f + "We1"].transpose(1, 0, 2).reshape(D, -1), g[f + "ws1"]], 1)),
        ("We3", np.concatenate([g[f + "We3"].transpose(1, 0, 2).reshape(D, -1), g[f + "ws3"]], 1)),
        ("We2", down(np.concatenate([g[f + "We2"].reshape(-1, D), g[f + "ws2"]], 0))),
        ("be1", feat(np.concatenate([g[f + "be1"].ravel(), g[f + "bs1"]]))),
        ("be3", feat(np.concatenate([g[f + "be3"].ravel(), g[f + "bs3"]]))),
        ("be2", g[f + "be2"]), ("bs2", rows(g[f + "bs2"])),
        ("Wq", g[q + "Wq"]), ("Wk", g[q + "Wk"]), ("Wv", g[q + "Wv"]), ("Wo", down(g[q + "Wo"])),
        ("W_T", g[l + "W"].T), ("R_T", g[l + "R"].T), ("A1_T", g[l + "A"].reshape(-1, D).T),
        ("B1", g[l + "B"].transpose(0, 2, 1).reshape(-1, D)), ("b_1", rows(g[l + "b"])),
        ("qkv2", g[m + "W_qkv"].T), ("o2", g[m + "W_o"].T),
        ("qkv3", np.concatenate([g[n_ + "Wq"], g[n_ + "Wk"], g[n_ + "Wv"]], 1)),
        ("bqkv3", rows(np.concatenate([g[n_ + "bq"], g[n_ + "bk"], g[n_ + "bv"]]))),
        ("o3", g[n_ + "Wo"]), ("bo3", rows(g[n_ + "bo"])), ("Wg2", g[n_ + "Wg"]), ("bg2", rows(g[n_ + "bg"])),
        ("W1_2", g[n_ + "W1"].transpose(1, 0, 2)), ("b1_2", feat(g[n_ + "b1"].ravel())),
        ("W2_2", down(g[n_ + "W2"].reshape(-1, D))), ("b2_2", g[n_ + "b2"]),
        ("g1", rows(g[n_ + "g1"])), ("be1_2", rows(g[n_ + "be1"])), ("g2", rows(g[n_ + "g2"])), ("be2_2", rows(g[n_ + "be2"])),
        ("qkv4", g[t + "W_qkv"].T), ("o4", g[t + "W_o"].T), ("LTM", feat(g[t + "W_LTM"].ravel())),
        ("Wg3", g[k + "Wg"].T), ("W1_3", g[k + "W1"].transpose(2, 0, 1)), ("W3_3", g[k + "W3"].transpose(2, 0, 1)),
        ("W2_3", down(g[k + "W2"].transpose(0, 2, 1).reshape(-1, D))),
        ("b1_3", feat(g[k + "b1"].ravel())), ("b3_3", feat(g[k + "b3"].ravel())), ("b2_3", g[k + "b2"]),
    ]
    for name, key in (("Vgs", "V_gs"), ("VT0", "V_T0"), ("btau", "beta_tau"), ("bgm", "beta_gm"), ("Cch", "C_ch"), ("gam", "gamma")):
        items.append((name, feat(np.repeat(g[t + key], HD * HD))))
    items += [("ppd", rows(g[t + "alpha_ppd"])), ("ICt", rows(g[t + "IC_threshold"])),
              ("ret", np.zeros((P, NG))), ("coef", np.zeros((P, NG)))]
    wf = pack(items, cols, P)
    wb = pack(list(consts_b.items()), cols_b, P, ml_dtypes.bfloat16)
    lora = pack([("A1", g[k + "A1"].transpose(1, 0, 2)), ("B1T", g[k + "B1"].transpose(2, 0, 1)),
                 ("A3", g[k + "A3"].transpose(1, 0, 2)), ("B3T", g[k + "B3"].transpose(2, 0, 1)),
                 ("A2", g[k + "A2"].transpose(1, 0, 2)), ("B2T", g[k + "B2"].transpose(2, 0, 1))], lora_cols, R1)
    arrays = {"in_x": np.ascontiguousarray(g[a + "x"]), "in_wf": wf, "in_wb": wb, "in_lora": lora,
              "in_onehot": relative_buckets(), "in_table": np.ascontiguousarray(g[q + "rel_bias_table"])}
    nc = _bacc.Bacc("TRN2", target_bir_lowering=False, num_devices=1)
    d = {n: nc.dram_tensor(n, v.shape, mybir.dt.from_np(v.dtype), kind="ExternalInput").ap() for n, v in arrays.items()}
    out = nc.dram_tensor("out_0", arrays["in_x"].shape, F32, kind="ExternalOutput").ap()
    bass_mk_seq(nc, d["in_x"], cols, cols_b, d["in_wf"], d["in_wb"], d["in_lora"], lora_cols, d["in_onehot"], d["in_table"], out)
    r = _run(nc, [arrays], core_ids=[0])
    return r.results[0]["out_0"]
```

```python
from contextlib import ExitStack

import numpy as np

import concourse.bass as bass
from concourse import mybir

ALU = mybir.AluOpType
ACT = mybir.ActivationFunctionType
F32 = mybir.dt.float32
BF16 = mybir.dt.bfloat16
AX = mybir.AxisListType

P = 128
D = 128
SEQ = 512
NJ = SEQ // P
BIG = 3.0e38
EPS = 1e-5

DI = 256
ND = DI // P
NS = 16
DTR = 8
KC = 4
PAD = KC - 1

H = 16
DK = 64
TW = SEQ + P * (NJ - 1)
HD = 8
HS = 64
SPLITS = 6
SK = SPLITS * HD
SM = SK + 3
VW = 32
GH = 4
E0, INTER = 16, 64
E1, R1 = 8, 16
E2, FF = 8, 512
E3, HID = 8, 256
NG = H * HD * HD // P


class Chain:

    def __init__(self, eng, sem):
        self.eng, self.sem, self.n = eng, sem, 0

    def __call__(self, ins):
        self.n += 1
        ins.then_inc(self.sem, 1)
        self.eng.wait_ge(self.sem, self.n)


def bass_mk_seq(nc, x, cols_f, cols_b, wf, wb, lora, lora_cols, onehot, table, out):
    top = ExitStack()

    def sbt(c, name, shape, dt=F32):
        return c.enter_context(nc.sbuf_tensor(name, shape, dt))

    WF = sbt(top, "WF", [P, wf.shape[1]])
    WB = sbt(top, "WB", [P, wb.shape[1]], BF16)

    def W(name, p=P):
        o, n = cols_f[name]
        return WF[0:p, o:o + n]

    def WBF(name, p=P):
        o, n = cols_b[name]
        return WB[0:p, o:o + n]

    X = sbt(top, "X", [P, NJ, D])
    XN = sbt(top, "XN", [P, NJ, D])
    XT = sbt(top, "XT", [P, SEQ])
    stats = sbt(top, "stats", [P, NJ, 6])
    mv = sbt(top, "mv", [P, NJ, 2])
    rstd = sbt(top, "rstd", [P, NJ])
    BANKS = top.enter_context(nc.psum_tensor("BANKS", [P, 8, 512], F32))
    PS = [BANKS[:, i, :] for i in range(8)]
    ident = W("ident")
    ident_b = WBF("ident_b")
    bias_dram = nc.dram_tensor("bias_line", [H, 1024], F32, kind="Internal").ap()

    tiles = "p (j d) -> p j d"

    class Stage:

        def __init__(self, name):
            self.name, self.ctx, self.sems = name, ExitStack(), {}

        def __enter__(self):
            return self

        def sb(self, name, shape, dt=F32, scope=None):
            return sbt(scope or self.ctx, f"{self.name}_{name}", shape, dt)

        def sem(self, name):
            s = self.ctx.enter_context(nc.semaphore(f"{self.name}_{name}"))
            self.sems[name] = s
            return s

        def __exit__(self, failed, *_):
            if failed:
                return
            sems = list(self.sems.values())
            with nc.Block() as block:
                @block.sync
                def _(sp):
                    for s in sems:
                        sp.sem_clear(s)
            self.ctx.close()

    def bc(ap, shape):
        return ap.to_broadcast(shape)

    def norm_tiles(st, tag, src, dst, dst_t, rms=False, gain_t=None, gain=None, shift=None, extra=None,
                   transposed=True):
        ch, normed = st.sem(f"{tag}_chain"), st.sem(f"{tag}_normed")
        turned, evac = st.sem(f"{tag}_turned"), st.sem(f"{tag}_evac")
        shifted, rooted = st.sem(f"{tag}_shifted"), st.sem(f"{tag}_rooted")
        sq = XT if rms else None
        with nc.Block() as block:
            @block.gpsimd
            def _(pool):
                pool.wait_ge(shifted, 1)
                nc.gpsimd.tensor_tensor(rstd[:, :], rstd[:, :], W("minus_half")[:, 0:NJ], ALU.pow).then_inc(rooted, 1)

            @block.vector
            def _(dve):
                link = Chain(dve, ch)
                if rms:
                    for j in range(NJ):
                        last = nc.vector.tensor_tensor_reduce(sq[:, j * D:(j + 1) * D], src[:, j, :], src[:, j, :], 1.0 / D, 0.0,
                                                              ALU.mult, ALU.add, rstd[:, j:j + 1])
                    link(last)
                    nc.vector.tensor_scalar(rstd[:, :], rstd[:, :], EPS, None, ALU.add).then_inc(shifted, 1)
                else:
                    for j in range(NJ):
                        last = nc.vector.bn_stats(stats[:, j, :], src[:, j, :])
                    link(last)
                    for j in range(NJ):
                        last = nc.vector.bn_aggr(mv[:, j, :], stats[:, j, :])
                    link(last)
                    nc.vector.tensor_scalar(rstd[:, :], mv[:, :, 1], EPS, None, ALU.add).then_inc(shifted, 1)
                dve.wait_ge(rooted, 1)
                for j in range(NJ):
                    if rms:
                        ins = nc.vector.tensor_scalar(dst[:, j, :], src[:, j, :], rstd[:, j:j + 1], None, ALU.mult)
                    else:
                        ins = nc.vector.tensor_scalar(dst[:, j, :], src[:, j, :], mv[:, j, 0:1], rstd[:, j:j + 1],
                                                      ALU.subtract, ALU.mult)
                    if gain is not None:
                        link(ins)
                        link(nc.vector.tensor_tensor(dst[:, j, :], dst[:, j, :], gain, ALU.mult))
                        ins = nc.vector.tensor_tensor(dst[:, j, :], dst[:, j, :], shift, ALU.add)
                    ins.then_inc(normed, 1)
                if extra is not None:
                    dve.wait_ge(normed, NJ)
                    extra(link)

            if transposed:
                @block.tensor
                def _(pe):
                    for j in range(NJ):
                        pe.wait_ge(normed, j + 1)
                        nc.tensor.transpose(PS[7][:, j * P:(j + 1) * P], dst[:, j, :], ident).then_inc(turned, 1)

                @block.scalar
                def _(act):
                    act.wait_ge(turned, NJ)
                    if gain_t is not None:
                        nc.scalar.activation(dst_t[:, :], PS[7][:, :], ACT.Copy, scale=gain_t).then_inc(evac, 1)
                    else:
                        nc.scalar.copy(dst_t[:, :], PS[7][:, :]).then_inc(evac, 1)

    def top2_mask(link, s, mask, E, big1, big2, rank):
        n = NJ * E * E
        a = big1[:, 0:n].rearrange("p (j g o) -> p j g o", j=NJ, g=E)
        b = big2[:, 0:n].rearrange("p (j g o) -> p j g o", j=NJ, g=E)
        other = bc(s.unsqueeze(2), [P, NJ, E, E])
        own = bc(s.unsqueeze(3), [P, NJ, E, E])
        tri = WBF(f"tri{E}").rearrange("p (g o) -> p g o", g=E)
        nc.vector.tensor_tensor(a, other, own, ALU.is_gt)
        link(nc.vector.tensor_tensor(b, other, own, ALU.is_equal))
        link(nc.vector.tensor_tensor(b, b, bc(tri.unsqueeze(1), [P, NJ, E, E]), ALU.mult))
        link(nc.vector.tensor_tensor(a, a, b, ALU.add))
        link(nc.vector.tensor_reduce(rank, a, AX.X, ALU.add))
        link(nc.vector.tensor_scalar(mask, rank, 2.0, None, ALU.is_lt))

    def gates(st, src_t, w_gate, E, comb, comb_t, bias=None, grouped_bias=None, eps=None):
        lg, ex, mask = st.sb("lg", [P, NJ, E]), st.sb("ex", [P, NJ, E]), st.sb("mask", [P, NJ, E])
        m1, t4 = st.sb("m1", [P, NJ]), st.sb("t4", [P, 6, NJ, 4])
        big1, big2 = st.sb("cmp1", [P, NJ * E * E]), st.sb("cmp2", [P, NJ * E * E])
        rank = st.sb("rank", [P, NJ, E])
        ch, logits, shifted = st.sem("gchain"), st.sem("logits"), st.sem("shifted")
        exped, combed, turned, evac = st.sem("exped"), st.sem("combed"), st.sem("gturned"), st.sem("gevac")
        with nc.Block() as block:
            @block.tensor
            def _(pe):
                for j in range(NJ):
                    last = nc.tensor.matmul(PS[0][:, j * E:(j + 1) * E], src_t[:, j * P:(j + 1) * P], w_gate,
                                            start=True, stop=True)
                last.then_inc(logits, 1)
                pe.wait_ge(combed, 1)
                for j in range(NJ):
                    last = nc.tensor.transpose(PS[1][0:E, j * P:(j + 1) * P], comb[:, j, :], ident)
                last.then_inc(turned, 1)

            @block.scalar
            def _(act):
                act.wait_ge(shifted, 1)
                nc.scalar.activation(ex[:, :, :], lg[:, :, :], ACT.Exp).then_inc(exped, 1)
                act.wait_ge(turned, 1)
                nc.scalar.copy(comb_t[0:E, :], PS[1][0:E, :]).then_inc(evac, 1)

            @block.vector
            def _(dve):
                link = Chain(dve, ch)
                V = nc.vector
                raw = PS[0][:, 0:NJ * E].rearrange("p (j e) -> p j e", e=E)
                dve.wait_ge(logits, 1)
                if bias is not None:
                    link(V.tensor_tensor(lg[:, :, :], raw, bc(bias.unsqueeze(1), [P, NJ, E]), ALU.add))
                    raw = lg[:, :, :]
                link(V.tensor_reduce(m1[:, :], raw, AX.X, ALU.max))
                V.tensor_tensor(lg[:, :, :], raw, bc(m1[:, :].unsqueeze(2), [P, NJ, E]),
                                ALU.subtract).then_inc(shifted, 1)
                dve.wait_ge(exped, 1)
                link(V.tensor_reduce(m1[:, :], ex[:, :, :], AX.X, ALU.add))
                link(V.reciprocal(m1[:, :], m1[:, :]))
                link(V.tensor_tensor(ex[:, :, :], ex[:, :, :], bc(m1[:, :].unsqueeze(2), [P, NJ, E]), ALU.mult))
                score = ex
                if grouped_bias is not None:
                    link(V.tensor_tensor(lg[:, :, :], ex[:, :, :], bc(grouped_bias.unsqueeze(1), [P, NJ, E]), ALU.add))
                    q = lg[:, :, :].rearrange("p j (g k) -> p j g k", k=4)
                    t = [t4[:, i, :, :] for i in range(6)]
                    V.tensor_tensor(t[0], q[:, :, :, 0], q[:, :, :, 1], ALU.max)
                    V.tensor_tensor(t[1], q[:, :, :, 0], q[:, :, :, 1], ALU.min)
                    V.tensor_tensor(t[2], q[:, :, :, 2], q[:, :, :, 3], ALU.max)
                    link(V.tensor_tensor(t[3], q[:, :, :, 2], q[:, :, :, 3], ALU.min))
                    V.tensor_tensor(t[4], t[0], t[2], ALU.max)
                    V.tensor_tensor(t[5], t[0], t[2], ALU.min)
                    link(V.tensor_tensor(t[1], t[1], t[3], ALU.max))
                    link(V.tensor_tensor(t[5], t[5], t[1], ALU.max))
                    link(V.tensor_tensor(t[4], t[4], t[5], ALU.add))
                    top2_mask(link, t[4], t[0], 4, big1, big2, rank[:, :, 0:4])
                    link(V.tensor_scalar(t[1], t[0], 1.0, BIG, ALU.subtract, ALU.mult))
                    link(V.tensor_tensor(q, q, bc(t[1].unsqueeze(3), [P, NJ, 4, 4]), ALU.add))
                    score = lg
                top2_mask(link, score[:, :, :], mask[:, :, :], E, big1, big2, rank[:, :, :])
                if eps is None:
                    V.tensor_tensor(comb[:, :, :], ex[:, :, :], mask[:, :, :], ALU.mult).then_inc(combed, 1)
                else:
                    link(V.tensor_tensor(ex[:, :, :], ex[:, :, :], mask[:, :, :], ALU.mult))
                    link(V.tensor_reduce(m1[:, :], ex[:, :, :], AX.X, ALU.add))
                    if eps:
                        link(V.tensor_scalar(m1[:, :], m1[:, :], eps, None, ALU.add))
                    link(V.reciprocal(m1[:, :], m1[:, :]))
                    V.tensor_tensor(comb[:, :, :], ex[:, :, :], bc(m1[:, :].unsqueeze(2), [P, NJ, E]),
                                    ALU.mult).then_inc(combed, 1)

    def attention(st, scores, vals, dv, O, causal=False, bias_of=None, evac_act=lambda u: u % 2,
                  loads=None, pe_ahead=None, act_ahead=None):
        U = H * NJ
        NS_, NP_, NT_ = 3, 3, 2
        short = ExitStack()
        prob = st.sb("prob", [P, NP_, SEQ], scope=short)
        probt = st.sb("probt", [P, NT_, SEQ], scope=short)
        biased = st.sb("biased", [P, NS_, SEQ], scope=short) if bias_of else None
        nmax = st.sb("nmax", [P, U], scope=short)
        rden = st.sb("rden", [P, 2, NJ], scope=short)
        scored, maxed, exped = st.sem("scored"), st.sem("maxed"), st.sem("exped_p")
        turned, evac_d, evac_a = st.sem("turned_p"), st.sem("evac_d"), st.sem("evac_a")
        weighed, normed, ch = st.sem("weighed"), st.sem("head_normed"), st.sem("achain")
        n_act = [0]
        n_dve = [0]
        for u in range(U):
            n_act.append(n_act[-1] + bool(evac_act(u)))
            n_dve.append(n_dve[-1] + (not evac_act(u)))

        def keys(u):
            return P * (u % NJ + 1) if causal else SEQ

        def evacuated(eng, u):
            if evac_act(u):
                eng.wait_ge(evac_a, n_act[u + 1])
            else:
                eng.wait_ge(evac_d, n_dve[u + 1])

        def out_ps(h):
            return PS[5 + h % 2][:, 0:NJ * (dv + 1)].rearrange("p (j v) -> p j v", j=NJ)

        with nc.Block() as block:
            if loads is not None:
                loads(block)

            @block.tensor
            def _(pe):
                for s in range(U + 3):
                    if pe_ahead is not None and s < U:
                        pe_ahead(pe, s)
                    if s < U:
                        if s >= NS_:
                            pe.wait_ge(maxed if bias_of else exped, s - NS_ + 1)
                        scores(pe, s, PS[s % NS_][:, 0:keys(s)]).then_inc(scored, 1)
                    u = s - 2
                    if 0 <= u < U:
                        pe.wait_ge(exped, u + 1)
                        if u >= NT_:
                            evacuated(pe, u - NT_)
                        for kt in range(keys(u) // P):
                            last = nc.tensor.transpose(PS[3 + u % NT_][:, kt * P:(kt + 1) * P],
                                                       prob[:, u % NP_, kt * P:(kt + 1) * P], ident)
                        last.then_inc(turned, 1)
                    u = s - 3
                    if 0 <= u < U:
                        h, j = u // NJ, u % NJ
                        evacuated(pe, u)
                        if j == 0 and h >= 2:
                            pe.wait_ge(normed, h - 1)
                        n = keys(u) // P
                        for kt in range(n):
                            last = nc.tensor.matmul(out_ps(h)[:, j, :], probt[:, u % NT_, kt * P:(kt + 1) * P],
                                                    vals[:, kt, h, :], start=(kt == 0), stop=(kt == n - 1))
                        last.then_inc(weighed, 1)

            def evac(eng, copy, sem, u):
                eng.wait_ge(turned, u + 1)
                if u >= NT_:
                    eng.wait_ge(weighed, u - NT_ + 1)
                copy(probt[:, u % NT_, 0:keys(u)], PS[3 + u % NT_][:, 0:keys(u)]).then_inc(sem, 1)

            @block.vector
            def _(dve):
                link = Chain(dve, ch)
                for s in range(U + 5):
                    if s < U:
                        dve.wait_ge(scored, s + 1)
                        if bias_of:
                            if s >= NS_:
                                dve.wait_ge(exped, s - NS_ + 1)
                            nc.vector.tensor_tensor_reduce(
                                biased[:, s % NS_, :], PS[s % NS_][:, :], bias_of(dve, s), -1.0, BIG,
                                ALU.add, ALU.min, nmax[:, s:s + 1]).then_inc(maxed, 1)
                        else:
                            nc.vector.tensor_reduce(nmax[:, s:s + 1], PS[s % NS_][:, 0:keys(s)], AX.X, ALU.max,
                                                    negate=True).then_inc(maxed, 1)
                    u = s - 2
                    if 0 <= u < U and not evac_act(u):
                        evac(dve, nc.vector.tensor_copy, evac_d, u)
                    u = s - 4
                    if u >= 0 and u % NJ == NJ - 1:
                        h = u // NJ
                        dve.wait_ge(weighed, u + 1)
                        r = rden[:, h % 2, :]
                        link(nc.vector.reciprocal(r, out_ps(h)[:, :, dv]))
                        nc.vector.tensor_tensor(O[:, :, h * dv:(h + 1) * dv], out_ps(h)[:, :, 0:dv],
                                                bc(r.unsqueeze(2), [P, NJ, dv]), ALU.mult).then_inc(normed, 1)

            @block.scalar
            def _(act):
                for s in range(U + 3):
                    if act_ahead is not None and s < U:
                        act_ahead(act, s)
                    if s < U:
                        act.wait_ge(maxed, s + 1)
                        if s >= NP_:
                            act.wait_ge(turned, s - NP_ + 1)
                        src = biased[:, s % NS_, :] if bias_of else PS[s % NS_][:, 0:keys(s)]
                        nc.scalar.activation(prob[:, s % NP_, 0:keys(s)], src, ACT.Exp, bias=nmax[:, s:s + 1],
                                             scale=-1.0 if bias_of else 1.0).then_inc(exped, 1)
                    u = s - 2
                    if 0 <= u < U and evac_act(u):
                        evac(act, nc.scalar.copy, evac_a, u)
        short.close()

    def head8_attention(st, parts_q, turned, vals, causal, O):
        NGR = H // GH
        PER = 2 * NJ
        LAG = PER + 2
        RING = 3
        PR = 4
        held = ExitStack()
        qm = st.sb("qm", [P, 2, 2, SEQ], BF16, scope=held)
        prob = st.sb("prob", [P, PR, 2, SEQ], scope=held)
        nmax = st.sb("nmax", [P, NJ, H], scope=held)
        ot = st.sb("o_t", [P, 2, SEQ], scope=held)
        rden = st.sb("rden", [P, NJ, GH], scope=held)
        s_done, t_done, maxed, exped, split = (st.sem(n) for n in ("s_done", "t_done", "maxed", "exped8", "split"))
        q_turned, q_moved, weighed, o_moved, o_turned, o_normed, ch = (
            st.sem(n) for n in ("q_turned", "q_moved", "weighed", "o_moved", "o_turned", "o_normed", "chain8"))
        N = NGR * PER
        order = []
        for s in range(N + LAG):
            order += [("S", s)] * (s < N) + [("T", s - LAG)] * (0 <= s - LAG)
        slot = {item: n % RING for n, item in enumerate(order)}

        def bank_free(pe, item):
            n = order.index(item)
            if n >= RING:
                kind, i = order[n - RING]
                pe.wait_ge(maxed if kind == "S" else exped, i + 1)

        def span(kind, i):
            tile = i % PER // 2
            if not causal:
                return 0, SEQ
            return (0, P * (tile + 1)) if kind == "S" else (P * tile, SEQ)

        def banks(kind, i):
            lo, hi = span(kind, i)
            k = 2 * slot[kind, i]
            return BANKS[:, k:k + 2, lo:hi]

        with nc.Block() as block:
            @block.tensor
            def _(pe):
                def score(kind, i, left, right, later, sem):
                    bank_free(pe, (kind, i))
                    tile = i % PER // 2
                    lo, hi = span(kind, i)
                    out = banks(kind, i)
                    for h in range(2):
                        a = left[HS * h:HS * (h + 1), P * tile:P * (tile + 1)]
                        last = nc.tensor.matmul(out[:, h, :], a, right[HS * h:HS * (h + 1), lo:hi],
                                                start=True, stop=not causal)
                    if causal:
                        for h in range(2):
                            o = P * tile - lo
                            last = nc.tensor.matmul(out[:, h, o:o + P], ident_b, later, start=False, stop=True)
                    last.then_inc(sem, 1)

                for s in range(N + LAG + 6):
                    if s < N:
                        r = 2 * (s // PER) + s % 2
                        score("S", s, turned[0][:, r, :], turned[1][:, r, :], WBF("later"), s_done)
                    if s % PER == 1 and 1 <= s // PER <= NGR:
                        g = s // PER - 1
                        pe.wait_ge(split, g + 1)
                        if g == 1:
                            pe.wait_ge(q_moved, 1)
                        if g >= 2:
                            pe.wait_ge(o_normed, g - 1)
                        view = parts_q[:, :, :].rearrange("p (j r) s -> p j (r s)", j=NJ)
                        bank = PS[7].bitcast(BF16)
                        for pair in range(2):
                            for j in range(NJ):
                                last = nc.tensor.transpose(bank[:, (pair * NJ + j) * P:(pair * NJ + j + 1) * P],
                                                           view[:, j, (2 * g + pair) * P:(2 * g + pair + 1) * P], ident_b)
                        last.then_inc(q_turned, 1)
                    i = s - LAG
                    if 0 <= i < N:
                        g = i // PER
                        if i % PER == 0:
                            pe.wait_ge(q_moved, g + 1)
                        r = 2 * g + i % 2
                        score("T", i, turned[1][:, r, :], qm[:, g % 2, i % 2, :], WBF("later_T"), t_done)
                    i = s - LAG - 2
                    if 0 <= i < N and i % 2:
                        g, kt = i // PER, i % PER // 2
                        pe.wait_ge(exped, i + 1)
                        if kt == 0 and g:
                            pe.wait_ge(o_moved, g)
                        lo = P * kt if causal else 0
                        for h in range(GH):
                            last = nc.tensor.matmul(PS[6][VW * h:VW * (h + 1), lo:], vals[:, kt, GH * g + h, :],
                                                    prob[:, (i - 1 + h // 2) % PR, h % 2, lo:],
                                                    start=(kt == 0), stop=(kt == NJ - 1))
                        last.then_inc(weighed, 1)
                    i = s - LAG - 4
                    if 0 <= i < N and i % PER == PER - 1:
                        g = i // PER
                        pe.wait_ge(o_moved, g + 1)
                        pe.wait_ge(q_moved, min(g + 2, NGR))
                        if g == NGR - 1:
                            pe.wait_ge(o_normed, g)
                        for j in range(NJ):
                            last = nc.tensor.transpose(PS[7][:, j * P:(j + 1) * P], ot[:, g % 2, j * P:(j + 1) * P], ident)
                        last.then_inc(o_turned, 1)

            @block.scalar
            def _(act):
                for s in range(N + LAG + 6):
                    if s % PER == 1 and 1 <= s // PER <= NGR:
                        g = s // PER - 1
                        act.wait_ge(q_turned, g + 1)
                        nc.scalar.copy(qm[:, g % 2, :, :].rearrange("p a t -> p (a t)"), PS[7].bitcast(BF16)).then_inc(q_moved, 1)
                    i = s - LAG - 3
                    if 0 <= i < N and i % PER == PER - 1:
                        g = i // PER
                        act.wait_ge(weighed, NJ * (g + 1))
                        if g >= 2:
                            act.wait_ge(o_turned, g - 1)
                        nc.scalar.copy(ot[:, g % 2, :], PS[6]).then_inc(o_moved, 1)
                    i = s - LAG
                    if 0 <= i < N:
                        act.wait_ge(t_done, i + 1)
                        if i >= PR:
                            act.wait_ge(weighed, (i - PR) // 2 + 1)
                        lo, hi = span("T", i)
                        nc.scalar.activation(prob[:, i % PR, :, lo:hi], banks("T", i), ACT.Exp).then_inc(exped, 1)

            @block.vector
            def _(dve):
                V = nc.vector
                link = Chain(dve, ch)
                part = parts_q[:, :, :].rearrange("p (j h) s -> p j h s", j=NJ)
                for s in range(N + LAG + 7):
                    if s < N:
                        g, j = s // PER, s % PER // 2
                        h = GH * g + 2 * (s % 2)
                        dve.wait_ge(s_done, s + 1)
                        V.tensor_reduce(nmax[:, j, h:h + 2], banks("S", s), AX.X, ALU.max, negate=True).then_inc(maxed, 1)
                        if s % PER == PER - 1:
                            dve.wait_ge(maxed, s + 1)
                            m = nmax[:, :, GH * g:GH * (g + 1)]
                            for lvl in range(3):
                                p = part[:, :, GH * g:GH * (g + 1), SK + lvl]
                                ins = V.tensor_copy(p, m)
                                if lvl < 2:
                                    link(ins)
                                    link(V.tensor_tensor(m, m, p, ALU.subtract))
                            ins.then_inc(split, 1)
                    i = s - LAG - 5
                    if 0 <= i < N and i % PER == PER - 1:
                        g = i // PER
                        dve.wait_ge(o_turned, g + 1)
                        got = PS[7].rearrange("p (j h v) -> p j h v", j=NJ, v=VW)
                        link(V.reciprocal(rden[:, :, :], got[:, :, :, HD]))
                        out = O[:, :, GH * g * HD:GH * (g + 1) * HD].rearrange("p j (h v) -> p j h v", v=HD)
                        V.tensor_tensor(out, got[:, :, :, 0:HD], bc(rden[:, :, :].unsqueeze(3), [P, NJ, GH, HD]),
                                        ALU.mult).then_inc(o_normed, 1)
        held.close()

    with Stage("init") as st:
        ld, ld_b, ld_x, ch = st.sem("ld"), st.sem("ld_b"), st.sem("ld_x"), st.sem("ch")
        fold, folded = st.sem("fold"), st.sem("folded")
        ach, line, lined, stored = st.sem("ach"), st.sem("line"), st.sem("lined"), st.sem("stored")
        LO = st.sb("LO", [R1, lora.shape[1]])
        OH = st.sb("OH", [32, 1024])
        TB = st.sb("TB", [32, H])
        LN = st.sb("LN", [H, 1024])

        def lo(name):
            o, n = lora_cols[name]
            return LO[:, o:o + n]

        with nc.Block() as block:
            @block.sync
            def _(sp):
                n = wf.shape[1]
                step = -(-n // 8)
                for c in range(0, n, step):
                    e = min(n, c + step)
                    sp.dma_start(WF[:, c:e], wf[:, c:e]).then_inc(ld, 16)
                sp.dma_start(WB[:, :], wb).then_inc(ld_b, 16)
                sp.dma_start(LO[:, :], lora).then_inc(ld_x, 16)
                sp.dma_start(OH[:, :], onehot).then_inc(ld_x, 16)
                sp.dma_start(TB[:, :], table).then_inc(ld_x, 16)
                sp.wait_ge(ld, 128)
                sp.wait_ge(ld_b, 16)
                sp.wait_ge(lined, 2)
                sp.dma_start(bias_dram, LN[:, :]).then_inc(stored, 16)
                sp.wait_ge(stored, 16)

            def jobs():
                for w, a, b in (("W1_3", "A1", "B1T"), ("W3_3", "A3", "B3T")):
                    for e in range(E3):
                        yield (lo(a)[:, e * D:(e + 1) * D], lo(b)[:, e * HID:(e + 1) * HID],
                               W(w)[:, e * HID:(e + 1) * HID])
                for e in range(E3):
                    for t in range(HID // P):
                        yield (lo("A2")[:, e * HID + t * P:e * HID + (t + 1) * P], lo("B2T")[:, e * D:(e + 1) * D],
                               W("W2_3")[:, (2 * e + t) * D:(2 * e + t + 1) * D])

            @block.tensor
            def _(pe):
                pe.wait_ge(ld_x, 48)
                for i in range(2):
                    nc.tensor.matmul(PS[6 + i][0:H, :], TB[:, :], OH[:, i * 512:(i + 1) * 512],
                                     start=True, stop=True).then_inc(line, 1)
                for i, (a, b, w) in enumerate(jobs()):
                    if i >= 4:
                        pe.wait_ge(folded, i - 3)
                    nc.tensor.matmul(PS[i % 4][:, 0:w.shape[1]], a, b, start=True, stop=True).then_inc(fold, 1)

            @block.vector
            def _(dve):
                link = Chain(dve, ch)
                V = nc.vector
                for i in range(2):
                    dve.wait_ge(line, i + 1)
                    V.tensor_copy(LN[:, i * 512:(i + 1) * 512], PS[6 + i][0:H, :]).then_inc(lined, 1)
                dve.wait_ge(ld, 128)
                for i, (a, b, w) in enumerate(jobs()):
                    dve.wait_ge(fold, i + 1)
                    V.tensor_tensor(w, w, PS[i % 4][:, 0:w.shape[1]], ALU.add).then_inc(folded, 1)
                dve.wait_ge(ach, 1)
                link(V.tensor_scalar(W("A"), W("A"), -1.0, None, ALU.mult))

            @block.scalar
            def _(act):
                act.wait_ge(ld, 128)
                nc.scalar.activation(W("A"), W("A"), ACT.Exp).then_inc(ach, 1)

        T = {n: st.sb(f"m_{n}", [P, NG]) for n in ("v", "a", "e", "l", "sp", "g", "t", "c", "u")}
        dv, da = st.sem("dv"), st.sem("da")
        with nc.Block() as block:
            @block.vector
            def _(dve):
                V = nc.vector
                n = [0]

                def link(ins):
                    ins.then_inc(dv, 1)
                    n[0] += 1
                    dve.wait_ge(dv, n[0])

                t = {k: v[:, :] for k, v in T.items()}
                link(V.tensor_tensor(t["v"], W("Vgs"), W("VT0"), ALU.subtract))
                link(V.tensor_tensor(t["v"], t["v"], W("LTM"), ALU.add))
                link(V.scalar_tensor_tensor(t["a"], t["v"], -1.0, t["v"], ALU.mult, ALU.max))
                dve.wait_ge(da, 2)
                link(V.tensor_scalar(t["u"], t["e"], 1.0, -1.0, ALU.add, ALU.add))
                link(V.tensor_tensor(t["l"], t["l"], t["u"], ALU.subtract))
                link(V.tensor_tensor(t["l"], t["l"], t["e"], ALU.add))
                link(V.tensor_scalar(t["u"], t["v"], 0.0, None, ALU.max))
                link(V.tensor_tensor(t["sp"], t["l"], t["u"], ALU.add))
                link(V.tensor_tensor(t["g"], t["sp"], W("btau"), ALU.mult))
                link(V.reciprocal(t["c"], W("Cch")))
                link(V.tensor_tensor(t["c"], t["c"], t["g"], ALU.mult))
                link(V.tensor_scalar(t["t"], t["g"], W("ICt"), W("ppd"), ALU.subtract, ALU.mult))
                dve.wait_ge(da, 5)
                link(V.tensor_scalar(t["u"], t["u"], 1.0, None, ALU.add))
                link(V.reciprocal(t["u"], t["u"]))
                link(V.tensor_tensor(t["u"], t["u"], t["sp"], ALU.mult))
                link(V.tensor_tensor(t["u"], t["u"], W("bgm"), ALU.mult))
                link(V.tensor_tensor(t["u"], t["u"], t["t"], ALU.mult))
                link(V.tensor_tensor(W("coef"), t["u"], W("gam"), ALU.mult))

            @block.scalar
            def _(act):
                t = {k: v[:, :] for k, v in T.items()}
                act.wait_ge(dv, 3)
                nc.scalar.activation(t["e"], t["a"], ACT.Exp, scale=-1.0).then_inc(da, 1)
                act.wait_ge(da, 1)
                nc.scalar.activation(t["l"], t["e"], ACT.Ln, bias=1.0).then_inc(da, 1)
                act.wait_ge(dv, 12)
                nc.scalar.activation(t["u"], t["v"], ACT.Exp, scale=-1.0).then_inc(da, 1)
                nc.scalar.activation(W("ret"), t["c"], ACT.Exp, scale=-1.0).then_inc(da, 1)
                nc.scalar.activation(t["t"], t["t"], ACT.Tanh).then_inc(da, 1)

    xs = x.rearrange("b (j p) d -> b p j d", p=P)
    ys = out.rearrange("b (j p) d -> b p j d", p=P)

    def one(v, b):
        return v[bass.ds(b, 1)].rearrange("o p j d -> (o p) j d")

    with nc.Fori(0, x.shape[0]) as b:
        with Stage("mamba") as st:
            got = st.sem("got")
            with nc.Block() as block:
                @block.sync
                def _(sp):
                    sp.dma_start(X[:, :, :], one(xs, b)).then_inc(got, 16)
                    sp.wait_ge(got, 16)

            norm_tiles(st, "outer", X, XN, None, transposed=False)

            def keep_residual(link):
                nc.vector.tensor_tensor(X[:, :, :], X[:, :, :], XN[:, :, :], ALU.add)

            zs = st.sb("zs", [P, ND, SEQ])
            xc = st.sb("xc", [P, 2, ND, SEQ])
            delta = st.sb("delta", [P, 2, ND, SEQ])
            du = st.sb("du", [P, 2, ND, SEQ])
            ysum = st.sb("ysum", [P, ND, SEQ])
            bcs = st.sb("bcs", [96, 2, SEQ], BF16)
            dts = st.sb("dts", [DTR + 1, 2, SEQ])
            short = ExitStack()
            XR = st.sb("XR", [P, NJ, D], scope=short)
            norm_tiles(st, "inner", XN, XR, XT, rms=True, gain_t=W("norm_w"), extra=keep_residual)

            xi = st.sb("xi", [P, 2, ND, SEQ + PAD], scope=short)
            pr, zr, conv, conved = st.sem("projected"), st.sem("padded"), st.sem("conv"), st.sem("conved")
            zed, xid, rch, silu = st.sem("zed"), st.sem("xid"), st.sem("reversed"), st.sem("silu")
            with nc.Block() as block:
                @block.tensor
                def _(pe):
                    for e in range(2 * ND):
                        nc.tensor.matmul(PS[e][:, :], W("in_T")[:, e * P:(e + 1) * P], XT[:, :],
                                         start=True, stop=True).then_inc(pr, 1)

                @block.scalar
                def _(act):
                    for t in range(ND):
                        act.wait_ge(pr, t + 1)
                        nc.scalar.copy(xi[:, 0, t, PAD:], PS[t][:, :]).then_inc(xid, 1)
                    for t in range(ND):
                        act.wait_ge(pr, ND + t + 1)
                        nc.scalar.activation(zs[:, t, :], PS[ND + t][:, :], ACT.Silu).then_inc(zed, 1)
                    for i in range(2 * ND):
                        act.wait_ge(conved, i + 1)
                        nc.scalar.activation(xc[:, i // ND, i % ND, :], xc[:, i // ND, i % ND, :],
                                             ACT.Silu).then_inc(silu, 1)

                @block.gpsimd
                def _(pool):
                    nc.gpsimd.memset(xi[:, :, :, 0:PAD], 0.0).then_inc(zr, 1)
                    nc.gpsimd.memset(dts[:, :, :], 1.0).then_inc(zr, 1)
                    for t in range(ND):
                        pool.wait_ge(xid, t + 1)
                        nc.gpsimd.tensor_copy(xi[:, 1, t, PAD:], xi[:, 0, t, SEQ + PAD - 1:PAD - 1:-1]).then_inc(rch, 1)

                @block.vector
                def _(dve):
                    link = Chain(dve, conv)
                    dve.wait_ge(zr, 2)
                    for i in range(2 * ND):
                        d, t = i // ND, i % ND
                        if d:
                            dve.wait_ge(rch, t + 1)
                        else:
                            dve.wait_ge(xid, t + 1)
                        cw = W("conv_w")[:, i * KC:(i + 1) * KC]
                        acc = xc[:, d, t, :]
                        link(nc.vector.tensor_scalar(acc, xi[:, d, t, 0:SEQ], cw[:, 0:1], W("conv_b")[:, i:i + 1],
                                                     ALU.mult, ALU.add))
                        for k in range(1, KC):
                            ins = nc.vector.scalar_tensor_tensor(acc, xi[:, d, t, k:k + SEQ], cw[:, k:k + 1], acc,
                                                                 ALU.mult, ALU.add)
                            if k < KC - 1:
                                link(ins)
                        ins.then_inc(conved, 1)

            short.close()
            short = ExitStack()
            rem = st.sb("rem", [96, SEQ], scope=short)
            soft = st.sb("soft", [P, 2, ND, SEQ], scope=short)

            xpd, xpb, sc, dtd, dpr = (st.sem(n) for n in ("xp_dt", "xp_bc", "bc_chain", "dt_moved", "delta_ps"))
            ab, ex, ln_, wch, dd, dud = (st.sem(n) for n in ("abs", "exp", "ln", "soft_chain", "delta_done", "du_done"))
            with nc.Block() as block:
                @block.tensor
                def _(pe):
                    for d in range(2):
                        for t in range(ND):
                            last = nc.tensor.matmul(PS[2 + d][0:DTR, :],
                                                    W("xp_dt")[:, (d * ND + t) * DTR:(d * ND + t + 1) * DTR],
                                                    xc[:, d, t, :], start=(t == 0), stop=(t == ND - 1))
                        last.then_inc(xpd, 1)
                    for d in range(2):
                        for t in range(ND):
                            last = nc.tensor.matmul(PS[d][0:96, :], W("xp_bc")[:, (d * ND + t) * 96:(d * ND + t + 1) * 96],
                                                    xc[:, d, t, :], start=(t == 0), stop=(t == ND - 1))
                        last.then_inc(xpb, 1)
                        pe.wait_ge(dtd, d + 1)
                        for t in range(ND):
                            i = d * ND + t
                            last = nc.tensor.matmul(PS[4 + i][:, :], W("dt_T", DTR + 1)[:, i * P:(i + 1) * P],
                                                    dts[:, d, :], start=True, stop=True)
                        last.then_inc(dpr, 1)

                @block.scalar
                def _(act):
                    for d in range(2):
                        act.wait_ge(xpd, d + 1)
                        nc.scalar.copy(dts[0:DTR, d, :], PS[2 + d][0:DTR, :]).then_inc(dtd, 1)
                    for d in range(2):
                        act.wait_ge(dpr, d + 1)
                        nc.scalar.activation(soft[:, d, :, :], BANKS[:, 4 + 2 * d:6 + 2 * d, :], ACT.Abs).then_inc(ab, 1)
                    for d in range(2):
                        act.wait_ge(ab, d + 1)
                        nc.scalar.activation(du[:, d, :, :], soft[:, d, :, :], ACT.Exp, scale=-1.0).then_inc(ex, 1)
                    for d in range(2):
                        act.wait_ge(ex, d + 1)
                        nc.scalar.activation(soft[:, d, :, :], du[:, d, :, :], ACT.Ln, bias=1.0).then_inc(ln_, 1)

                @block.vector
                def _(dve):
                    V = nc.vector
                    link = Chain(dve, sc)
                    for d in range(2):
                        dve.wait_ge(xpb, d + 1)
                        src = PS[d]
                        link(V.tensor_copy(bcs[:, d, :], src[0:96, :]))
                        link(V.tensor_tensor(rem[:, :], src[0:96, :], bcs[:, d, :], ALU.subtract))
                        V.tensor_copy(bcs[32:64, d, :], rem[32:64, :])
                        link(V.tensor_copy(bcs[64:96, d, :], rem[64:96, :]))
                        link(V.tensor_tensor(rem[64:96, :], rem[64:96, :], bcs[64:96, d, :], ALU.subtract))
                        link(V.tensor_copy(bcs[64:96, d, :], rem[64:96, :]))
                    link = Chain(dve, wch)
                    for d in range(2):
                        dve.wait_ge(ex, d + 1)
                        link(V.tensor_scalar(delta[:, d, :, :], du[:, d, :, :], 1.0, -1.0, ALU.add, ALU.add))
                        link(V.tensor_tensor(delta[:, d, :, :], du[:, d, :, :], delta[:, d, :, :], ALU.subtract))
                    for d in range(2):
                        dve.wait_ge(ln_, d + 1)
                        link(V.tensor_tensor(soft[:, d, :, :], soft[:, d, :, :], delta[:, d, :, :], ALU.add))
                        V.scalar_tensor_tensor(delta[:, d, :, :], BANKS[:, 4 + 2 * d:6 + 2 * d, :], 0.0, soft[:, d, :, :],
                                               ALU.max, ALU.add).then_inc(dd, 1)

                @block.gpsimd
                def _(pool):
                    for d in range(2):
                        pool.wait_ge(dd, d + 1)
                        nc.gpsimd.tensor_tensor(du[:, d, :, :], delta[:, d, :, :], xc[:, d, :, :], ALU.mult).then_inc(dud, 1)

            short.close()

            STEPS = 2 * NS
            RD, RW, AHEAD = 2, 4, 3
            decay = st.sb("decay", [P, RD, ND, SEQ])
            work = st.sb("work", [P, RW, ND, SEQ])
            c_all = st.sb("c_all", [P, 2, SEQ])
            bcast, c_cp, dec, drv = st.sem("bcast"), st.sem("c_cp"), st.sem("dec"), st.sem("drv")
            scn, rd, acc, yev = st.sem("scn"), st.sem("rd"), st.sem("acc"), st.sem("yev")
            ych, outp, cleared = st.sem("ych"), st.sem("outp"), st.sem("cleared")
            with nc.Block() as block:
                @block.tensor
                def _(pe):
                    for s in range(STEPS + AHEAD):
                        if s < STEPS:
                            d, n = s // NS, s % NS
                            if s >= 2:
                                pe.wait_ge(drv, s - 1)
                                pe.wait_ge(c_cp, s - 1)
                            for k in range(2):
                                last = nc.tensor.matmul(PS[2 * k + s % 2][:, :], bc(WBF("pick", 96)[:, k * NS + n:k * NS + n + 1], [96, P]),
                                                        bcs[:, d, :], start=True, stop=True)
                            last.then_inc(bcast, 1)
                        m = s - AHEAD
                        if m >= 0:
                            d, n = m // NS, m % NS
                            pe.wait_ge(rd, m + 1)
                            for t in range(ND):
                                last = nc.tensor.matmul(PS[4 + 2 * d + t][:, :], ident, work[:, m % RW, t, :],
                                                        start=(n == 0), stop=(n == NS - 1))
                            last.then_inc(acc, 1)
                    pe.wait_ge(yev, 1)
                    for j in range(NJ):
                        for t in range(ND):
                            last = nc.tensor.matmul(PS[0][:, j * D:(j + 1) * D], ysum[:, t, j * P:(j + 1) * P],
                                                    W("out_T")[:, t * D:(t + 1) * D], start=(t == 0), stop=(t == ND - 1))
                    last.then_inc(outp, 1)

                @block.scalar
                def _(act):
                    for m in range(STEPS):
                        d, n = m // NS, m % NS
                        act.wait_ge(bcast, m + 1)
                        if m >= 2:
                            act.wait_ge(rd, m - 1)
                        nc.scalar.copy(c_all[:, m % 2, :], PS[2 + m % 2][:, :]).then_inc(c_cp, 1)
                        if m >= RD:
                            act.wait_ge(scn, m - RD + 1)
                        for t in range(ND):
                            a = (d * ND + t) * NS + n
                            last = nc.scalar.activation(decay[:, m % RD, t, 1:], delta[:, d, t, 1:], ACT.Exp,
                                                        scale=W("A")[:, a:a + 1])
                        last.then_inc(dec, 1)

                @block.vector
                def _(dve):
                    V = nc.vector
                    dve.wait_ge(cleared, 1)
                    for s in range(STEPS + 1):
                        if s < STEPS:
                            dve.wait_ge(bcast, s + 1)
                            if s >= RW:
                                dve.wait_ge(acc, s - RW + 1)
                            V.tensor_tensor(work[:, s % RW, :, :], bc(PS[s % 2].unsqueeze(1), [P, ND, SEQ]),
                                            du[:, s // NS, :, :], ALU.mult).then_inc(drv, 1)
                        m = s - 1
                        if m >= 0:
                            dve.wait_ge(dec, m + 1)
                            dve.wait_ge(drv, m + 1)
                            w = work[:, m % RW, :, :].rearrange("p t s -> p (t s)")
                            V.tensor_tensor_scan(w, decay[:, m % RD, :, :].rearrange("p t s -> p (t s)"), w, 0.0,
                                                 ALU.mult, ALU.add).then_inc(scn, 1)
                    link = Chain(dve, ych)
                    dve.wait_ge(acc, STEPS)
                    for t in range(ND):
                        V.scalar_tensor_tensor(ysum[:, t, :], xc[:, 0, t, :], W("D")[:, t:t + 1], PS[4 + t][:, :],
                                               ALU.mult, ALU.add)
                        link(V.scalar_tensor_tensor(xc[:, 1, t, :], xc[:, 1, t, :], W("D")[:, ND + t:ND + t + 1],
                                                    PS[6 + t][:, :], ALU.mult, ALU.add))
                        link(V.tensor_tensor(ysum[:, t, :], ysum[:, t, :], xc[:, 1, t, ::-1], ALU.add))
                        ins = V.scalar_tensor_tensor(ysum[:, t, :], ysum[:, t, :], 0.5, zs[:, t, :], ALU.mult, ALU.mult)
                    ins.then_inc(yev, 1)
                    dve.wait_ge(outp, 1)
                    V.tensor_tensor(X[:, :, :], X[:, :, :], PS[0][:, :].rearrange(tiles, j=NJ), ALU.add)

                @block.gpsimd
                def _(pool):
                    nc.gpsimd.memset(decay[:, :, :, 0:1], 0.0).then_inc(cleared, 1)
                    for m in range(STEPS):
                        pool.wait_ge(scn, m + 1)
                        pool.wait_ge(c_cp, m + 1)
                        nc.gpsimd.tensor_tensor(work[:, m % RW, :, :], work[:, m % RW, :, :],
                                                bc(c_all[:, m % 2, :].unsqueeze(1), [P, ND, SEQ]), ALU.mult).then_inc(rd, 1)

        with Stage("moe0") as st:
            norm_tiles(st, "ln", X, XN, XT)
            comb, comb_t = st.sb("comb", [P, NJ, E0]), st.sb("comb_t", [E0, SEQ])
            gates(st, XT, W("gate_T"), E0, comb, comb_t, grouped_bias=W("gate_b"))
            NP0 = E0 * INTER // P + 1
            cp3, cp3_t, left = st.sb("cp3", [P, NJ, 96], BF16), st.sb("cp3_t", [96, SEQ], BF16), st.sb("left", [P, NJ, E0])
            pz, pch, pd, pt, pe_ = (st.sem(n) for n in ("pz", "pch", "pd", "pt", "pe"))
            with nc.Block() as block:
                @block.gpsimd
                def _(pool):
                    nc.gpsimd.memset(cp3[:, :, :], 0.0).then_inc(pz, 1)

                @block.vector
                def _(dve):
                    link = Chain(dve, pch)
                    dve.wait_ge(pz, 1)
                    src = comb[:, :, :]
                    for lvl in range(3):
                        part = cp3[:, :, 32 * lvl:32 * lvl + E0]
                        ins = nc.vector.tensor_copy(part, src)
                        if lvl < 2:
                            link(ins)
                            link(nc.vector.tensor_tensor(left[:, :, :], src, part, ALU.subtract))
                            src = left[:, :, :]
                    ins.then_inc(pd, 1)

                @block.tensor
                def _(pe):
                    pe.wait_ge(pd, 1)
                    for j in range(NJ):
                        last = nc.tensor.transpose(PS[7].bitcast(BF16)[0:96, j * P:(j + 1) * P], cp3[:, j, :], ident_b)
                    last.then_inc(pt, 1)

                @block.scalar
                def _(act):
                    act.wait_ge(pt, 1)
                    nc.scalar.copy(cp3_t[:, :], PS[7].bitcast(BF16)[0:96, 0:SEQ]).then_inc(pe_, 1)

            s1 = st.sb("s1", [P, 2, SEQ])
            g = st.sb("g", [P, 2, SEQ])
            hid, act1, gated, used, ch = st.sem("hid"), st.sem("act1"), st.sem("gated"), st.sem("used"), st.sem("ch")
            with nc.Block() as block:
                @block.tensor
                def _(pe):
                    def down(r):
                        pe.wait_ge(gated, r + 1)
                        for j in range(NJ):
                            last = nc.tensor.matmul(PS[6][:, j * D:(j + 1) * D], g[:, r % 2, j * P:(j + 1) * P],
                                                    W("We2")[:, r * D:(r + 1) * D], start=(r == 0 and j == 0), stop=False,
                                                    skip_group_check=True)
                        last.then_inc(used, 1)

                    for r in range(NP0):
                        if r >= 2:
                            pe.wait_ge(gated, r - 1)
                        k = 3 * (r % 2)
                        nc.tensor.matmul(PS[k][:, :], W("We1")[:, r * P:(r + 1) * P], XT[:, :], start=True, stop=True)
                        last = nc.tensor.matmul(PS[k + 1][:, :], W("We3")[:, r * P:(r + 1) * P], XT[:, :],
                                                start=True, stop=True)
                        if r < NP0 - 1:
                            last = nc.tensor.matmul(PS[k + 2][:, :], WBF("pick_e", 96)[:, r * P:(r + 1) * P], cp3_t[:, :],
                                                    start=True, stop=True)
                        last.then_inc(hid, 1)
                        if r:
                            down(r - 1)
                    down(NP0 - 1)
                    for j in range(NJ):
                        last = nc.tensor.matmul(PS[6][:, j * D:(j + 1) * D], comb_t[:, j * P:(j + 1) * P],
                                                W("be2", E0), start=False, stop=(j == NJ - 1), skip_group_check=True)
                    last.then_inc(used, 1)

                @block.scalar
                def _(act):
                    for r in range(NP0):
                        act.wait_ge(hid, r + 1)
                        if r >= 2:
                            act.wait_ge(gated, r - 1)
                        nc.scalar.activation(s1[:, r % 2, :], PS[3 * (r % 2)][:, :], ACT.Silu,
                                             bias=W("be1")[:, r:r + 1]).then_inc(act1, 1)

                @block.vector
                def _(dve):
                    link = Chain(dve, ch)
                    V = nc.vector
                    for r in range(NP0):
                        dve.wait_ge(act1, r + 1)
                        if r >= 2:
                            dve.wait_ge(used, r - 1)
                        k = 3 * (r % 2)
                        ins = V.scalar_tensor_tensor(g[:, r % 2, :], PS[k + 1][:, :], W("be3")[:, r:r + 1],
                                                     s1[:, r % 2, :], ALU.add, ALU.mult)
                        if r < NP0 - 1:
                            link(ins)
                            ins = V.tensor_tensor(g[:, r % 2, :], g[:, r % 2, :], PS[k + 2][:, :], ALU.mult)
                        ins.then_inc(gated, 1)
                    link(V.tensor_tensor(X[:, :, :], X[:, :, :], bc(W("bs2").unsqueeze(1), [P, NJ, D]), ALU.add))
                    dve.wait_ge(used, NP0 + 1)
                    V.tensor_tensor(X[:, :, :], X[:, :, :], PS[6][:, :].rearrange(tiles, j=NJ), ALU.add)

        with Stage("attn1") as st:
            norm_tiles(st, "ln", X, XN, XT)
            vals = st.sb("vals", [P, NJ, H, DK + 1])
            O = st.sb("O", [P, NJ, H * DK])
            qk = st.sb("qk", [P, 2, 2, SEQ])
            toep = st.sb("toep", [P, 2, TW])
            vp, vc = st.sem("vp"), st.sem("vc")
            with nc.Block() as block:
                @block.tensor
                def _(pe):
                    for i in range(2 * NJ):
                        j, c = i // 2, i % 2
                        if i >= 4:
                            pe.wait_ge(vc, i - 3)
                        nc.tensor.matmul(PS[i % 4][:, :], XT[:, j * P:(j + 1) * P], W("Wv")[:, c * 512:(c + 1) * 512],
                                         start=True, stop=True).then_inc(vp, 1)

                @block.gpsimd
                def _(pool):
                    nc.gpsimd.memset(vals[:, :, :, DK], 1.0)

                @block.scalar
                def _(act):
                    for i in range(2 * NJ):
                        j, c = i // 2, i % 2
                        act.wait_ge(vp, i + 1)
                        nc.scalar.copy(vals[:, j, c * 8:(c + 1) * 8, 0:DK],
                                       PS[i % 4][:, :].rearrange("p (h v) -> p h v", v=DK)).then_inc(vc, 1)

            toep_ld = [st.sem(f"toep_ld{i}") for i in range(2)]
            qk_ps, qk_cp = st.sem("qk_ps"), st.sem("qk_cp")

            def load_bias(block):
                @block.sync
                def _(sp):
                    for h in range(H):
                        if h >= 2:
                            sp.wait_ge(st.sems["maxed"], NJ * (h - 1))
                        line = bias_dram[h:h + 1, :]
                        src = bass.AP(line.tensor, line.offset, [[1, P], [1, TW]])
                        sp.dma_start(toep[:, h % 2, :], src).then_inc(toep_ld[h % 2], 16)

            def copies(s):
                if s == 0:
                    return [(0, 0), (0, 1)]
                at = {4: 0, 6: 1}.get(s % (2 * NJ))
                return [(s // (2 * NJ) + 1, at)] if at is not None and s // (2 * NJ) + 1 < H // 2 else []

            def project_ahead(pe, s):
                for r, i in copies(s + 1) if s else copies(0):
                    if 2 * r + i:
                        pe.wait_ge(qk_cp, 2 * r + i)
                    nc.tensor.matmul(PS[7][:, :], W(("Wq", "Wk")[i])[:, r * P:(r + 1) * P], XT[:, :],
                                     start=True, stop=True).then_inc(qk_ps, 1)

            def copy_ahead(act, s):
                for r, i in copies(s):
                    act.wait_ge(qk_ps, 2 * r + i + 1)
                    dst = qk[:, r % 2, i, :].rearrange("p (j t) -> p j t", j=NJ)
                    nc.scalar.copy(dst if i else dst[:, :, ::-1],
                                   PS[7][:, :].rearrange("p (j t) -> p j t", j=NJ)).then_inc(qk_cp, 1)

            def scores1(pe, u, ps):
                h, j = u // NJ, u % NJ
                if j == 0 and h % 2 == 0:
                    pe.wait_ge(qk_cp, h + 2)
                o = DK * (h % 2)
                q, k = qk[o:o + DK, (h // 2) % 2, 0, :], qk[o:o + DK, (h // 2) % 2, 1, :]
                return nc.tensor.matmul(ps, q[:, j * P:(j + 1) * P], k, start=True, stop=True)

            def bias_of(dve, u):
                h, j = u // NJ, u % NJ
                if j == 0:
                    dve.wait_ge(toep_ld[h % 2], 16 * (h // 2 + 1))
                c = P * (NJ - 1 - j)
                return toep[:, h % 2, c:c + SEQ]

            attention(st, scores1, vals, DK, O, bias_of=bias_of, loads=load_bias, pe_ahead=project_ahead,
                      act_ahead=copy_ahead)

            ot = st.sb("ot", [P, 2, SEQ])
            tn, ev, dn, ad = st.sem("tn"), st.sem("ev"), st.sem("dn"), st.sem("ad")
            NC1 = H * DK // P
            with nc.Block() as block:
                @block.tensor
                def _(pe):
                    def project(c):
                        pe.wait_ge(ev, c + 1)
                        for j in range(NJ):
                            last = nc.tensor.matmul(PS[4][:, j * D:(j + 1) * D], ot[:, c % 2, j * P:(j + 1) * P],
                                                    W("Wo")[:, c * D:(c + 1) * D], start=(c == 0 and j == 0),
                                                    stop=(c == NC1 - 1 and j == NJ - 1), skip_group_check=True)
                        last.then_inc(dn, 1)

                    for c in range(NC1):
                        if c >= 2:
                            pe.wait_ge(ev, c - 1)
                        for j in range(NJ):
                            last = nc.tensor.transpose(PS[c % 2][:, j * P:(j + 1) * P], O[:, j, c * P:(c + 1) * P], ident)
                        last.then_inc(tn, 1)
                        if c:
                            project(c - 1)
                    project(NC1 - 1)

                @block.scalar
                def _(act):
                    for c in range(NC1):
                        act.wait_ge(tn, c + 1)
                        if c >= 2:
                            act.wait_ge(dn, c - 1)
                        nc.scalar.copy(ot[:, c % 2, :].rearrange("p (j t) -> p j t", j=NJ)[:, :, ::-1],
                                       PS[c % 2][:, :].rearrange("p (j t) -> p j t", j=NJ)).then_inc(ev, 1)

                @block.vector
                def _(dve):
                    dve.wait_ge(dn, NC1)
                    nc.vector.tensor_tensor(X[:, :, :], X[:, :, :], PS[4][:, :].rearrange(tiles, j=NJ), ALU.add)

        with Stage("lora1") as st:
            norm_tiles(st, "ln", X, XN, XT)
            comb, comb_t = st.sb("comb", [P, NJ, E1]), st.sb("comb_t", [E1, SEQ])
            gates(st, XT, W("R_T"), E1, comb, comb_t, eps=1e-6)
            gh, gh_t = st.sb("gh", [P, NJ, E1 * R1]), st.sb("gh_t", [P, SEQ])
            low, gated, tn, ev, dn, ch = (st.sem(n) for n in ("low", "gated", "tn", "ev", "dn", "ch"))
            with nc.Block() as block:
                @block.tensor
                def _(pe):
                    for j in range(NJ):
                        last = nc.tensor.matmul(PS[0][:, j * P:(j + 1) * P], XT[:, j * P:(j + 1) * P], W("A1_T"),
                                                start=True, stop=True)
                    last.then_inc(low, 1)
                    pe.wait_ge(gated, 1)
                    for j in range(NJ):
                        last = nc.tensor.transpose(PS[1][:, j * P:(j + 1) * P], gh[:, j, :], ident)
                    last.then_inc(tn, 1)
                    pe.wait_ge(ev, 1)
                    for j in range(NJ):
                        nc.tensor.matmul(PS[2][:, j * P:(j + 1) * P], XT[:, j * P:(j + 1) * P], W("W_T"),
                                         start=True, stop=False)
                        last = nc.tensor.matmul(PS[2][:, j * P:(j + 1) * P], gh_t[:, j * P:(j + 1) * P], W("B1"),
                                                start=False, stop=True)
                    last.then_inc(dn, 1)

                @block.vector
                def _(dve):
                    link = Chain(dve, ch)
                    dve.wait_ge(low, 1)
                    for j in range(NJ):
                        last = nc.vector.tensor_tensor(
                            gh[:, j, :].rearrange("p (e r) -> p e r", r=R1),
                            PS[0][:, j * P:(j + 1) * P].rearrange("p (e r) -> p e r", r=R1),
                            bc(comb[:, j, :].unsqueeze(2), [P, E1, R1]), ALU.mult)
                    last.then_inc(gated, 1)
                    link(nc.vector.tensor_tensor(X[:, :, :], X[:, :, :], bc(W("b_1").unsqueeze(1), [P, NJ, D]), ALU.add))
                    dve.wait_ge(dn, 1)
                    nc.vector.tensor_tensor(X[:, :, :], X[:, :, :], PS[2][:, :].rearrange(tiles, j=NJ), ALU.add)

                @block.scalar
                def _(act):
                    act.wait_ge(tn, 1)
                    nc.scalar.copy(gh_t[:, :], PS[1][:, :]).then_inc(ev, 1)

        def rope_attention(st, w_qkv, bias, half, causal, O):
            held = ExitStack()
            vals = st.sb("vals", [P, NJ, H, VW], scope=held)
            parts = [st.sb(f"parts_{n}", [P, NJ * H, HS], BF16, scope=held) for n in "qk"]
            turned = [st.sb(f"parts_{n}T", [P, H // 2, SEQ], BF16, scope=held) for n in "qk"]
            short = ExitStack()
            qkv = st.sb("qkv", [P, NJ, 2 * D], scope=short)
            rot = st.sb("rot", [P, NJ, 2 * D], scope=short)
            tmp = st.sb("tmp", [P, 2, NJ, D], scope=short)
            pj, vcp, qcp, ch = (st.sem(n) for n in ("pj", "vcp", "qcp", "rchain"))
            ready, tn, ev, zero = (st.sem(n) for n in ("ready", "ttn", "tev", "zero"))
            with nc.Block() as block:
                @block.gpsimd
                def _(pool):
                    nc.gpsimd.memset(vals[:, :, :, HD + 1:], 0.0)
                    nc.gpsimd.memset(vals[:, :, :, HD], 1.0)
                    nc.gpsimd.memset(parts[0][:, :, SK:], 0.0).then_inc(zero, 1)
                    nc.gpsimd.memset(parts[1][:, :, SK:SM], 1.0).then_inc(zero, 1)
                    nc.gpsimd.memset(parts[1][:, :, SM:], 0.0).then_inc(zero, 1)

                @block.tensor
                def _(pe):
                    for j in range(NJ):
                        nc.tensor.matmul(PS[j][:, 0:3 * D], XT[:, j * P:(j + 1) * P], w_qkv,
                                         start=True, stop=True).then_inc(pj, 1)
                    pe.wait_ge(zero, 3)
                    n = 0
                    for i in range(2):
                        pe.wait_ge(ready, i + 1)
                        view = parts[i][:, :, :].rearrange("p (j r) s -> p j (r s)", j=NJ)
                        for r in range(H // 2):
                            if n >= 4:
                                pe.wait_ge(ev, n - 3)
                            bank = PS[4 + n % 4].bitcast(BF16)
                            for j in range(NJ):
                                last = nc.tensor.transpose(bank[:, j * P:(j + 1) * P],
                                                           view[:, j, r * P:(r + 1) * P], ident_b)
                            last.then_inc(tn, 1)
                            n += 1

                @block.scalar
                def _(act):
                    for j in range(NJ if bias is None else 0):
                        act.wait_ge(pj, j + 1)
                        nc.scalar.copy(qkv[:, j, :], PS[j][:, 0:2 * D]).then_inc(qcp, 1)
                        nc.scalar.copy(vals[:, j, :, 0:HD],
                                       PS[j][:, 2 * D:3 * D].rearrange("p (h v) -> p h v", v=HD)).then_inc(vcp, 1)
                    n = 0
                    for i in range(2):
                        for r in range(H // 2):
                            act.wait_ge(tn, n + 1)
                            nc.scalar.copy(turned[i][:, r, :], PS[4 + n % 4][:, 0:SEQ // 2].bitcast(BF16)).then_inc(ev, 1)
                            n += 1

                @block.vector
                def _(dve):
                    V = nc.vector
                    link = Chain(dve, ch)
                    if bias is None:
                        dve.wait_ge(qcp, NJ)
                    else:
                        for j in range(NJ):
                            dve.wait_ge(pj, j + 1)
                            V.tensor_tensor(vals[:, j, :, 0:HD], PS[j][:, 2 * D:3 * D].rearrange("p (h v) -> p h v", v=HD),
                                            bias[:, 2 * D:3 * D].rearrange("p (h v) -> p h v", v=HD), ALU.add)
                            last = V.tensor_tensor(qkv[:, j, :], PS[j][:, 0:2 * D], bias[:, 0:2 * D], ALU.add)
                        link(last)

                    def ends(t):
                        if half:
                            v = t[:, :, :].rearrange("p j (h a f) -> p j h a f", a=2, f=HD // 2)
                            return v[:, :, :, 0, :], v[:, :, :, 1, :]
                        v = t[:, :, :].rearrange("p j (h f a) -> p j h f a", a=2, f=HD // 2)
                        return v[:, :, :, :, 0], v[:, :, :, :, 1]

                    x1, x2 = ends(qkv)
                    r1, r2 = ends(rot)
                    shape = [P, NJ, 2 * H, HD // 2]
                    f = "p (j f) -> p j f"
                    cos = bc(W("cos").rearrange(f, j=NJ).unsqueeze(2), shape)
                    sin = bc(W("sin").rearrange(f, j=NJ).unsqueeze(2), shape)
                    t1, t2 = (tmp[:, i, :, :].rearrange("p j (h f) -> p j h f", f=HD // 2) for i in range(2))
                    V.tensor_tensor(t1, x1, cos, ALU.mult)
                    link(V.tensor_tensor(t2, x2, sin, ALU.mult))
                    link(V.tensor_tensor(r1, t1, t2, ALU.subtract))
                    V.tensor_tensor(t1, x1, sin, ALU.mult)
                    link(V.tensor_tensor(t2, x2, cos, ALU.mult))
                    link(V.tensor_tensor(r2, t1, t2, ALU.add))
                    link(V.tensor_scalar(rot[:, :, 0:D], rot[:, :, 0:D], float(HD) ** -0.5, None, ALU.mult))
                    for i, slots in enumerate((((0, 1, 2), (3, 4), (5,)), ((0, 3, 5), (1, 4), (2,)))):
                        left = rot[:, :, i * D:(i + 1) * D]
                        flat = left.rearrange("p j (h f) -> p j h f", f=HD)
                        part = parts[i][:, :, :].rearrange("p (j h) s -> p j h s", j=NJ)
                        for lvl, where in enumerate(slots):
                            first = part[:, :, :, where[0] * HD:(where[0] + 1) * HD]
                            if lvl == 2:
                                V.tensor_copy(first, flat).then_inc(ready, 1)
                                continue
                            link(V.tensor_copy(first, flat))
                            for w in where[1:]:
                                V.tensor_copy(part[:, :, :, w * HD:(w + 1) * HD], first)
                            link(V.tensor_tensor(flat, flat, first, ALU.subtract))

            short.close()
            head8_attention(st, parts[0], turned, vals, causal, O)
            held.close()

        def project_back(st, tag, O, w_o, add_to, bias=None):
            tn, ev, dn, ch = (st.sem(f"{tag}_{n}") for n in ("tn", "ev", "dn", "ch"))
            ot = st.sb(f"{tag}_ot", [P, SEQ])
            with nc.Block() as block:
                @block.tensor
                def _(pe):
                    for j in range(NJ):
                        last = nc.tensor.transpose(PS[0][:, j * P:(j + 1) * P], O[:, j, :], ident)
                    last.then_inc(tn, 1)
                    pe.wait_ge(ev, 1)
                    for j in range(NJ):
                        last = nc.tensor.matmul(PS[1][:, j * P:(j + 1) * P], ot[:, j * P:(j + 1) * P], w_o,
                                                start=True, stop=True)
                    last.then_inc(dn, 1)

                @block.scalar
                def _(act):
                    act.wait_ge(tn, 1)
                    nc.scalar.copy(ot[:, :], PS[0][:, :]).then_inc(ev, 1)

                @block.vector
                def _(dve):
                    link = Chain(dve, ch)
                    if bias is not None:
                        link(nc.vector.tensor_tensor(add_to[:, :, :], add_to[:, :, :], bc(bias.unsqueeze(1), [P, NJ, D]), ALU.add))
                    dve.wait_ge(dn, 1)
                    nc.vector.tensor_tensor(add_to[:, :, :], add_to[:, :, :], PS[1][:, :].rearrange(tiles, j=NJ), ALU.add)

        with Stage("attn2") as st:
            norm_tiles(st, "ln", X, XN, XT)
            O = st.sb("O", [P, NJ, D])
            rope_attention(st, W("qkv2"), None, False, True, O)
            project_back(st, "pb", O, W("o2"), X)

        def experts(st, w_up, w_gate, b_up, b_gate, w_down, b_down, E, tiles_per, func, comb, comb_t, acc):
            n = E * tiles_per
            NB = 2 if w_gate is not None else 4
            a1 = st.sb("a1", [P, 3, SEQ])
            s1 = st.sb("s1", [P, 2, SEQ]) if w_gate is not None else None
            hid, acted, gated, used, weighed, ch = (st.sem(f"x_{k}") for k in ("hid", "acted", "gated", "used", "weighed", "ch"))
            hidden_done = gated if w_gate is not None else acted
            with nc.Block() as block:
                @block.tensor
                def _(pe):
                    def down(i):
                        e, t = i // tiles_per, i % tiles_per
                        pe.wait_ge(hidden_done, i + 1)
                        if t == 0 and e >= 2:
                            pe.wait_ge(weighed, e - 1)
                        for j in range(NJ):
                            last = nc.tensor.matmul(PS[4 + e % 2][:, j * D:(j + 1) * D], a1[:, i % 3, j * P:(j + 1) * P],
                                                    w_down[:, i * D:(i + 1) * D], start=(t == 0 and j == 0),
                                                    stop=(t == tiles_per - 1 and j == NJ - 1), skip_group_check=True)
                        last.then_inc(used, 1)

                    for j in range(NJ):
                        nc.tensor.matmul(PS[6][:, j * D:(j + 1) * D], comb_t[:, j * P:(j + 1) * P], b_down,
                                         start=True, stop=True)
                    for i in range(n):
                        if i >= NB:
                            pe.wait_ge(hidden_done, i - NB + 1)
                        last = nc.tensor.matmul(PS[i % NB][:, :], w_up[:, i * P:(i + 1) * P], XT[:, :], start=True, stop=True)
                        if w_gate is not None:
                            last = nc.tensor.matmul(PS[2 + i % NB][:, :], w_gate[:, i * P:(i + 1) * P], XT[:, :],
                                                    start=True, stop=True)
                        last.then_inc(hid, 1)
                        if i >= 1:
                            down(i - 1)
                    down(n - 1)

                @block.scalar
                def _(act):
                    for i in range(n):
                        act.wait_ge(hid, i + 1)
                        if w_gate is None:
                            if i >= 3:
                                act.wait_ge(used, i - 2)
                            nc.scalar.activation(a1[:, i % 3, :], PS[i % NB][:, :], func, bias=b_up[:, i:i + 1]).then_inc(acted, 1)
                        else:
                            if i >= 2:
                                act.wait_ge(gated, i - 1)
                            nc.scalar.activation(s1[:, i % 2, :], PS[i % NB][:, :], func, bias=b_up[:, i:i + 1]).then_inc(acted, 1)

                @block.vector
                def _(dve):
                    V = nc.vector
                    link = Chain(dve, ch)

                    def weigh(e):
                        dve.wait_ge(used, (e + 1) * tiles_per)
                        for j in range(NJ):
                            last = V.scalar_tensor_tensor(acc[:, j, :], PS[4 + e % 2][:, j * D:(j + 1) * D],
                                                          comb[:, j, e:e + 1], acc[:, j, :], ALU.mult, ALU.add)
                        last.then_inc(weighed, 1)
                        dve.wait_ge(weighed, e + 1)

                    for i in range(n):
                        if w_gate is not None:
                            dve.wait_ge(acted, i + 1)
                            if i >= 3:
                                dve.wait_ge(used, i - 2)
                            V.scalar_tensor_tensor(a1[:, i % 3, :], PS[2 + i % NB][:, :], b_gate[:, i:i + 1], s1[:, i % 2, :],
                                                   ALU.add, ALU.mult).then_inc(gated, 1)
                        if i % tiles_per == 1 and i >= tiles_per:
                            weigh(i // tiles_per - 1)
                    weigh(E - 1)
                    V.tensor_tensor(acc[:, :, :], acc[:, :, :], PS[6][:, :].rearrange(tiles, j=NJ), ALU.add)

        with Stage("block2") as st0:
            Y = st0.sb("Y", [P, NJ, D])
            with Stage("inner2") as st:
                norm_tiles(st, "ln", X, XN, XT)
                O = st.sb("O", [P, NJ, D])
                rope_attention(st, W("qkv3"), W("bqkv3"), True, False, O)
                project_back(st, "pb", O, W("o3"), XN, bias=W("bo3"))
            norm_tiles(st0, "ln1", XN, Y, XT, gain=W("g1"), shift=W("be1_2"))
            comb, comb_t = st0.sb("comb", [P, NJ, E2]), st0.sb("comb_t", [E2, SEQ])
            gates(st0, XT, W("Wg2"), E2, comb, comb_t, bias=W("bg2"), eps=0.0)
            experts(st0, W("W1_2"), None, W("b1_2"), None, W("W2_2"), W("b2_2", E2), E2, FF // P, ACT.Gelu, comb, comb_t, Y)

            def add_back(link):
                nc.vector.tensor_tensor(X[:, :, :], X[:, :, :], XN[:, :, :], ALU.add)

            norm_tiles(st0, "ln2", Y, XN, None, gain=W("g2"), shift=W("be2_2"), extra=add_back, transposed=False)

        with Stage("memory") as st:
            norm_tiles(st, "ln", X, XN, XT)
            qkv = st.sb("qkv", [P, NJ, 3 * D])
            sq = st.sb("sq", [P, NJ, D])
            mu = st.sb("mu", [P, NJ * H])
            var = st.sb("var", [P, NJ * H])
            root = st.sb("root", [P, NJ * H])
            qkv_t = st.sb("qkv_t", [P, 3, SEQ])
            pj, cp, ch, kn, tn, ev, vsh, vrt = (st.sem(n) for n in ("pj", "cp", "ch", "kn", "tn", "ev", "vsh", "vrt"))
            with nc.Block() as block:
                @block.tensor
                def _(pe):
                    for j in range(NJ):
                        nc.tensor.matmul(PS[j][:, 0:3 * D], XT[:, j * P:(j + 1) * P], W("qkv4"),
                                         start=True, stop=True).then_inc(pj, 1)
                    for n, i in enumerate((0, 2, 1)):
                        if i == 1:
                            pe.wait_ge(kn, 1)
                        else:
                            pe.wait_ge(cp, NJ)
                        for j in range(NJ):
                            last = nc.tensor.transpose(PS[4 + n][:, j * P:(j + 1) * P], qkv[:, j, i * D:(i + 1) * D], ident)
                        last.then_inc(tn, 1)

                @block.scalar
                def _(act):
                    for j in range(NJ):
                        act.wait_ge(pj, j + 1)
                        nc.scalar.copy(qkv[:, j, :], PS[j][:, 0:3 * D]).then_inc(cp, 1)
                    act.wait_ge(vsh, 1)
                    nc.scalar.activation(root[:, :], var[:, :], ACT.Sqrt).then_inc(vrt, 1)
                    for n, i in enumerate((0, 2, 1)):
                        act.wait_ge(tn, n + 1)
                        nc.scalar.copy(qkv_t[:, i, :], PS[4 + n][:, :]).then_inc(ev, 1)

                @block.vector
                def _(dve):
                    link = Chain(dve, ch)
                    V = nc.vector
                    dve.wait_ge(cp, NJ)
                    k = qkv[:, :, D:2 * D].rearrange("p j (h f) -> p j h f", f=HD)
                    s4 = sq[:, :, :].rearrange("p j (h f) -> p j h f", f=HD)
                    shape = [P, NJ, H, HD]
                    mu_v = mu[:, :].rearrange("p (j h) -> p j h", j=NJ)
                    var_v = var[:, :].rearrange("p (j h) -> p j h", j=NJ)
                    link(V.tensor_reduce(mu_v, k, AX.X, ALU.add))
                    link(V.tensor_scalar(mu[:, :], mu[:, :], 1.0 / HD, None, ALU.mult))
                    link(V.tensor_tensor(k, k, bc(mu_v.unsqueeze(3), shape), ALU.subtract))
                    link(V.tensor_tensor(s4, k, k, ALU.mult))
                    link(V.tensor_reduce(var_v, s4, AX.X, ALU.add))
                    V.tensor_scalar(var[:, :], var[:, :], 1.0 / HD, EPS, ALU.mult, ALU.add).then_inc(vsh, 1)
                    dve.wait_ge(vrt, 1)
                    link(V.reciprocal(root[:, :], root[:, :]))
                    link(V.tensor_tensor(mu[:, :], root[:, :], root[:, :], ALU.mult))
                    link(V.tensor_tensor(mu[:, :], mu[:, :], var[:, :], ALU.mult))
                    link(V.tensor_scalar(mu[:, :], mu[:, :], -0.5, 1.5, ALU.mult, ALU.add))
                    link(V.tensor_tensor(var[:, :], mu[:, :], root[:, :], ALU.mult))
                    V.tensor_tensor(k, k, bc(var_v.unsqueeze(3), shape), ALU.mult).then_inc(kn, 1)

            vrc = st.sb("vrc", [P, 2, SEQ])
            heb = st.sb("heb", [P, 2, SEQ])
            mem = st.sb("mem", [P, 2, SEQ])
            red = st.sb("red", [P, 2, SEQ])
            yt = st.sb("yt", [P, SEQ])
            reps, vd, hd, sd, gd, summed, yev, dn = (st.sem(n) for n in ("reps", "vd", "hd", "sd", "gd", "summed", "yev", "dn"))
            with nc.Block() as block:
                @block.tensor
                def _(pe):
                    def total(g):
                        pe.wait_ge(gd, g + 1)
                        nc.tensor.matmul(PS[6][:, :], W("sum_e")[:, P - 2 * HD * (g + 1):2 * P - 2 * HD * (g + 1)], red[:, g % 2, :],
                                         start=(g == 0), stop=(g == NG - 1)).then_inc(summed, 1)

                    for g in range(NG):
                        if g >= 2:
                            pe.wait_ge(gd, g - 1)
                        k = 3 * (g % 2)
                        by_d, by_e = W("rows_d")[:, g * P:(g + 1) * P], W("rows_e")[:, g * P:(g + 1) * P]
                        nc.tensor.matmul(PS[k][:, :], by_d, qkv_t[:, 2, :], start=True, stop=True)
                        nc.tensor.matmul(PS[k + 1][:, :], by_e, qkv_t[:, 1, :], start=True, stop=True)
                        nc.tensor.matmul(PS[k + 2][:, :], by_e, qkv_t[:, 0, :],
                                         start=True, stop=True).then_inc(reps, 1)
                        if g:
                            total(g - 1)
                    total(NG - 1)
                    pe.wait_ge(yev, 1)
                    for j in range(NJ):
                        last = nc.tensor.matmul(PS[7][:, j * D:(j + 1) * D], yt[:, j * P:(j + 1) * P], W("o4"), start=True, stop=True)
                    last.then_inc(dn, 1)

                @block.scalar
                def _(act):
                    for g in range(NG):
                        act.wait_ge(reps, g + 1)
                        if g >= 2:
                            act.wait_ge(hd, g - 1)
                        nc.scalar.activation(vrc[:, g % 2, :], PS[3 * (g % 2)][:, :], ACT.Copy,
                                             scale=W("coef")[:, g:g + 1]).then_inc(vd, 1)
                    act.wait_ge(summed, NG)
                    nc.scalar.copy(yt[:, :], PS[6][:, :]).then_inc(yev, 1)

                @block.vector
                def _(dve):
                    V = nc.vector
                    for g in range(NG):
                        k = 3 * (g % 2)
                        dve.wait_ge(vd, g + 1)
                        V.tensor_tensor(heb[:, g % 2, :], PS[k + 1][:, :], vrc[:, g % 2, :], ALU.mult).then_inc(hd, 1)
                        dve.wait_ge(hd, g + 1)
                        V.tensor_tensor_scan(mem[:, g % 2, :], bc(W("ret")[:, g:g + 1], [P, SEQ]), heb[:, g % 2, :], 0.0,
                                             ALU.mult, ALU.add).then_inc(sd, 1)
                        dve.wait_ge(sd, g + 1)
                        if g >= 2:
                            dve.wait_ge(summed, g - 1)
                        V.scalar_tensor_tensor(red[:, g % 2, :], mem[:, g % 2, :], W("LTM")[:, g:g + 1], PS[k + 2][:, :],
                                               ALU.add, ALU.mult).then_inc(gd, 1)
                    dve.wait_ge(dn, 1)
                    V.tensor_tensor(X[:, :, :], X[:, :, :], PS[7][:, :].rearrange(tiles, j=NJ), ALU.add)

        with Stage("moe3") as st:
            norm_tiles(st, "ln", X, XN, XT)
            comb, comb_t = st.sb("comb", [P, NJ, E3]), st.sb("comb_t", [E3, SEQ])
            gates(st, XT, W("Wg3"), E3, comb, comb_t, eps=0.0)
            experts(st, W("W1_3"), W("W3_3"), W("b1_3"), W("b3_3"), W("W2_3"), W("b2_3", E3), E3, HID // P, ACT.Silu,
                    comb, comb_t, X)
            written = st.sem("written")
            with nc.Block() as block:
                @block.sync
                def _(sp):
                    sp.dma_start(one(ys, b), X[:, :, :]).then_inc(written, 16)
                    sp.wait_ge(written, 16)
    top.close()


def constants():
    c = {"ident": np.eye(P), "minus_half": np.full((P, NJ), -0.5)}
    tri = {}
    for E in (4, E1, E0):
        tri[f"tri{E}"] = np.broadcast_to(np.tril(np.ones((E, E)), -1).ravel(), (P, E * E))
    inv = (1.0 / (np.float32(10000.0) ** (np.arange(0, HD, 2, dtype=np.float32) / np.float32(HD)))).astype(np.float32)
    ang = (np.arange(SEQ, dtype=np.float32)[:, None] * inv[None]).astype(np.float32)
    for n, f in (("cos", np.cos), ("sin", np.sin)):
        c[n] = f(ang.astype(np.float64)).reshape(NJ, P, HD // 2).transpose(1, 0, 2).reshape(P, -1)
    pairs = P // HD
    c["sum_e"] = np.pad(np.repeat(np.eye(pairs), HD, axis=0), ((0, 0), (P - pairs, P - pairs)))
    b = {**tri, "ident_b": np.eye(P), "later": np.triu(np.full((P, P), -1e30), 1),
         "later_T": np.tril(np.full((P, P), -1e30), -1)}
    b["pick"] = np.tile(np.eye(2 * NS), (3, 1))
    b["pick_e"] = np.tile(np.repeat(np.eye(2 * NS)[:, :E0], INTER, axis=1), (3, 1))
    eye = np.eye(P)
    c["rows_d"] = np.repeat(eye, HD, axis=1)
    c["rows_e"] = np.tile(eye.reshape(P, H, 1, HD), (1, 1, HD, 1)).reshape(P, -1)
    return c, b


def relative_buckets():
    rel = np.arange(1024) - (SEQ - 1)
    nb = 16
    out = (rel > 0).astype(np.int32) * nb
    rp = np.abs(rel)
    large = 8 + (np.log(np.maximum(rp, 1).astype(np.float32) / np.float32(8)) / np.float32(np.log(128 / 8)) * np.float32(8)).astype(np.int32)
    out = out + np.where(rp < 8, rp, np.minimum(large, nb - 1))
    return (np.arange(32)[:, None] == out[None]).astype(np.float32)


def kernel(**inputs):
    import ml_dtypes
    import concourse.bacc as _bacc
    from concourse.bass_utils import run_bass_kernel_spmd as _run

    g = {k: np.asarray(v) for k, v in inputs.items()}
    consts, consts_b = constants()
    cols, cols_b, lora_cols = {}, {}, {}

    def pack(items, index, rows, dtype=np.float32):
        at, parts = 0, []
        for name, a in items:
            a = np.asarray(a)
            a = a.reshape(a.shape[0], -1)
            full = np.zeros((rows, a.shape[1]), dtype)
            full[:a.shape[0]] = a
            index[name] = (at, a.shape[1])
            at += a.shape[1]
            parts.append(full)
        return np.ascontiguousarray(np.concatenate(parts, 1))

    def rows(v):
        return np.broadcast_to(v.reshape(1, -1), (P, v.size))

    def feat(v):
        return v.reshape(-1, P).T

    def down(w):
        return w.reshape(-1, P, w.shape[-1]).transpose(1, 0, 2)

    a, f, q, l, m, n_, t, k = ("L0_attn_", "L0_ffn_", "L1_attn_", "L1_ffn_", "L2_attn_", "L2_ffn_", "L3_attn_", "L3_ffn_")
    both = ("_f", "_b")
    items = list(consts.items())
    items += [
        ("norm_w", g[a + "norm_w"][:, None]), ("in_T", g[a + "in_proj_w"].T), ("out_T", down(g[a + "out_proj_w"].T)),
        ("conv_w", np.stack([g[a + "conv_w" + s].reshape(ND, P, KC) for s in both]).transpose(2, 0, 1, 3)),
        ("conv_b", np.stack([g[a + "conv_b" + s].reshape(ND, P) for s in both]).transpose(2, 0, 1)),
        ("xp_bc", np.stack([np.tile(g[a + "xproj_w" + s][DTR:].T.reshape(ND, P, 2 * NS), (1, 1, 3)) for s in both]).transpose(2, 0, 1, 3)),
        ("xp_dt", np.stack([g[a + "xproj_w" + s][:DTR].T.reshape(ND, P, DTR) for s in both]).transpose(2, 0, 1, 3)),
        ("dt_T", np.concatenate([np.concatenate([g[a + "dtproj_w" + s].T, g[a + "dtproj_b" + s][None]], 0) for s in both], 1)),
        ("A", np.stack([g[a + "A_log" + s].reshape(ND, P, NS) for s in both]).transpose(2, 0, 1, 3)),
        ("D", np.stack([g[a + "D" + s].reshape(ND, P) for s in both]).transpose(2, 0, 1)),
        ("gate_T", g[f + "gate_w"].T), ("gate_b", rows(g[f + "gate_b"])),
        ("We1", np.concatenate([g[f + "We1"].transpose(1, 0, 2).reshape(D, -1), g[f + "ws1"]], 1)),
        ("We3", np.concatenate([g[f + "We3"].transpose(1, 0, 2).reshape(D, -1), g[f + "ws3"]], 1)),
        ("We2", down(np.concatenate([g[f + "We2"].reshape(-1, D), g[f + "ws2"]], 0))),
        ("be1", feat(np.concatenate([g[f + "be1"].ravel(), g[f + "bs1"]]))),
        ("be3", feat(np.concatenate([g[f + "be3"].ravel(), g[f + "bs3"]]))),
        ("be2", g[f + "be2"]), ("bs2", rows(g[f + "bs2"])),
        ("Wq", g[q + "Wq"]), ("Wk", g[q + "Wk"]), ("Wv", g[q + "Wv"]), ("Wo", down(g[q + "Wo"])),
        ("W_T", g[l + "W"].T), ("R_T", g[l + "R"].T), ("A1_T", g[l + "A"].reshape(-1, D).T),
        ("B1", g[l + "B"].transpose(0, 2, 1).reshape(-1, D)), ("b_1", rows(g[l + "b"])),
        ("qkv2", g[m + "W_qkv"].T), ("o2", g[m + "W_o"].T),
        ("qkv3", np.concatenate([g[n_ + "Wq"], g[n_ + "Wk"], g[n_ + "Wv"]], 1)),
        ("bqkv3", rows(np.concatenate([g[n_ + "bq"], g[n_ + "bk"], g[n_ + "bv"]]))),
        ("o3", g[n_ + "Wo"]), ("bo3", rows(g[n_ + "bo"])), ("Wg2", g[n_ + "Wg"]), ("bg2", rows(g[n_ + "bg"])),
        ("W1_2", g[n_ + "W1"].transpose(1, 0, 2)), ("b1_2", feat(g[n_ + "b1"].ravel())),
        ("W2_2", down(g[n_ + "W2"].reshape(-1, D))), ("b2_2", g[n_ + "b2"]),
        ("g1", rows(g[n_ + "g1"])), ("be1_2", rows(g[n_ + "be1"])), ("g2", rows(g[n_ + "g2"])), ("be2_2", rows(g[n_ + "be2"])),
        ("qkv4", g[t + "W_qkv"].T), ("o4", g[t + "W_o"].T), ("LTM", feat(g[t + "W_LTM"].ravel())),
        ("Wg3", g[k + "Wg"].T), ("W1_3", g[k + "W1"].transpose(2, 0, 1)), ("W3_3", g[k + "W3"].transpose(2, 0, 1)),
        ("W2_3", down(g[k + "W2"].transpose(0, 2, 1).reshape(-1, D))),
        ("b1_3", feat(g[k + "b1"].ravel())), ("b3_3", feat(g[k + "b3"].ravel())), ("b2_3", g[k + "b2"]),
    ]
    for name, key in (("Vgs", "V_gs"), ("VT0", "V_T0"), ("btau", "beta_tau"), ("bgm", "beta_gm"), ("Cch", "C_ch"), ("gam", "gamma")):
        items.append((name, feat(np.repeat(g[t + key], HD * HD))))
    items += [("ppd", rows(g[t + "alpha_ppd"])), ("ICt", rows(g[t + "IC_threshold"])),
              ("ret", np.zeros((P, NG))), ("coef", np.zeros((P, NG)))]
    wf = pack(items, cols, P)
    wb = pack(list(consts_b.items()), cols_b, P, ml_dtypes.bfloat16)
    lora = pack([("A1", g[k + "A1"].transpose(1, 0, 2)), ("B1T", g[k + "B1"].transpose(2, 0, 1)),
                 ("A3", g[k + "A3"].transpose(1, 0, 2)), ("B3T", g[k + "B3"].transpose(2, 0, 1)),
                 ("A2", g[k + "A2"].transpose(1, 0, 2)), ("B2T", g[k + "B2"].transpose(2, 0, 1))], lora_cols, R1)
    arrays = {"in_x": np.ascontiguousarray(g[a + "x"]), "in_wf": wf, "in_wb": wb, "in_lora": lora,
              "in_onehot": relative_buckets(), "in_table": np.ascontiguousarray(g[q + "rel_bias_table"])}
    nc = _bacc.Bacc("TRN2", target_bir_lowering=False, num_devices=1)
    d = {n: nc.dram_tensor(n, v.shape, mybir.dt.from_np(v.dtype), kind="ExternalInput").ap() for n, v in arrays.items()}
    out = nc.dram_tensor("out_0", arrays["in_x"].shape, F32, kind="ExternalOutput").ap()
    bass_mk_seq(nc, d["in_x"], cols, cols_b, d["in_wf"], d["in_wb"], d["in_lora"], lora_cols, d["in_onehot"], d["in_table"], out)
    r = _run(nc, [arrays], core_ids=[0])
    return r.results[0]["out_0"]
```

```python
from contextlib import ExitStack

import numpy as np

import concourse.bass as bass
from concourse import mybir

ALU = mybir.AluOpType
ACT = mybir.ActivationFunctionType
F32 = mybir.dt.float32
BF16 = mybir.dt.bfloat16
AX = mybir.AxisListType

P = 128
D = 128
SEQ = 512
NJ = SEQ // P
BIG = 3.0e38
EPS = 1e-5

DI = 256
ND = DI // P
NS = 16
DTR = 8
KC = 4
PAD = KC - 1

H = 16
DK = 64
TW = SEQ + P * (NJ - 1)
HD = 8
HS = 64
SPLITS = 6
SK = SPLITS * HD
SM = SK + 3
VW = 32
GH = 4
E0, INTER = 16, 64
E1, R1 = 8, 16
E2, FF = 8, 512
E3, HID = 8, 256
NG = H * HD * HD // P


class Chain:

    def __init__(self, eng, sem):
        self.eng, self.sem, self.n = eng, sem, 0

    def __call__(self, ins):
        self.n += 1
        ins.then_inc(self.sem, 1)
        self.eng.wait_ge(self.sem, self.n)


class Pieces:
    pass


def bass_mk_seq(nc, x, cols_f, cols_b, ends, wf, wb, lora, lora_cols, onehot, table, out):
    top = ExitStack()

    def sbt(c, name, shape, dt=F32):
        return c.enter_context(nc.sbuf_tensor(name, shape, dt))

    WF = sbt(top, "WF", [P, wf.shape[1]])
    WB = sbt(top, "WB", [P, wb.shape[1]], BF16)

    def W(name, p=P):
        o, n = cols_f[name]
        return WF[0:p, o:o + n]

    def WBF(name, p=P):
        o, n = cols_b[name]
        return WB[0:p, o:o + n]

    X = sbt(top, "X", [P, NJ, D])
    XIN = sbt(top, "XIN", [P, NJ, D])
    XN = sbt(top, "XN", [P, NJ, D])
    XT = sbt(top, "XT", [P, SEQ])
    stats = sbt(top, "stats", [P, NJ, 6])
    mv = sbt(top, "mv", [P, NJ, 2])
    rstd = sbt(top, "rstd", [P, NJ])
    BANKS = top.enter_context(nc.psum_tensor("BANKS", [P, 8, 512], F32))
    PS = [BANKS[:, i, :] for i in range(8)]
    ident = W("ident")
    ident_b = WBF("ident_b")
    bias_dram = nc.dram_tensor("bias_line", [H, 1024], F32, kind="Internal").ap()

    tiles = "p (j d) -> p j d"

    stale = []

    class Stage:

        def __init__(self, name, last=False, at_end=lambda sp: None):
            self.name, self.last, self.at_end = name, last, at_end
            self.ctx, self.sem_ctx, self.sems = ExitStack(), ExitStack(), []

        def __enter__(self):
            return self

        def sb(self, name, shape, dt=F32, scope=None):
            return sbt(scope or self.ctx, f"{self.name}_{name}", shape, dt)

        def sem(self, name):
            s = self.sem_ctx.enter_context(nc.semaphore(f"{self.name}_{name}"))
            self.sems.append(s)
            return s

        def __exit__(self, failed, *_):
            if failed:
                return
            stale.append(self)
            if self.last:
                with nc.Block() as block:
                    clear_stale(block, self.at_end)
                release_stale()
            self.ctx.close()

    def clear_stale(block, first=lambda sp: None):
        if stale:
            @block.sync
            def _(sp):
                first(sp)
                for stage in stale:
                    for s in stage.sems:
                        sp.sem_clear(s)

    def release_stale():
        for stage in stale:
            stage.sem_ctx.close()
        stale.clear()

    def bc(ap, shape):
        return ap.to_broadcast(shape)

    def norm_tiles(st, tag, src, dst, dst_t, rms=False, gain_t=None, gain=None, shift=None, extra=None,
                   transposed=True, beside=lambda sp: None):
        ch, normed = st.sem(f"{tag}_chain"), st.sem(f"{tag}_normed")
        turned = st.sem(f"{tag}_turned")
        shifted, rooted = st.sem(f"{tag}_shifted"), st.sem(f"{tag}_rooted")
        sq = XT if rms else None
        HALF = SEQ // 2
        with nc.Block() as block:
            clear_stale(block, beside)

            @block.gpsimd
            def _(pool):
                pool.wait_ge(shifted, 1)
                nc.gpsimd.tensor_tensor(rstd[:, :], rstd[:, :], W("minus_half")[:, 0:NJ], ALU.pow).then_inc(rooted, 1)

            @block.vector
            def _(dve):
                link = Chain(dve, ch)
                if rms:
                    for j in range(NJ):
                        last = nc.vector.tensor_tensor_reduce(sq[:, j * D:(j + 1) * D], src[:, j, :], src[:, j, :], 1.0 / D, 0.0,
                                                              ALU.mult, ALU.add, rstd[:, j:j + 1])
                    link(last)
                    nc.vector.tensor_scalar(rstd[:, :], rstd[:, :], EPS, None, ALU.add).then_inc(shifted, 1)
                else:
                    for j in range(NJ):
                        last = nc.vector.bn_stats(stats[:, j, :], src[:, j, :])
                    link(last)
                    for j in range(NJ):
                        last = nc.vector.bn_aggr(mv[:, j, :], stats[:, j, :])
                    link(last)
                    nc.vector.tensor_scalar(rstd[:, :], mv[:, :, 1], EPS, None, ALU.add).then_inc(shifted, 1)
                dve.wait_ge(rooted, 1)
                for j in range(NJ):
                    if rms:
                        ins = nc.vector.tensor_scalar(dst[:, j, :], src[:, j, :], rstd[:, j:j + 1], None, ALU.mult)
                    else:
                        ins = nc.vector.tensor_scalar(dst[:, j, :], src[:, j, :], mv[:, j, 0:1], rstd[:, j:j + 1],
                                                      ALU.subtract, ALU.mult)
                    if gain is None:
                        ins.then_inc(normed, 1)
                if gain is not None:
                    link(ins)
                    link(nc.vector.tensor_tensor(dst[:, :, :], dst[:, :, :], bc(gain.unsqueeze(1), [P, NJ, D]), ALU.mult))
                    nc.vector.tensor_tensor(dst[:, :, :], dst[:, :, :], bc(shift.unsqueeze(1), [P, NJ, D]),
                                            ALU.add).then_inc(normed, NJ)
                if transposed:
                    dve.wait_ge(turned, NJ)
                    if gain_t is not None:
                        nc.vector.tensor_scalar(dst_t[:, HALF:], PS[6][:, HALF:], gain_t, None, ALU.mult)
                    else:
                        nc.vector.tensor_copy(dst_t[:, HALF:], PS[6][:, HALF:])
                if extra is not None:
                    dve.wait_ge(normed, NJ)
                    extra(dve, link)

            if transposed:
                @block.tensor
                def _(pe):
                    for j in range(NJ):
                        pe.wait_ge(normed, j + 1)
                        bank = PS[7] if j * P < HALF else PS[6]
                        nc.tensor.transpose(bank[:, j * P:(j + 1) * P], dst[:, j, :], ident).then_inc(turned, 1)

                @block.scalar
                def _(act):
                    act.wait_ge(turned, NJ // 2)
                    if gain_t is not None:
                        nc.scalar.activation(dst_t[:, 0:HALF], PS[7][:, 0:HALF], ACT.Copy, scale=gain_t)
                    else:
                        nc.scalar.copy(dst_t[:, 0:HALF], PS[7][:, 0:HALF])
        release_stale()

    def top2_mask(link, s, mask, E, big1, big2, rank):
        n = NJ * E * E
        a = big1[:, 0:n].rearrange("p (j g o) -> p j g o", j=NJ, g=E)
        b = big2[:, 0:n].rearrange("p (j g o) -> p j g o", j=NJ, g=E)
        other = bc(s.unsqueeze(2), [P, NJ, E, E])
        own = bc(s.unsqueeze(3), [P, NJ, E, E])
        tri = WBF(f"tri{E}").rearrange("p (g o) -> p g o", g=E)
        nc.vector.tensor_tensor(a, other, own, ALU.is_gt)
        link(nc.vector.tensor_tensor(b, other, own, ALU.is_equal))
        link(nc.vector.tensor_tensor(b, b, bc(tri.unsqueeze(1), [P, NJ, E, E]), ALU.mult))
        link(nc.vector.tensor_tensor(a, a, b, ALU.add))
        link(nc.vector.tensor_reduce(rank, a, AX.X, ALU.add))
        link(nc.vector.tensor_scalar(mask, rank, 2.0, None, ALU.is_lt))

    def gates(st, src_t, w_gate, E, comb, comb_t, bias=None, grouped_bias=None, eps=None):
        lg, ex, mask = st.sb("lg", [P, NJ, E]), st.sb("ex", [P, NJ, E]), st.sb("mask", [P, NJ, E])
        m1, t4 = st.sb("m1", [P, NJ]), st.sb("t4", [P, 6, NJ, 4])
        big1, big2 = st.sb("cmp1", [P, NJ * E * E]), st.sb("cmp2", [P, NJ * E * E])
        rank = st.sb("rank", [P, NJ, E])
        ch, logits, shifted = st.sem("gchain"), st.sem("logits"), st.sem("shifted")
        exped, combed, turned, moved = st.sem("exped"), st.sem("combed"), st.sem("gturned"), st.sem("gmoved")
        def products(pe):
            for j in range(NJ):
                last = nc.tensor.matmul(PS[7][:, j * E:(j + 1) * E], src_t[:, j * P:(j + 1) * P], w_gate, start=True, stop=True)
            last.then_inc(logits, 1)

        def turn(pe):
            pe.wait_ge(combed, 1)
            for j in range(NJ):
                last = nc.tensor.transpose(PS[7][0:E, j * P:(j + 1) * P], comb[:, j, :], ident)
            last.then_inc(turned, 1)

        def exponents(act):
            act.wait_ge(shifted, 1)
            nc.scalar.activation(ex[:, :, :], lg[:, :, :], ACT.Exp).then_inc(exped, 1)

        def move(act):
            act.wait_ge(turned, 1)
            nc.scalar.copy(comb_t[0:E, :], PS[7][0:E, :]).then_inc(moved, 1)

        def weights(dve, beside=lambda i: None):
            link = Chain(dve, ch)
            V = nc.vector
            raw = PS[7][:, 0:NJ * E].rearrange("p (j e) -> p j e", e=E)
            dve.wait_ge(logits, 1)
            if bias is not None:
                link(V.tensor_tensor(lg[:, :, :], raw, bc(bias.unsqueeze(1), [P, NJ, E]), ALU.add))
                raw = lg[:, :, :]
            link(V.tensor_reduce(m1[:, :], raw, AX.X, ALU.max))
            V.tensor_tensor(lg[:, :, :], raw, bc(m1[:, :].unsqueeze(2), [P, NJ, E]),
                            ALU.subtract).then_inc(shifted, 1)
            dve.wait_ge(exped, 1)
            link(V.tensor_reduce(m1[:, :], ex[:, :, :], AX.X, ALU.add))
            link(V.reciprocal(m1[:, :], m1[:, :]))
            link(V.tensor_tensor(ex[:, :, :], ex[:, :, :], bc(m1[:, :].unsqueeze(2), [P, NJ, E]), ALU.mult))
            beside(0)
            score = ex
            if grouped_bias is not None:
                link(V.tensor_tensor(lg[:, :, :], ex[:, :, :], bc(grouped_bias.unsqueeze(1), [P, NJ, E]), ALU.add))
                q = lg[:, :, :].rearrange("p j (g k) -> p j g k", k=4)
                t = [t4[:, i, :, :] for i in range(6)]
                V.tensor_tensor(t[0], q[:, :, :, 0], q[:, :, :, 1], ALU.max)
                V.tensor_tensor(t[1], q[:, :, :, 0], q[:, :, :, 1], ALU.min)
                V.tensor_tensor(t[2], q[:, :, :, 2], q[:, :, :, 3], ALU.max)
                link(V.tensor_tensor(t[3], q[:, :, :, 2], q[:, :, :, 3], ALU.min))
                V.tensor_tensor(t[4], t[0], t[2], ALU.max)
                V.tensor_tensor(t[5], t[0], t[2], ALU.min)
                link(V.tensor_tensor(t[1], t[1], t[3], ALU.max))
                link(V.tensor_tensor(t[5], t[5], t[1], ALU.max))
                link(V.tensor_tensor(t[4], t[4], t[5], ALU.add))
                top2_mask(link, t[4], t[0], 4, big1, big2, rank[:, :, 0:4])
                link(V.tensor_scalar(t[1], t[0], 1.0, BIG, ALU.subtract, ALU.mult))
                link(V.tensor_tensor(q, q, bc(t[1].unsqueeze(3), [P, NJ, 4, 4]), ALU.add))
                score = lg
            beside(1)
            top2_mask(link, score[:, :, :], mask[:, :, :], E, big1, big2, rank[:, :, :])
            if eps is None:
                V.tensor_tensor(comb[:, :, :], ex[:, :, :], mask[:, :, :], ALU.mult).then_inc(combed, 1)
            else:
                link(V.tensor_tensor(ex[:, :, :], ex[:, :, :], mask[:, :, :], ALU.mult))
                link(V.tensor_reduce(m1[:, :], ex[:, :, :], AX.X, ALU.add))
                if eps:
                    link(V.tensor_scalar(m1[:, :], m1[:, :], eps, None, ALU.add))
                link(V.reciprocal(m1[:, :], m1[:, :]))
                V.tensor_tensor(comb[:, :, :], ex[:, :, :], bc(m1[:, :].unsqueeze(2), [P, NJ, E]),
                                ALU.mult).then_inc(combed, 1)
            beside(2)

        pieces = Pieces()
        pieces.products, pieces.turn, pieces.exponents, pieces.move, pieces.weights = products, turn, exponents, move, weights
        pieces.combed, pieces.moved = combed, moved
        return pieces

    def head8_attention(st, parts, vals, causal, O):
        NGR = H // GH
        PER = GH * NJ
        LAG = PER + 4
        RING = 6
        PR = 2 * GH
        held = ExitStack()
        parts_q = parts[0]
        NTURN = H
        turned = [st.sb(f"parts_{n}T", [P, H // 2, SEQ], BF16, scope=held) for n in "qk"]
        qm = st.sb("qm", [P, 2, 2, SEQ], BF16, scope=held)
        prob = st.sb("prob", [P, PR, SEQ], scope=held)
        nmax = st.sb("nmax", [P, NJ, H], scope=held)
        ot = st.sb("o_t", [P, 2, SEQ], scope=held)
        rden = st.sb("rden", [P, NJ, GH], scope=held)
        s_done, t_done, maxed, exped, split = (st.sem(n) for n in ("s_done", "t_done", "maxed", "exped8", "split"))
        q_turned, q_moved, weighed, o_moved, o_turned, o_normed, ch, tn, ev = (st.sem(n) for n in (
            "q_turned", "q_moved", "weighed", "o_moved", "o_turned", "o_normed", "chain8", "parts_turned", "parts_moved"))
        N = NGR * PER
        order = []
        for s in range(N + LAG):
            order += [("S", s)] * (s < N) + [("T", s - LAG)] * (0 <= s - LAG)
        slot = {item: n % RING for n, item in enumerate(order)}

        def bank_free(pe, item):
            n = order.index(item)
            if n >= RING:
                kind, i = order[n - RING]
                pe.wait_ge(maxed if kind == "S" else exped, i + 1)

        def span(kind, i):
            tile = i % PER // GH
            if not causal:
                return 0, SEQ
            return (0, P * (tile + 1)) if kind == "S" else (P * tile, SEQ)

        def bank(kind, i):
            lo, hi = span(kind, i)
            return PS[slot[kind, i]][:, lo:hi]

        with nc.Block() as block:
            @block.tensor
            def _(pe):
                def score(kind, i, left, right, later, sem):
                    bank_free(pe, (kind, i))
                    tile, rows = i % PER // GH, slice(HS * (i % 2), HS * (i % 2 + 1))
                    lo, hi = span(kind, i)
                    out = bank(kind, i)
                    last = nc.tensor.matmul(out, left[rows, P * tile:P * (tile + 1)], right[rows, lo:hi],
                                            start=True, stop=not causal)
                    if causal:
                        o = P * tile - lo
                        last = nc.tensor.matmul(out[:, o:o + P], ident_b, later, start=False, stop=True)
                    last.then_inc(sem, 1)

                def turn(n):
                    r, i = n // 2, (1, 0)[n % 2]
                    if n >= 2:
                        pe.wait_ge(ev, n - 1)
                    view = parts[i][:, :, :].rearrange("p (j r) s -> p j (r s)", j=NJ)
                    for j in range(NJ):
                        last = nc.tensor.transpose(PS[6 + n % 2].bitcast(BF16)[:, j * P:(j + 1) * P],
                                                   view[:, j, r * P:(r + 1) * P], ident_b)
                    last.then_inc(tn, 1)

                for s in range(N + LAG + 8):
                    if s < N:
                        r = 2 * (s // PER) + s % GH // 2
                        if s in (0, 2):
                            turn(s)
                            turn(s + 1)
                        if s % PER < GH:
                            pe.wait_ge(ev, 2 * (r + 1))
                        score("S", s, turned[0][:, r, :], turned[1][:, r, :], WBF("later"), s_done)
                        if 4 <= s < NTURN:
                            turn(s)
                    if s % PER == 2 and 1 <= s // PER <= NGR:
                        g = s // PER - 1
                        pe.wait_ge(split, g + 1)
                        if g == 0:
                            pe.wait_ge(ev, NTURN)
                        if g == 1:
                            pe.wait_ge(q_moved, 1)
                        if g >= 2:
                            pe.wait_ge(o_normed, g - 1)
                        view = parts_q[:, :, :].rearrange("p (j r) s -> p j (r s)", j=NJ)
                        for pair in range(2):
                            for j in range(NJ):
                                last = nc.tensor.transpose(PS[7].bitcast(BF16)[:, (pair * NJ + j) * P:(pair * NJ + j + 1) * P],
                                                           view[:, j, (2 * g + pair) * P:(2 * g + pair + 1) * P], ident_b)
                        last.then_inc(q_turned, 1)
                    i = s - LAG
                    if 0 <= i < N:
                        g = i // PER
                        if i % PER == 0:
                            pe.wait_ge(q_moved, g + 1)
                        pair = i % GH // 2
                        score("T", i, turned[1][:, 2 * g + pair, :], qm[:, g % 2, pair, :], WBF("later_T"), t_done)
                    i = s - LAG - 4
                    if 0 <= i < N and i % GH == GH - 1:
                        g, kt = i // PER, i % PER // GH
                        pe.wait_ge(exped, i + 1)
                        if kt == 0 and g:
                            pe.wait_ge(o_moved, g)
                        lo = P * kt if causal else 0
                        for h in range(GH):
                            last = nc.tensor.matmul(PS[6][VW * h:VW * (h + 1), lo:], vals[:, kt, GH * g + h, :],
                                                    prob[:, (i - (GH - 1) + h) % PR, lo:],
                                                    start=(kt == 0), stop=(kt == NJ - 1))
                        last.then_inc(weighed, 1)
                    i = s - LAG - 7
                    if 0 <= i < N and i % PER == PER - 1:
                        g = i // PER
                        pe.wait_ge(o_moved, g + 1)
                        pe.wait_ge(q_moved, min(g + 2, NGR))
                        if g == NGR - 1:
                            pe.wait_ge(o_normed, g)
                        for j in range(NJ):
                            last = nc.tensor.transpose(PS[7][:, j * P:(j + 1) * P], ot[:, g % 2, j * P:(j + 1) * P], ident)
                        last.then_inc(o_turned, 1)

            @block.scalar
            def _(act):
                for n in range(NTURN):
                    act.wait_ge(tn, n + 1)
                    nc.scalar.copy(turned[(1, 0)[n % 2]][:, n // 2, :],
                                   PS[6 + n % 2][:, 0:SEQ // 2].bitcast(BF16)).then_inc(ev, 1)
                for s in range(N + LAG + 6):
                    if s % PER == 2 and 1 <= s // PER <= NGR:
                        g = s // PER - 1
                        act.wait_ge(q_turned, g + 1)
                        nc.scalar.copy(qm[:, g % 2, :, :].rearrange("p a t -> p (a t)"), PS[7].bitcast(BF16)).then_inc(q_moved, 1)
                    i = s - LAG - 5
                    if 0 <= i < N and i % PER == PER - 1:
                        g = i // PER
                        act.wait_ge(weighed, NJ * (g + 1))
                        if g >= 2:
                            act.wait_ge(o_turned, g - 1)
                        nc.scalar.copy(ot[:, g % 2, :], PS[6]).then_inc(o_moved, 1)
                    i = s - LAG
                    if 0 <= i < N:
                        act.wait_ge(t_done, i + 1)
                        if i >= PR:
                            act.wait_ge(weighed, (i - PR) // GH + 1)
                        lo, hi = span("T", i)
                        nc.scalar.activation(prob[:, i % PR, lo:hi], bank("T", i), ACT.Exp).then_inc(exped, 1)

            @block.vector
            def _(dve):
                V = nc.vector
                link = Chain(dve, ch)
                part = parts_q[:, :, :].rearrange("p (j h) s -> p j h s", j=NJ)
                for s in range(N + LAG + 9):
                    if s < N:
                        g, j = s // PER, s % PER // GH
                        h = GH * g + s % GH
                        dve.wait_ge(s_done, s + 1)
                        V.tensor_reduce(nmax[:, j, h:h + 1], bank("S", s), AX.X, ALU.max, negate=True).then_inc(maxed, 1)
                        if s % PER == PER - 1:
                            dve.wait_ge(maxed, s + 1)
                            m = nmax[:, :, GH * g:GH * (g + 1)]
                            for lvl in range(3):
                                p = part[:, :, GH * g:GH * (g + 1), SK + lvl]
                                ins = V.tensor_copy(p, m)
                                if lvl < 2:
                                    link(ins)
                                    link(V.tensor_tensor(m, m, p, ALU.subtract))
                            ins.then_inc(split, 1)
                    i = s - LAG - 8
                    if 0 <= i < N and i % PER == PER - 1:
                        g = i // PER
                        dve.wait_ge(o_turned, g + 1)
                        got = PS[7].rearrange("p (j h v) -> p j h v", j=NJ, v=VW)
                        link(V.reciprocal(rden[:, :, :], got[:, :, :, HD]))
                        out = O[:, :, GH * g * HD:GH * (g + 1) * HD].rearrange("p j (h v) -> p j h v", v=HD)
                        V.tensor_tensor(out, got[:, :, :, 0:HD], bc(rden[:, :, :].unsqueeze(3), [P, NJ, GH, HD]),
                                        ALU.mult).then_inc(o_normed, 1)
        held.close()

    xs = x.rearrange("b (j p) d -> b p j d", p=P)
    ys = out.rearrange("b (j p) d -> b p j d", p=P)

    def one(v, b):
        return v[bass.ds(b, 1)].rearrange("o p j d -> (o p) j d")

    ld_rest = top.enter_context(nc.semaphore("ld_rest"))
    x_free = top.enter_context(nc.semaphore("x_free"))

    with Stage("init", last=True) as st:
        ld_fold, ld_first, ld_b, ld_x, ch = (st.sem(n) for n in ("ld_fold", "ld_first", "ld_b", "ld_x", "ch"))
        fold, folded = st.sem("fold"), st.sem("folded")
        ach, line, lined, stored = st.sem("ach"), st.sem("line"), st.sem("lined"), st.sem("stored")
        LO = st.sb("LO", [R1, lora.shape[1]])
        OH = st.sb("OH", [32, 1024])
        TB = st.sb("TB", [32, H])
        LN = st.sb("LN", [H, 1024])

        def lo(name):
            o, n = lora_cols[name]
            return LO[:, o:o + n]

        with nc.Block() as block:
            @block.sync
            def _(sp):
                at = 0
                for end, sem in zip(ends, (ld_fold, ld_first, ld_rest)):
                    step = -(-(end - at) // 4)
                    for c in range(at, end, step):
                        sp.dma_start(WF[:, c:min(c + step, end)], wf[:, c:min(c + step, end)]).then_inc(sem, 16)
                    at = end
                    if sem is ld_fold:
                        sp.dma_start(LO[:, :], lora).then_inc(ld_x, 16)
                        sp.dma_start(OH[:, :], onehot).then_inc(ld_x, 16)
                        sp.dma_start(TB[:, :], table).then_inc(ld_x, 16)
                    if sem is ld_first:
                        sp.dma_start(WB[:, :], wb).then_inc(ld_b, 16)
                        sp.dma_start(XIN[:, :, :], one(xs, 0)).then_inc(ld_b, 16)
                        sp.dma_start(X[:, :, :], one(xs, 0)).then_inc(x_free, 16)
                        sp.wait_ge(lined, 2)
                        sp.dma_start(bias_dram, LN[:, :]).then_inc(stored, 16)
                sp.wait_ge(ld_first, 64)
                sp.wait_ge(ld_b, 32)
                sp.wait_ge(stored, 16)

            def jobs():
                for w, a, b in (("W1_3", "A1", "B1T"), ("W3_3", "A3", "B3T")):
                    for e in range(E3):
                        yield (lo(a)[:, e * D:(e + 1) * D], lo(b)[:, e * HID:(e + 1) * HID],
                               W(w)[:, e * HID:(e + 1) * HID])
                for e in range(E3):
                    for t in range(HID // P):
                        yield (lo("A2")[:, e * HID + t * P:e * HID + (t + 1) * P], lo("B2T")[:, e * D:(e + 1) * D],
                               W("W2_3")[:, (2 * e + t) * D:(2 * e + t + 1) * D])

            @block.tensor
            def _(pe):
                pe.wait_ge(ld_x, 48)
                for i in range(2):
                    nc.tensor.matmul(PS[6 + i][0:H, :], TB[:, :], OH[:, i * 512:(i + 1) * 512],
                                     start=True, stop=True).then_inc(line, 1)
                for i, (a, b, w) in enumerate(jobs()):
                    if i >= 4:
                        pe.wait_ge(folded, i - 3)
                    nc.tensor.matmul(PS[i % 4][:, 0:w.shape[1]], a, b, start=True, stop=True).then_inc(fold, 1)

            @block.vector
            def _(dve):
                link = Chain(dve, ch)
                V = nc.vector
                for i in range(2):
                    dve.wait_ge(line, i + 1)
                    V.tensor_copy(LN[:, i * 512:(i + 1) * 512], PS[6 + i][0:H, :]).then_inc(lined, 1)
                dve.wait_ge(ld_fold, 64)
                for i, (a, b, w) in enumerate(jobs()):
                    dve.wait_ge(fold, i + 1)
                    V.tensor_tensor(w, w, PS[i % 4][:, 0:w.shape[1]], ALU.add).then_inc(folded, 1)
                dve.wait_ge(ach, 1)
                link(V.tensor_scalar(W("A"), W("A"), -1.0, None, ALU.mult))

            @block.scalar
            def _(act):
                act.wait_ge(ld_fold, 64)
                nc.scalar.activation(W("A"), W("A"), ACT.Exp).then_inc(ach, 1)

        T = {n: st.sb(f"m_{n}", [P, NG]) for n in ("v", "a", "e", "l", "sp", "g", "t", "c", "u")}
        dv, da = st.sem("dv"), st.sem("da")
        with nc.Block() as block:
            @block.vector
            def _(dve):
                V = nc.vector
                n = [0]

                def link(ins):
                    ins.then_inc(dv, 1)
                    n[0] += 1
                    dve.wait_ge(dv, n[0])

                t = {k: v[:, :] for k, v in T.items()}
                link(V.tensor_tensor(t["v"], W("Vgs"), W("VT0"), ALU.subtract))
                link(V.tensor_tensor(t["v"], t["v"], W("LTM"), ALU.add))
                link(V.scalar_tensor_tensor(t["a"], t["v"], -1.0, t["v"], ALU.mult, ALU.max))
                dve.wait_ge(da, 2)
                link(V.tensor_scalar(t["u"], t["e"], 1.0, -1.0, ALU.add, ALU.add))
                link(V.tensor_tensor(t["l"], t["l"], t["u"], ALU.subtract))
                link(V.tensor_tensor(t["l"], t["l"], t["e"], ALU.add))
                link(V.tensor_scalar(t["u"], t["v"], 0.0, None, ALU.max))
                link(V.tensor_tensor(t["sp"], t["l"], t["u"], ALU.add))
                link(V.tensor_tensor(t["g"], t["sp"], W("btau"), ALU.mult))
                link(V.reciprocal(t["c"], W("Cch")))
                link(V.tensor_tensor(t["c"], t["c"], t["g"], ALU.mult))
                link(V.tensor_scalar(t["t"], t["g"], W("ICt"), W("ppd"), ALU.subtract, ALU.mult))
                dve.wait_ge(da, 5)
                link(V.tensor_scalar(t["u"], t["u"], 1.0, None, ALU.add))
                link(V.reciprocal(t["u"], t["u"]))
                link(V.tensor_tensor(t["u"], t["u"], t["sp"], ALU.mult))
                link(V.tensor_tensor(t["u"], t["u"], W("bgm"), ALU.mult))
                link(V.tensor_tensor(t["u"], t["u"], t["t"], ALU.mult))
                link(V.tensor_tensor(W("coef"), t["u"], W("gam"), ALU.mult))

            @block.scalar
            def _(act):
                t = {k: v[:, :] for k, v in T.items()}
                act.wait_ge(dv, 3)
                nc.scalar.activation(t["e"], t["a"], ACT.Exp, scale=-1.0).then_inc(da, 1)
                act.wait_ge(da, 1)
                nc.scalar.activation(t["l"], t["e"], ACT.Ln, bias=1.0).then_inc(da, 1)
                act.wait_ge(dv, 12)
                nc.scalar.activation(t["u"], t["v"], ACT.Exp, scale=-1.0).then_inc(da, 1)
                nc.scalar.activation(W("ret"), t["c"], ACT.Exp, scale=-1.0).then_inc(da, 1)
                nc.scalar.activation(t["t"], t["t"], ACT.Tanh).then_inc(da, 1)

    with nc.Fori(0, out.shape[0]) as b:
        with Stage("mamba") as st:
            norm_tiles(st, "outer", XIN, XN, None, transposed=False)

            def keep_residual(dve, link):
                dve.wait_ge(x_free, 16)
                nc.vector.tensor_tensor(X[:, :, :], XIN[:, :, :], XN[:, :, :], ALU.add)

            zs = st.sb("zs", [P, ND, SEQ])
            xc = st.sb("xc", [P, 2, ND, SEQ])
            delta = st.sb("delta", [P, 2, ND, SEQ])
            du = st.sb("du", [P, 2, ND, SEQ])
            ysum = st.sb("ysum", [P, ND, SEQ])
            bcs = st.sb("bcs", [96, 2, SEQ], BF16)
            dts = st.sb("dts", [DTR + 1, 2, SEQ])
            short = ExitStack()
            XR = st.sb("XR", [P, NJ, D], scope=short)
            norm_tiles(st, "inner", XN, XR, XT, rms=True, gain_t=W("norm_w"), extra=keep_residual)

            xi = st.sb("xi", [P, 2, ND, SEQ + PAD], scope=short)
            rem = st.sb("rem", [96, SEQ], scope=short)
            soft = st.sb("soft", [P, 2, ND, SEQ], scope=short)
            pr, zr, conv, conved = st.sem("projected"), st.sem("padded"), st.sem("conv"), st.sem("conved")
            zed, xid, rch, silu = st.sem("zed"), st.sem("xid"), st.sem("reversed"), st.sem("silu")
            xpd, xpb, sc, dtd, dpr = (st.sem(n) for n in ("xp_dt", "xp_bc", "bc_chain", "dt_moved", "delta_ps"))
            ab, ex, ln_, wch, dd = (st.sem(n) for n in ("abs", "exp", "ln", "soft_chain", "delta_done"))
            with nc.Block() as block:
                @block.sync
                def _(sp):
                    sp.sem_clear(x_free)

                @block.tensor
                def _(pe):
                    for e in range(2 * ND):
                        nc.tensor.matmul(PS[e][:, :], W("in_T")[:, e * P:(e + 1) * P], XT[:, :],
                                         start=True, stop=True).then_inc(pr, 1)
                    pe.wait_ge(xid, ND)
                    pe.wait_ge(zed, ND)
                    for d in range(2):
                        for t in range(ND):
                            pe.wait_ge(silu, d * ND + t + 1)
                            last = nc.tensor.matmul(PS[2 + d][0:DTR, :],
                                                    W("xp_dt")[:, (d * ND + t) * DTR:(d * ND + t + 1) * DTR],
                                                    xc[:, d, t, :], start=(t == 0), stop=(t == ND - 1))
                        last.then_inc(xpd, 1)
                        for t in range(ND):
                            last = nc.tensor.matmul(PS[d][0:96, :], W("xp_bc")[:, (d * ND + t) * 96:(d * ND + t + 1) * 96],
                                                    xc[:, d, t, :], start=(t == 0), stop=(t == ND - 1))
                        last.then_inc(xpb, 1)
                        pe.wait_ge(dtd, d + 1)
                        for t in range(ND):
                            i = d * ND + t
                            last = nc.tensor.matmul(PS[4 + i][:, :], W("dt_T", DTR + 1)[:, i * P:(i + 1) * P],
                                                    dts[:, d, :], start=True, stop=True)
                        last.then_inc(dpr, 1)

                @block.scalar
                def _(act):
                    def dt_rows(d):
                        act.wait_ge(xpd, d + 1)
                        nc.scalar.copy(dts[0:DTR, d, :], PS[2 + d][0:DTR, :]).then_inc(dtd, 1)

                    for t in range(ND):
                        act.wait_ge(pr, t + 1)
                        nc.scalar.copy(xi[:, 0, t, PAD:], PS[t][:, :]).then_inc(xid, 1)
                    for t in range(ND):
                        act.wait_ge(pr, ND + t + 1)
                        nc.scalar.activation(zs[:, t, :], PS[ND + t][:, :], ACT.Silu).then_inc(zed, 1)
                    for i in range(2 * ND):
                        if i == 2 * ND - 1:
                            dt_rows(0)
                        act.wait_ge(conved, i + 1)
                        nc.scalar.activation(xc[:, i // ND, i % ND, :], xc[:, i // ND, i % ND, :],
                                             ACT.Silu).then_inc(silu, 1)
                    dt_rows(1)
                    for d in range(2):
                        act.wait_ge(dpr, d + 1)
                        nc.scalar.activation(soft[:, d, :, :], BANKS[:, 4 + 2 * d:6 + 2 * d, :], ACT.Abs).then_inc(ab, 1)
                    for d in range(2):
                        act.wait_ge(ab, d + 1)
                        nc.scalar.activation(du[:, d, :, :], soft[:, d, :, :], ACT.Exp, scale=-1.0).then_inc(ex, 1)
                    for d in range(2):
                        act.wait_ge(ex, d + 1)
                        nc.scalar.activation(soft[:, d, :, :], du[:, d, :, :], ACT.Ln, bias=1.0).then_inc(ln_, 1)

                @block.gpsimd
                def _(pool):
                    nc.gpsimd.memset(xi[:, :, :, 0:PAD], 0.0).then_inc(zr, 1)
                    nc.gpsimd.memset(dts[:, :, :], 1.0).then_inc(zr, 1)
                    for t in range(ND):
                        pool.wait_ge(xid, t + 1)
                        nc.gpsimd.tensor_copy(xi[:, 1, t, PAD:], xi[:, 0, t, SEQ + PAD - 1:PAD - 1:-1]).then_inc(rch, 1)
                    pool.wait_ge(dd, 1)
                    nc.gpsimd.tensor_tensor(du[:, 0, :, :], delta[:, 0, :, :], xc[:, 0, :, :], ALU.mult)

                @block.vector
                def _(dve):
                    link = Chain(dve, conv)
                    dve.wait_ge(zr, 2)
                    for i in range(2 * ND):
                        d, t = i // ND, i % ND
                        if d:
                            dve.wait_ge(rch, t + 1)
                        else:
                            dve.wait_ge(xid, t + 1)
                        cw = W("conv_w")[:, i * KC:(i + 1) * KC]
                        acc = xc[:, d, t, :]
                        link(nc.vector.tensor_scalar(acc, xi[:, d, t, 0:SEQ], cw[:, 0:1], W("conv_b")[:, i:i + 1],
                                                     ALU.mult, ALU.add))
                        for k in range(1, KC):
                            ins = nc.vector.scalar_tensor_tensor(acc, xi[:, d, t, k:k + SEQ], cw[:, k:k + 1], acc,
                                                                 ALU.mult, ALU.add)
                            if k < KC - 1:
                                link(ins)
                        ins.then_inc(conved, 1)
                    V = nc.vector
                    link = Chain(dve, sc)
                    for d in range(2):
                        dve.wait_ge(xpb, d + 1)
                        src = PS[d]
                        link(V.tensor_copy(bcs[:, d, :], src[0:96, :]))
                        link(V.tensor_tensor(rem[:, :], src[0:96, :], bcs[:, d, :], ALU.subtract))
                        V.tensor_copy(bcs[32:64, d, :], rem[32:64, :])
                        link(V.tensor_copy(bcs[64:96, d, :], rem[64:96, :]))
                        link(V.tensor_tensor(rem[64:96, :], rem[64:96, :], bcs[64:96, d, :], ALU.subtract))
                        link(V.tensor_copy(bcs[64:96, d, :], rem[64:96, :]))
                    link = Chain(dve, wch)
                    for d in range(2):
                        dve.wait_ge(ex, d + 1)
                        link(V.tensor_scalar(delta[:, d, :, :], du[:, d, :, :], 1.0, -1.0, ALU.add, ALU.add))
                        link(V.tensor_tensor(delta[:, d, :, :], du[:, d, :, :], delta[:, d, :, :], ALU.subtract))
                    for d in range(2):
                        dve.wait_ge(ln_, d + 1)
                        link(V.tensor_tensor(soft[:, d, :, :], soft[:, d, :, :], delta[:, d, :, :], ALU.add))
                        V.scalar_tensor_tensor(delta[:, d, :, :], BANKS[:, 4 + 2 * d:6 + 2 * d, :], 0.0, soft[:, d, :, :],
                                               ALU.max, ALU.add).then_inc(dd, 1)

            short.close()

            STEPS = 2 * NS
            RD, RW, AHEAD = 2, 4, 4
            decay = st.sb("decay", [P, RD, ND, SEQ])
            work = st.sb("work", [P, RW, ND, SEQ])
            c_all = st.sb("c_all", [P, 2, SEQ])
            b_cast, c_cast, c_cp, dec, drv = st.sem("b_cast"), st.sem("c_cast"), st.sem("c_cp"), st.sem("dec"), st.sem("drv")
            scn, rd, acc, yev = st.sem("scn"), st.sem("rd"), st.sem("acc"), st.sem("yev")
            dud = st.sem("du_done")
            ych, outp, cleared = st.sem("ych"), st.sem("outp"), st.sem("cleared")
            with nc.Block() as block:
                @block.tensor
                def _(pe):
                    def spread(k, s):
                        row = WBF("pick", 96)[:, k * NS + s % NS:k * NS + s % NS + 1]
                        return nc.tensor.matmul(PS[2 * k + s % 2], bc(row, [96, P]), bcs[:, s // NS, :], start=True, stop=True)

                    for s in range(STEPS + AHEAD):
                        if s < STEPS:
                            if s >= 2:
                                pe.wait_ge(drv, s - 1)
                            spread(0, s).then_inc(b_cast, 1)
                        if 1 <= s <= STEPS:
                            if s >= 3:
                                pe.wait_ge(c_cp, s - 2)
                            spread(1, s - 1).then_inc(c_cast, 1)
                        m = s - AHEAD
                        if m >= 0:
                            d, n = m // NS, m % NS
                            pe.wait_ge(rd, m + 1)
                            for t in range(ND):
                                last = nc.tensor.matmul(PS[4 + 2 * d + t][:, :], ident, work[:, m % RW, t, :],
                                                        start=(n == 0), stop=(n == NS - 1))
                            last.then_inc(acc, 1)
                    pe.wait_ge(yev, 1)
                    for j in range(NJ):
                        for t in range(ND):
                            last = nc.tensor.matmul(PS[0][:, j * D:(j + 1) * D], ysum[:, t, j * P:(j + 1) * P],
                                                    W("out_T")[:, t * D:(t + 1) * D], start=(t == 0), stop=(t == ND - 1))
                    last.then_inc(outp, 1)

                @block.scalar
                def _(act):
                    for m in range(STEPS):
                        d, n = m // NS, m % NS
                        if m >= RD:
                            act.wait_ge(scn, m - RD + 1)
                        for t in range(ND):
                            a = (d * ND + t) * NS + n
                            last = nc.scalar.activation(decay[:, m % RD, t, 1:], delta[:, d, t, 1:], ACT.Exp,
                                                        scale=W("A")[:, a:a + 1])
                        last.then_inc(dec, 1)
                        act.wait_ge(c_cast, m + 1)
                        if m >= 2:
                            act.wait_ge(rd, m - 1)
                        nc.scalar.copy(c_all[:, m % 2, :], PS[2 + m % 2][:, :]).then_inc(c_cp, 1)

                @block.vector
                def _(dve):
                    V = nc.vector
                    dve.wait_ge(cleared, 1)
                    for s in range(STEPS + 1):
                        if s < STEPS:
                            dve.wait_ge(b_cast, s + 1)
                            if s == NS:
                                dve.wait_ge(dud, 1)
                            if s >= RW:
                                dve.wait_ge(acc, s - RW + 1)
                            V.tensor_tensor(work[:, s % RW, :, :], bc(PS[s % 2].unsqueeze(1), [P, ND, SEQ]),
                                            du[:, s // NS, :, :], ALU.mult).then_inc(drv, 1)
                        m = s - 1
                        if m >= 0:
                            dve.wait_ge(dec, m + 1)
                            dve.wait_ge(drv, m + 1)
                            w = work[:, m % RW, :, :].rearrange("p t s -> p (t s)")
                            V.tensor_tensor_scan(w, decay[:, m % RD, :, :].rearrange("p t s -> p (t s)"), w, 0.0,
                                                 ALU.mult, ALU.add).then_inc(scn, 1)
                    link = Chain(dve, ych)
                    dve.wait_ge(acc, STEPS)
                    for t in range(ND):
                        V.scalar_tensor_tensor(ysum[:, t, :], xc[:, 0, t, :], W("D")[:, t:t + 1], PS[4 + t][:, :],
                                               ALU.mult, ALU.add)
                        link(V.scalar_tensor_tensor(xc[:, 1, t, :], xc[:, 1, t, :], W("D")[:, ND + t:ND + t + 1],
                                                    PS[6 + t][:, :], ALU.mult, ALU.add))
                        link(V.tensor_tensor(ysum[:, t, :], ysum[:, t, :], xc[:, 1, t, ::-1], ALU.add))
                        ins = V.scalar_tensor_tensor(ysum[:, t, :], ysum[:, t, :], 0.5, zs[:, t, :], ALU.mult, ALU.mult)
                    ins.then_inc(yev, 1)
                    dve.wait_ge(outp, 1)
                    V.tensor_tensor(X[:, :, :], X[:, :, :], PS[0][:, :].rearrange(tiles, j=NJ), ALU.add)

                @block.gpsimd
                def _(pool):
                    nc.gpsimd.memset(decay[:, :, :, 0:1], 0.0).then_inc(cleared, 1)
                    nc.gpsimd.tensor_tensor(du[:, 1, :, :], delta[:, 1, :, :], xc[:, 1, :, :], ALU.mult).then_inc(dud, 1)
                    for m in range(STEPS):
                        pool.wait_ge(scn, m + 1)
                        pool.wait_ge(c_cp, m + 1)
                        nc.gpsimd.tensor_tensor(work[:, m % RW, :, :], work[:, m % RW, :, :],
                                                bc(c_all[:, m % 2, :].unsqueeze(1), [P, ND, SEQ]), ALU.mult).then_inc(rd, 1)

        with Stage("moe0") as st:
            norm_tiles(st, "ln", X, XN, XT)
            comb, comb_t = st.sb("comb", [P, NJ, E0]), st.sb("comb_t", [E0, SEQ])
            gate = gates(st, XT, W("gate_T"), E0, comb, comb_t, grouped_bias=W("gate_b"))
            NP0 = E0 * INTER // P
            cp3, cp3_t, left = st.sb("cp3", [P, NJ, 96], BF16), st.sb("cp3_t", [96, SEQ], BF16), st.sb("left", [P, NJ, E0])
            s1, s3 = st.sb("s1", [P, 2, SEQ]), st.sb("s3", [P, 2, SEQ])
            g = st.sb("g", [P, NP0 + 1, SEQ])
            zeroed, pch, parted, parts_turned, parts_moved = (
                st.sem(n) for n in ("zeroed", "pch", "parted", "parts_turned", "parts_moved"))
            hid, acted, multiplied, picked, weighed, down, ch = (
                st.sem(n) for n in ("hid", "acted", "multiplied", "picked", "weighed", "down", "ch"))
            order = [NP0] + list(range(NP0))
            with nc.Block() as block:
                @block.tensor
                def _(pe):
                    def project_down(r):
                        for j in range(NJ):
                            last = nc.tensor.matmul(PS[6][:, j * D:(j + 1) * D], g[:, r, j * P:(j + 1) * P],
                                                    W("We2")[:, r * D:(r + 1) * D], start=(r == NP0 and j == 0), stop=False,
                                                    skip_group_check=True)
                        last.then_inc(down, 1)

                    gate.products(pe)
                    for i, r in enumerate(order):
                        if i >= 2:
                            pe.wait_ge(acted, i - 1)
                        nc.tensor.matmul(PS[i % 2], W("We1")[:, r * P:(r + 1) * P], XT[:, :], start=True, stop=True)
                        nc.tensor.matmul(PS[2 + i % 2], W("We3")[:, r * P:(r + 1) * P], XT[:, :],
                                         start=True, stop=True).then_inc(hid, 1)
                    pe.wait_ge(multiplied, 1)
                    project_down(NP0)
                    pe.wait_ge(parted, 1)
                    for j in range(NJ):
                        last = nc.tensor.transpose(PS[7].bitcast(BF16)[0:96, j * P:(j + 1) * P], cp3[:, j, :], ident_b)
                    last.then_inc(parts_turned, 1)
                    pe.wait_ge(parts_moved, 1)
                    gate.turn(pe)
                    for r in range(NP0 + 2):
                        if r < NP0:
                            if r >= 2:
                                pe.wait_ge(weighed, r - 1)
                            nc.tensor.matmul(PS[4 + r % 2], WBF("pick_e", 96)[:, r * P:(r + 1) * P], cp3_t[:, :],
                                             start=True, stop=True).then_inc(picked, 1)
                        if r >= 2:
                            pe.wait_ge(weighed, r - 1)
                            project_down(r - 2)
                    pe.wait_ge(gate.moved, 1)
                    for j in range(NJ):
                        last = nc.tensor.matmul(PS[6][:, j * D:(j + 1) * D], comb_t[:, j * P:(j + 1) * P],
                                                W("be2", E0), start=False, stop=(j == NJ - 1), skip_group_check=True)
                    last.then_inc(down, 1)

                @block.scalar
                def _(act):
                    gate.exponents(act)
                    for i, r in enumerate(order):
                        act.wait_ge(hid, i + 1)
                        if i >= 2:
                            act.wait_ge(multiplied, i - 1)
                        nc.scalar.activation(s1[:, i % 2, :], PS[i % 2], ACT.Silu, bias=W("be1")[:, r:r + 1])
                        nc.scalar.activation(s3[:, i % 2, :], PS[2 + i % 2], ACT.Identity,
                                             bias=W("be3")[:, r:r + 1]).then_inc(acted, 1)
                    act.wait_ge(parts_turned, 1)
                    nc.scalar.copy(cp3_t[:, :], PS[7].bitcast(BF16)[0:96, 0:SEQ]).then_inc(parts_moved, 1)
                    gate.move(act)

                @block.gpsimd
                def _(pool):
                    nc.gpsimd.memset(cp3[:, :, :], 0.0).then_inc(zeroed, 1)
                    for i, r in enumerate(order):
                        pool.wait_ge(acted, i + 1)
                        nc.gpsimd.tensor_tensor(g[:, r, :], s1[:, i % 2, :], s3[:, i % 2, :], ALU.mult).then_inc(multiplied, 1)

                @block.vector
                def _(dve):
                    V = nc.vector
                    gate.weights(dve)
                    link = Chain(dve, pch)
                    dve.wait_ge(zeroed, 1)
                    dve.wait_ge(gate.combed, 1)
                    src = comb[:, :, :]
                    for lvl in range(3):
                        part = cp3[:, :, 32 * lvl:32 * lvl + E0]
                        ins = V.tensor_copy(part, src)
                        if lvl < 2:
                            link(ins)
                            link(V.tensor_tensor(left[:, :, :], src, part, ALU.subtract))
                            src = left[:, :, :]
                    ins.then_inc(parted, 1)
                    link = Chain(dve, ch)
                    link(V.tensor_tensor(X[:, :, :], X[:, :, :], bc(W("bs2").unsqueeze(1), [P, NJ, D]), ALU.add))
                    for r in range(NP0):
                        dve.wait_ge(multiplied, r + 2)
                        dve.wait_ge(picked, r + 1)
                        V.tensor_tensor(g[:, r, :], g[:, r, :], PS[4 + r % 2], ALU.mult).then_inc(weighed, 1)
                    dve.wait_ge(down, NP0 + 2)
                    V.tensor_tensor(X[:, :, :], X[:, :, :], PS[6].rearrange(tiles, j=NJ), ALU.add)

        with Stage("attn1") as st:
            def await_weights(sp):
                sp.wait_ge(ld_rest, 64)

            norm_tiles(st, "ln", X, XN, XT, beside=await_weights)
            PAIR = 2 * NJ
            U, NPAIR = H * NJ, H // 2
            TURN, WEIGH, EMPTY, PROJECT = 2, 3, 5, 7
            AHEAD_AT = (1, 3, 5)
            NS_, NP_, NT_ = 3, 4, 2 * PAIR
            qk = st.sb("qk", [P, 2, 2, SEQ])
            vals = st.sb("vals", [P, 2, NJ, 2 * DK])
            toep = st.sb("toep", [P, 4, TW])
            biased = st.sb("biased", [P, NS_, SEQ])
            prob = st.sb("prob", [P, NP_, SEQ])
            probt = st.sb("probt", [P, NT_, SEQ])
            nmax, den, rden = (st.sb(n, [P, U]) for n in ("nmax", "den", "rden"))
            ot = st.sb("ot", [P, 2, SEQ])
            toep_ld = [st.sem(f"toep_ld{i}") for i in range(4)]
            made, moved, scored, maxed, exped, inverted, scaled = (
                st.sem(n) for n in ("made", "moved", "scored", "maxed", "exped", "inverted", "scaled"))
            turned, evac, weighed, emptied, projected = (
                st.sem(n) for n in ("turned", "evac", "weighed", "emptied", "projected"))

            def unit(u):
                return u // PAIR, u % PAIR // 2, u % 2

            def ahead(s):
                r, at = s // PAIR + 1, s % PAIR
                return [(r, AHEAD_AT.index(at))] if at in AHEAD_AT and r < NPAIR else []

            def made_bank(r, i):
                return PS[7] if r else PS[(7, 5, 6)[i]]

            with nc.Block() as block:
                @block.sync
                def _(sp):
                    for h in range(H):
                        if h >= 4:
                            sp.wait_ge(maxed, PAIR * (h // 2 - 1))
                        line = bias_dram[h:h + 1, :]
                        src = bass.AP(line.tensor, line.offset, [[1, P], [1, TW]])
                        sp.dma_start(toep[:, h % 4, :], src).then_inc(toep_ld[h % 4], 16)

                @block.tensor
                def _(pe):
                    def make(r, i):
                        if r:
                            pe.wait_ge(moved, 3 * r + i)
                        if i < 2:
                            last = nc.tensor.matmul(made_bank(r, i), W(("Wq", "Wk")[i])[:, r * P:(r + 1) * P], XT[:, :],
                                                    start=True, stop=True)
                        else:
                            for j in range(NJ):
                                last = nc.tensor.matmul(made_bank(r, i)[:, j * P:(j + 1) * P], XT[:, j * P:(j + 1) * P],
                                                        W("Wv")[:, r * P:(r + 1) * P], start=True, stop=True)
                        last.then_inc(made, 1)

                    for i in range(3):
                        make(0, i)
                    for s in range(U + PROJECT):
                        if s < U:
                            r, j, a = unit(s)
                            if s % PAIR == 0:
                                pe.wait_ge(moved, 3 * r + 2)
                            if s >= NS_:
                                pe.wait_ge(maxed, s - NS_ + 1)
                            o = DK * a
                            q, k = qk[o:o + DK, r % 2, 0, :], qk[o:o + DK, r % 2, 1, :]
                            nc.tensor.matmul(PS[s % NS_], q[:, j * P:(j + 1) * P], k, start=True, stop=True).then_inc(scored, 1)
                        u = s - TURN
                        if 0 <= u < U:
                            pe.wait_ge(scaled, u + 1)
                            if u >= 2:
                                pe.wait_ge(evac, u - 1)
                            for kt in range(NJ):
                                last = nc.tensor.transpose(PS[3 + u % 2][:, kt * P:(kt + 1) * P],
                                                           prob[:, u % NP_, kt * P:(kt + 1) * P], ident)
                            last.then_inc(turned, 1)
                        u = s - WEIGH
                        if 0 <= u < U and u % PAIR == PAIR - 1:
                            r = u // PAIR
                            pe.wait_ge(evac, u + 1)
                            pe.wait_ge(moved, 3 * r + 3)
                            if r:
                                pe.wait_ge(emptied, r)
                            for kt in range(NJ):
                                for a in range(2):
                                    first = PAIR * (r % 2) + a
                                    last = nc.tensor.matmul(PS[5][DK * a:DK * (a + 1), :],
                                                            vals[:, r % 2, kt, DK * a:DK * (a + 1)],
                                                            probt[:, first:first + PAIR - 1:2, kt * P:(kt + 1) * P],
                                                            start=(kt == 0), stop=(kt == NJ - 1), skip_group_check=True)
                            last.then_inc(weighed, 1)
                        u = s - PROJECT
                        if 0 <= u < U and u % PAIR == PAIR - 1:
                            r = u // PAIR
                            pe.wait_ge(emptied, r + 1)
                            for j in range(NJ):
                                last = nc.tensor.matmul(PS[6][:, j * D:(j + 1) * D], ot[:, r % 2, j * P:(j + 1) * P],
                                                        W("Wo")[:, r * D:(r + 1) * D], start=(r == 0 and j == 0),
                                                        stop=(r == NPAIR - 1 and j == NJ - 1), skip_group_check=True)
                            last.then_inc(projected, 1)
                        for r, i in ahead(s):
                            make(r, i)

                @block.scalar
                def _(act):
                    def move(r, i):
                        act.wait_ge(made, 3 * r + i + 1)
                        bank = made_bank(r, i)
                        if i == 2:
                            if r >= 2:
                                act.wait_ge(weighed, r - 1)
                            nc.scalar.copy(vals[:, r % 2, :, :], bank.rearrange("p (j v) -> p j v", j=NJ)).then_inc(moved, 1)
                        else:
                            dst = qk[:, r % 2, i, :].rearrange("p (j t) -> p j t", j=NJ)
                            nc.scalar.copy(dst if i else dst[:, :, ::-1],
                                           bank.rearrange("p (j t) -> p j t", j=NJ)).then_inc(moved, 1)

                    for i in range(3):
                        move(0, i)
                    for s in range(U + PROJECT):
                        if s < U:
                            act.wait_ge(maxed, s + 1)
                            if s >= NP_:
                                act.wait_ge(turned, s - NP_ + 1)
                            nc.scalar.activation(prob[:, s % NP_, :], biased[:, s % NS_, :], ACT.Exp, bias=nmax[:, s:s + 1],
                                                 scale=-1.0, accum_out=den[:, s:s + 1]).then_inc(exped, 1)
                        u = s - TURN
                        if 0 <= u < U:
                            act.wait_ge(turned, u + 1)
                            if u >= NT_:
                                act.wait_ge(weighed, (u - NT_) // PAIR + 1)
                            nc.scalar.copy(probt[:, u % NT_, :], PS[3 + u % 2]).then_inc(evac, 1)
                        u = s - EMPTY
                        if 0 <= u < U and u % PAIR == PAIR - 1:
                            r = u // PAIR
                            act.wait_ge(weighed, r + 1)
                            if r >= 2:
                                act.wait_ge(projected, r - 1)
                            nc.scalar.copy(ot[:, r % 2, :].rearrange("p (j t) -> p j t", j=NJ)[:, :, ::-1],
                                           PS[5].rearrange("p (j t) -> p j t", j=NJ)).then_inc(emptied, 1)
                        for r, i in ahead(s):
                            move(r, i)

                @block.vector
                def _(dve):
                    V = nc.vector
                    for s in range(U + 1):
                        if s < U:
                            r, j, a = unit(s)
                            h = 2 * r + a
                            if j == 0:
                                dve.wait_ge(toep_ld[h % 4], 16 * (h // 4 + 1))
                            dve.wait_ge(scored, s + 1)
                            if s >= NS_:
                                dve.wait_ge(exped, s - NS_ + 1)
                            c = P * (NJ - 1 - j)
                            V.tensor_tensor_reduce(biased[:, s % NS_, :], PS[s % NS_], toep[:, h % 4, c:c + SEQ], -1.0, BIG,
                                                   ALU.add, ALU.min, nmax[:, s:s + 1]).then_inc(maxed, 1)
                        u = s - 1
                        if u >= 0:
                            dve.wait_ge(exped, u + 1)
                            V.reciprocal(rden[:, u:u + 1], den[:, u:u + 1]).then_inc(inverted, 1)
                            dve.wait_ge(inverted, u + 1)
                            V.tensor_scalar(prob[:, u % NP_, :], prob[:, u % NP_, :], rden[:, u:u + 1], None,
                                            ALU.mult).then_inc(scaled, 1)
                    dve.wait_ge(projected, NPAIR)
                    V.tensor_tensor(X[:, :, :], X[:, :, :], PS[6].rearrange(tiles, j=NJ), ALU.add)

        with Stage("lora1") as st:
            norm_tiles(st, "ln", X, XN, XT)
            comb, comb_t = st.sb("comb", [P, NJ, E1]), st.sb("comb_t", [E1, SEQ])
            gate = gates(st, XT, W("R_T"), E1, comb, comb_t, eps=1e-6)
            gh, gh_t = st.sb("gh", [P, NJ, E1 * R1]), st.sb("gh_t", [P, SEQ])
            low, gated, tn, ev, dn, ch = (st.sem(n) for n in ("low", "gated", "tn", "ev", "dn", "ch"))
            with nc.Block() as block:
                @block.tensor
                def _(pe):
                    gate.products(pe)
                    for j in range(NJ):
                        last = nc.tensor.matmul(PS[0][:, j * P:(j + 1) * P], XT[:, j * P:(j + 1) * P], W("A1_T"),
                                                start=True, stop=True)
                    last.then_inc(low, 1)
                    for j in range(NJ):
                        nc.tensor.matmul(PS[2][:, j * P:(j + 1) * P], XT[:, j * P:(j + 1) * P], W("W_T"),
                                         start=(j == 0), stop=False, skip_group_check=True)
                    pe.wait_ge(gated, 1)
                    for j in range(NJ):
                        last = nc.tensor.transpose(PS[1][:, j * P:(j + 1) * P], gh[:, j, :], ident)
                    last.then_inc(tn, 1)
                    pe.wait_ge(ev, 1)
                    for j in range(NJ):
                        last = nc.tensor.matmul(PS[2][:, j * P:(j + 1) * P], gh_t[:, j * P:(j + 1) * P], W("B1"),
                                                start=False, stop=(j == NJ - 1), skip_group_check=True)
                    last.then_inc(dn, 1)

                @block.vector
                def _(dve):
                    gate.weights(dve)
                    link = Chain(dve, ch)
                    dve.wait_ge(gate.combed, 1)
                    dve.wait_ge(low, 1)
                    for j in range(NJ):
                        last = nc.vector.tensor_tensor(
                            gh[:, j, :].rearrange("p (e r) -> p e r", r=R1),
                            PS[0][:, j * P:(j + 1) * P].rearrange("p (e r) -> p e r", r=R1),
                            bc(comb[:, j, :].unsqueeze(2), [P, E1, R1]), ALU.mult)
                    last.then_inc(gated, 1)
                    link(nc.vector.tensor_tensor(X[:, :, :], X[:, :, :], bc(W("b_1").unsqueeze(1), [P, NJ, D]), ALU.add))
                    dve.wait_ge(dn, 1)
                    nc.vector.tensor_tensor(X[:, :, :], X[:, :, :], PS[2][:, :].rearrange(tiles, j=NJ), ALU.add)

                @block.scalar
                def _(act):
                    gate.exponents(act)
                    act.wait_ge(tn, 1)
                    nc.scalar.copy(gh_t[:, :], PS[1][:, :]).then_inc(ev, 1)

        def rope_attention(st, w_qkv, bias, half, causal, O):
            held = ExitStack()
            vals = st.sb("vals", [P, NJ, H, VW], scope=held)
            parts = [st.sb(f"parts_{n}", [P, NJ * H, HS], BF16, scope=held) for n in "qk"]
            short = ExitStack()
            qkv = st.sb("qkv", [P, NJ, 2 * D], scope=short)
            rot = st.sb("rot", [P, NJ, 2 * D], scope=short)
            tmp = st.sb("tmp", [P, 2, NJ, D], scope=short)
            pj, qcp, vcp, ch, split_off = (st.sem(n) for n in ("pj", "qcp", "vcp", "rchain", "split_off"))
            slots = (((0, 1, 2), (3, 4), (5,)), ((0, 3, 5), (1, 4), (2,)))
            part = [t[:, :, :].rearrange("p (j h) s -> p j h s", j=NJ) for t in parts]
            with nc.Block() as block:
                @block.gpsimd
                def _(pool):
                    nc.gpsimd.memset(vals[:, :, :, HD + 1:], 0.0)
                    nc.gpsimd.memset(vals[:, :, :, HD], 1.0)
                    for j in range(NJ if bias is not None else 0):
                        pool.wait_ge(vcp, j + 1)
                        nc.gpsimd.tensor_tensor(vals[:, j, :, 0:HD], vals[:, j, :, 0:HD],
                                                bias[:, 2 * D:3 * D].rearrange("p (h v) -> p h v", v=HD), ALU.add)
                    nc.gpsimd.memset(parts[0][:, :, SK:], 0.0)
                    nc.gpsimd.memset(parts[1][:, :, SK:SM], 1.0)
                    nc.gpsimd.memset(parts[1][:, :, SM:], 0.0)

                @block.tensor
                def _(pe):
                    for j in range(NJ):
                        nc.tensor.matmul(PS[j][:, 0:3 * D], XT[:, j * P:(j + 1) * P], w_qkv,
                                         start=True, stop=True).then_inc(pj, 1)

                @block.scalar
                def _(act):
                    for j in range(NJ):
                        act.wait_ge(pj, j + 1)
                        if bias is None:
                            nc.scalar.copy(qkv[:, j, :], PS[j][:, 0:2 * D]).then_inc(qcp, 1)
                        nc.scalar.copy(vals[:, j, :, 0:HD],
                                       PS[j][:, 2 * D:3 * D].rearrange("p (h v) -> p h v", v=HD)).then_inc(vcp, 1)
                    n = 0
                    for i in range(2):
                        for where in slots[i][:2]:
                            n += 1
                            act.wait_ge(split_off, n)
                            for w in where[1:]:
                                nc.scalar.copy(part[i][:, :, :, w * HD:(w + 1) * HD], part[i][:, :, :, where[0] * HD:(where[0] + 1) * HD])

                @block.vector
                def _(dve):
                    V = nc.vector
                    link = Chain(dve, ch)
                    if bias is None:
                        dve.wait_ge(qcp, NJ)
                    else:
                        for j in range(NJ):
                            dve.wait_ge(vcp, j + 1)
                            last = V.tensor_tensor(qkv[:, j, :], PS[j][:, 0:2 * D], bias[:, 0:2 * D], ALU.add)
                        link(last)

                    def ends(t):
                        if half:
                            v = t[:, :, :].rearrange("p j (h a f) -> p j h a f", a=2, f=HD // 2)
                            return v[:, :, :, 0, :], v[:, :, :, 1, :]
                        v = t[:, :, :].rearrange("p j (h f a) -> p j h f a", a=2, f=HD // 2)
                        return v[:, :, :, :, 0], v[:, :, :, :, 1]

                    x1, x2 = ends(qkv)
                    r1, r2 = ends(rot)
                    shape = [P, NJ, 2 * H, HD // 2]
                    f = "p (j f) -> p j f"
                    cos = bc(W("cos").rearrange(f, j=NJ).unsqueeze(2), shape)
                    sin = bc(W("sin").rearrange(f, j=NJ).unsqueeze(2), shape)
                    t1, t2 = (tmp[:, i, :, :].rearrange("p j (h f) -> p j h f", f=HD // 2) for i in range(2))
                    V.tensor_tensor(t1, x1, cos, ALU.mult)
                    link(V.tensor_tensor(t2, x2, sin, ALU.mult))
                    link(V.tensor_tensor(r1, t1, t2, ALU.subtract))
                    V.tensor_tensor(t1, x1, sin, ALU.mult)
                    link(V.tensor_tensor(t2, x2, cos, ALU.mult))
                    link(V.tensor_tensor(r2, t1, t2, ALU.add))
                    link(V.tensor_scalar(rot[:, :, 0:D], rot[:, :, 0:D], float(HD) ** -0.5, None, ALU.mult))
                    n = 0
                    for i in range(2):
                        flat = rot[:, :, i * D:(i + 1) * D].rearrange("p j (h f) -> p j h f", f=HD)
                        for lvl, where in enumerate(slots[i]):
                            first = part[i][:, :, :, where[0] * HD:(where[0] + 1) * HD]
                            if lvl == 2:
                                V.tensor_copy(first, flat)
                                continue
                            n += 1
                            V.tensor_copy(first, flat).then_inc(split_off, 1)
                            dve.wait_ge(split_off, n)
                            link(V.tensor_tensor(flat, flat, first, ALU.subtract))

            short.close()
            head8_attention(st, parts, vals, causal, O)
            held.close()

        def project_back(st, tag, O, w_o, add_to, bias=None):
            tn, ev, dn, ch = (st.sem(f"{tag}_{n}") for n in ("tn", "ev", "dn", "ch"))
            ot = st.sb(f"{tag}_ot", [P, SEQ])
            with nc.Block() as block:
                @block.tensor
                def _(pe):
                    for j in range(NJ):
                        last = nc.tensor.transpose(PS[0][:, j * P:(j + 1) * P], O[:, j, :], ident)
                    last.then_inc(tn, 1)
                    pe.wait_ge(ev, 1)
                    for j in range(NJ):
                        last = nc.tensor.matmul(PS[1][:, j * P:(j + 1) * P], ot[:, j * P:(j + 1) * P], w_o,
                                                start=True, stop=True)
                    last.then_inc(dn, 1)

                @block.scalar
                def _(act):
                    act.wait_ge(tn, 1)
                    nc.scalar.copy(ot[:, :], PS[0][:, :]).then_inc(ev, 1)

                @block.vector
                def _(dve):
                    link = Chain(dve, ch)
                    if bias is not None:
                        link(nc.vector.tensor_tensor(add_to[:, :, :], add_to[:, :, :], bc(bias.unsqueeze(1), [P, NJ, D]), ALU.add))
                    dve.wait_ge(dn, 1)
                    nc.vector.tensor_tensor(add_to[:, :, :], add_to[:, :, :], PS[1][:, :].rearrange(tiles, j=NJ), ALU.add)

        with Stage("attn2") as st:
            norm_tiles(st, "ln", X, XN, XT)
            O = st.sb("O", [P, NJ, D])
            rope_attention(st, W("qkv2"), None, False, True, O)
            project_back(st, "pb", O, W("o2"), X)

        def experts(st, gate, w_up, w_gate, b_up, b_gate, w_down, b_down, E, tiles_per, func, comb, comb_t, acc,
                    load=None):
            n = E * tiles_per
            NB = 2 if w_gate is not None else 4
            a1 = st.sb("a1", [P, 3, SEQ])
            s1 = st.sb("s1", [P, 2, SEQ]) if w_gate is not None else None
            hid, acted, gated, used, weighed, ch = (st.sem(f"x_{k}") for k in ("hid", "acted", "gated", "used", "weighed", "ch"))
            hidden_done = gated if w_gate is not None else acted
            with nc.Block() as block:
                if load is not None:
                    block.sync(load)

                @block.tensor
                def _(pe):
                    def down(i):
                        e, t = i // tiles_per, i % tiles_per
                        pe.wait_ge(hidden_done, i + 1)
                        if t == 0 and e >= 2:
                            pe.wait_ge(weighed, e - 1)
                        for j in range(NJ):
                            last = nc.tensor.matmul(PS[4 + e % 2][:, j * D:(j + 1) * D], a1[:, i % 3, j * P:(j + 1) * P],
                                                    w_down[:, i * D:(i + 1) * D], start=(t == 0 and j == 0),
                                                    stop=(t == tiles_per - 1 and j == NJ - 1), skip_group_check=True)
                        last.then_inc(used, 1)

                    gate.products(pe)
                    for i in range(n):
                        if i >= NB:
                            pe.wait_ge(hidden_done, i - NB + 1)
                        last = nc.tensor.matmul(PS[i % NB][:, :], w_up[:, i * P:(i + 1) * P], XT[:, :], start=True, stop=True)
                        if w_gate is not None:
                            last = nc.tensor.matmul(PS[2 + i % NB][:, :], w_gate[:, i * P:(i + 1) * P], XT[:, :],
                                                    start=True, stop=True)
                        last.then_inc(hid, 1)
                        if i >= 1:
                            down(i - 1)
                        if i == n // 2:
                            gate.turn(pe)
                    pe.wait_ge(gate.moved, 1)
                    for j in range(NJ):
                        nc.tensor.matmul(PS[6][:, j * D:(j + 1) * D], comb_t[:, j * P:(j + 1) * P], b_down,
                                         start=True, stop=True)
                    down(n - 1)

                @block.scalar
                def _(act):
                    gate.exponents(act)
                    for i in range(n):
                        if i == n // 2 + 2:
                            gate.move(act)
                        act.wait_ge(hid, i + 1)
                        if w_gate is None:
                            if i >= 3:
                                act.wait_ge(used, i - 2)
                            nc.scalar.activation(a1[:, i % 3, :], PS[i % NB][:, :], func, bias=b_up[:, i:i + 1]).then_inc(acted, 1)
                        else:
                            if i >= 2:
                                act.wait_ge(gated, i - 1)
                            nc.scalar.activation(s1[:, i % 2, :], PS[i % NB][:, :], func, bias=b_up[:, i:i + 1]).then_inc(acted, 1)

                @block.vector
                def _(dve):
                    V = nc.vector
                    link = Chain(dve, ch)

                    def weigh(e):
                        dve.wait_ge(used, (e + 1) * tiles_per)
                        for j in range(NJ):
                            last = V.scalar_tensor_tensor(acc[:, j, :], PS[4 + e % 2][:, j * D:(j + 1) * D],
                                                          comb[:, j, e:e + 1], acc[:, j, :], ALU.mult, ALU.add)
                        last.then_inc(weighed, 1)
                        dve.wait_ge(weighed, e + 1)

                    def multiply(i):
                        if w_gate is not None:
                            dve.wait_ge(acted, i + 1)
                            if i >= 3:
                                dve.wait_ge(used, i - 2)
                            V.scalar_tensor_tensor(a1[:, i % 3, :], PS[2 + i % NB][:, :], b_gate[:, i:i + 1], s1[:, i % 2, :],
                                                   ALU.add, ALU.mult).then_inc(gated, 1)

                    gate.weights(dve, beside=multiply)
                    dve.wait_ge(gate.combed, 1)
                    for i in range(n):
                        if i >= 3:
                            multiply(i)
                        if i % tiles_per == 1 and i >= tiles_per:
                            weigh(i // tiles_per - 1)
                    weigh(E - 1)
                    V.tensor_tensor(acc[:, :, :], acc[:, :, :], PS[6][:, :].rearrange(tiles, j=NJ), ALU.add)

        with Stage("block2") as st0:
            Y = st0.sb("Y", [P, NJ, D])
            with Stage("inner2") as st:
                norm_tiles(st, "ln", X, XN, XT)
                O = st.sb("O", [P, NJ, D])
                rope_attention(st, W("qkv3"), W("bqkv3"), True, False, O)
                project_back(st, "pb", O, W("o3"), XN, bias=W("bo3"))
            norm_tiles(st0, "ln1", XN, Y, XT, gain=W("g1"), shift=W("be1_2"))
            comb, comb_t = st0.sb("comb", [P, NJ, E2]), st0.sb("comb_t", [E2, SEQ])
            gate = gates(st0, XT, W("Wg2"), E2, comb, comb_t, bias=W("bg2"), eps=0.0)
            experts(st0, gate, W("W1_2"), None, W("b1_2"), None, W("W2_2"), W("b2_2", E2), E2, FF // P, ACT.Gelu, comb, comb_t, Y)

            def add_back(dve, link):
                nc.vector.tensor_tensor(X[:, :, :], X[:, :, :], XN[:, :, :], ALU.add)

            norm_tiles(st0, "ln2", Y, XN, None, gain=W("g2"), shift=W("be2_2"), extra=add_back, transposed=False)

        with Stage("memory") as st:
            norm_tiles(st, "ln", X, XN, XT)
            qkv = st.sb("qkv", [P, NJ, 3 * D])
            sq = st.sb("sq", [P, NJ, D])
            mu = st.sb("mu", [P, NJ * H])
            var = st.sb("var", [P, NJ * H])
            root = st.sb("root", [P, NJ * H])
            TF = 32
            NTF = D // TF
            parts = st.sb("parts", [P, NJ, 3, NTF, 3, TF], BF16)
            rows3 = st.sb("rows3", [3 * TF, 3, NTF, SEQ], BF16)
            pj, cp, ch, cast, subbed, kn, tn, ev, vsh, vrt = (
                st.sem(n) for n in ("pj", "cp", "ch", "cast", "subbed", "kn", "tn", "ev", "vsh", "vrt"))

            def part(i, lvl):
                return parts[:, :, i, :, lvl, :]

            def values(i):
                return qkv[:, :, i * D:(i + 1) * D].rearrange("p j (t f) -> p j t f", f=TF)

            vrc = st.sb("vrc", [P, 2, SEQ])
            heb = st.sb("heb", [P, 2, SEQ])
            mem = st.sb("mem", [P, 2, SEQ])
            red = st.sb("red", [P, 3, SEQ])
            yt = st.sb("yt", [P, SEQ])
            reps, q_up, vd, hd, sd, gd, summed, yev, dn = (st.sem(n) for n in ("reps", "q_up", "vd", "hd", "sd", "gd", "summed", "yev", "dn"))
            GP = P // (HD * HD) * HD
            with nc.Block() as block:
                @block.tensor
                def _(pe):
                    for j in range(NJ):
                        nc.tensor.matmul(PS[j][:, 0:3 * D], XT[:, j * P:(j + 1) * P], W("qkv4"),
                                         start=True, stop=True).then_inc(pj, 1)
                    pe.wait_ge(cp, NJ)
                    for n, i in enumerate((2, 0, 1)):
                        if i == 1:
                            pe.wait_ge(kn, 1)
                        else:
                            pe.wait_ge(cast, 5 + n)
                        for half in range(2):
                            for t in range(2):
                                for j in range(NJ):
                                    src = parts[:, j, i, 2 * half + t, :, :].rearrange("p l f -> p (l f)")
                                    last = nc.tensor.transpose(PS[2 * n + half].bitcast(BF16)[0:3 * TF, (t * NJ + j) * P:(t * NJ + j + 1) * P],
                                                               src, ident_b)
                            last.then_inc(tn, 1)

                    def total(g):
                        pe.wait_ge(gd, g + 1)
                        nc.tensor.matmul(PS[6][:, :], W("sum_e")[:, P - GP * (g + 1):2 * P - GP * (g + 1)], red[:, g % 3, :],
                                         start=(g == 0), stop=(g == NG - 1)).then_inc(summed, 1)

                    for g in range(NG):
                        if g < 2:
                            pe.wait_ge(ev, 5 + g)
                        k = 3 * (g % 2)
                        t, o = g * GP // TF, g * GP % TF // GP
                        by_d, by_e = (WBF(n, 3 * TF)[:, o * P:(o + 1) * P] for n in ("rows_d", "rows_e"))
                        if g >= 2:
                            pe.wait_ge(vd, g - 1)
                        nc.tensor.matmul(PS[k], by_d, rows3[:, 2, t, :], start=True, stop=True)
                        if g >= 2:
                            pe.wait_ge(hd, g - 1)
                        nc.tensor.matmul(PS[k + 1], by_e, rows3[:, 1, t, :], start=True, stop=True).then_inc(reps, 1)
                        if g >= 2:
                            pe.wait_ge(gd, g - 1)
                        nc.tensor.matmul(PS[k + 2], by_e, rows3[:, 0, t, :], start=True, stop=True).then_inc(q_up, 1)
                        if g >= 2:
                            total(g - 2)
                    total(NG - 2)
                    total(NG - 1)
                    pe.wait_ge(yev, 1)
                    for j in range(NJ):
                        last = nc.tensor.matmul(PS[7][:, j * D:(j + 1) * D], yt[:, j * P:(j + 1) * P], W("o4"), start=True, stop=True)
                    last.then_inc(dn, 1)

                @block.scalar
                def _(act):
                    for j in range(NJ):
                        act.wait_ge(pj, j + 1)
                        nc.scalar.copy(qkv[:, j, :], PS[j][:, 0:3 * D]).then_inc(cp, 1)
                    act.wait_ge(cp, NJ)
                    for lvl in range(3):
                        if lvl == 2:
                            act.wait_ge(vsh, 1)
                            nc.scalar.activation(root[:, :], var[:, :], ACT.Sqrt).then_inc(vrt, 1)
                        for n, i in enumerate((2, 0)):
                            if lvl:
                                act.wait_ge(subbed, 2 * (lvl - 1) + n + 1)
                            nc.scalar.copy(part(i, lvl), values(i)).then_inc(cast, 1)
                    for n, i in enumerate((2, 0, 1)):
                        for half in range(2):
                            act.wait_ge(tn, 2 * n + half + 1)
                            nc.scalar.copy(rows3[:, i, 2 * half:2 * half + 2, :].rearrange("p t s -> p (t s)"),
                                           PS[2 * n + half].bitcast(BF16)[0:3 * TF, :]).then_inc(ev, 1)
                    for g in range(NG):
                        act.wait_ge(reps, g + 1)
                        if g >= 2:
                            act.wait_ge(hd, g - 1)
                        nc.scalar.activation(vrc[:, g % 2, :], PS[3 * (g % 2)][:, :], ACT.Copy,
                                             scale=W("coef")[:, g:g + 1]).then_inc(vd, 1)
                    act.wait_ge(summed, NG)
                    nc.scalar.copy(yt[:, :], PS[6][:, :]).then_inc(yev, 1)

                @block.vector
                def _(dve):
                    link = Chain(dve, ch)
                    V = nc.vector

                    def take_off(lvl):
                        for n, i in enumerate((2, 0)):
                            dve.wait_ge(cast, 2 * lvl + n + 1)
                            V.tensor_tensor(values(i), values(i), part(i, lvl), ALU.subtract).then_inc(subbed, 1)

                    dve.wait_ge(cp, NJ)
                    k = qkv[:, :, D:2 * D].rearrange("p j (h f) -> p j h f", f=HD)
                    s4 = sq[:, :, :].rearrange("p j (h f) -> p j h f", f=HD)
                    shape = [P, NJ, H, HD]
                    mu_v = mu[:, :].rearrange("p (j h) -> p j h", j=NJ)
                    var_v = var[:, :].rearrange("p (j h) -> p j h", j=NJ)
                    link(V.tensor_reduce(mu_v, k, AX.X, ALU.add))
                    link(V.tensor_scalar(mu[:, :], mu[:, :], 1.0 / HD, None, ALU.mult))
                    link(V.tensor_tensor(k, k, bc(mu_v.unsqueeze(3), shape), ALU.subtract))
                    take_off(0)
                    link(V.tensor_tensor(s4, k, k, ALU.mult))
                    link(V.tensor_reduce(var_v, s4, AX.X, ALU.add))
                    V.tensor_scalar(var[:, :], var[:, :], 1.0 / HD, EPS, ALU.mult, ALU.add).then_inc(vsh, 1)
                    take_off(1)
                    dve.wait_ge(vrt, 1)
                    link(V.reciprocal(root[:, :], root[:, :]))
                    link(V.tensor_tensor(mu[:, :], root[:, :], root[:, :], ALU.mult))
                    link(V.tensor_tensor(mu[:, :], mu[:, :], var[:, :], ALU.mult))
                    link(V.tensor_scalar(mu[:, :], mu[:, :], -0.5, 1.5, ALU.mult, ALU.add))
                    link(V.tensor_tensor(var[:, :], mu[:, :], root[:, :], ALU.mult))
                    link(V.tensor_tensor(k, k, bc(var_v.unsqueeze(3), shape), ALU.mult))
                    for lvl in range(3):
                        ins = V.tensor_copy(part(1, lvl), values(1))
                        if lvl < 2:
                            link(ins)
                            link(V.tensor_tensor(values(1), values(1), part(1, lvl), ALU.subtract))
                    ins.then_inc(kn, 1)
                    for g in range(NG):
                        b3 = 3 * (g % 2)
                        dve.wait_ge(vd, g + 1)
                        V.tensor_tensor(heb[:, g % 2, :], PS[b3 + 1], vrc[:, g % 2, :], ALU.mult).then_inc(hd, 1)
                        dve.wait_ge(hd, g + 1)
                        V.tensor_tensor_scan(mem[:, g % 2, :], bc(W("ret")[:, g:g + 1], [P, SEQ]), heb[:, g % 2, :], 0.0,
                                             ALU.mult, ALU.add).then_inc(sd, 1)
                        dve.wait_ge(sd, g + 1)
                        if g >= 3:
                            dve.wait_ge(summed, g - 2)
                        dve.wait_ge(q_up, g + 1)
                        V.scalar_tensor_tensor(red[:, g % 3, :], mem[:, g % 2, :], W("LTM")[:, g:g + 1], PS[b3 + 2],
                                               ALU.add, ALU.mult).then_inc(gd, 1)
                    dve.wait_ge(dn, 1)
                    V.tensor_tensor(X[:, :, :], X[:, :, :], PS[7][:, :].rearrange(tiles, j=NJ), ALU.add)

        def store(sp):
            sp.dma_start(one(ys, b), X[:, :, :]).then_inc(x_free, 16)
            sp.wait_ge(loaded, 16)

        with Stage("moe3", last=True, at_end=store) as st:
            loaded = st.sem("loaded")

            def load_next(sp):
                sp.dma_start(XIN[:, :, :], one(xs, b + 1)).then_inc(loaded, 16)

            norm_tiles(st, "ln", X, XN, XT)
            comb, comb_t = st.sb("comb", [P, NJ, E3]), st.sb("comb_t", [E3, SEQ])
            gate = gates(st, XT, W("Wg3"), E3, comb, comb_t, eps=0.0)
            experts(st, gate, W("W1_3"), W("W3_3"), W("b1_3"), W("b3_3"), W("W2_3"), W("b2_3", E3), E3, HID // P, ACT.Silu,
                    comb, comb_t, X, load=load_next)

    with nc.Block() as block:
        @block.sync
        def _(sp):
            sp.wait_ge(x_free, 16)
            sp.sem_clear(x_free)
            sp.sem_clear(ld_rest)
    top.close()


def constants():
    c = {"ident": np.eye(P), "minus_half": np.full((P, NJ), -0.5)}
    tri = {}
    for E in (4, E1, E0):
        tri[f"tri{E}"] = np.broadcast_to(np.tril(np.ones((E, E)), -1).ravel(), (P, E * E))
    inv = (1.0 / (np.float32(10000.0) ** (np.arange(0, HD, 2, dtype=np.float32) / np.float32(HD)))).astype(np.float32)
    ang = (np.arange(SEQ, dtype=np.float32)[:, None] * inv[None]).astype(np.float32)
    for n, f in (("cos", np.cos), ("sin", np.sin)):
        c[n] = f(ang.astype(np.float64)).reshape(NJ, P, HD // 2).transpose(1, 0, 2).reshape(P, -1)
    pairs = P // HD
    c["sum_e"] = np.pad(np.repeat(np.eye(pairs), HD, axis=0), ((0, 0), (P - pairs, P - pairs)))
    b = {**tri, "ident_b": np.eye(P), "later": np.triu(np.full((P, P), -1e30), 1),
         "later_T": np.tril(np.full((P, P), -1e30), -1)}
    b["pick"] = np.tile(np.eye(2 * NS), (3, 1))
    b["pick_e"] = np.tile(np.repeat(np.eye(2 * NS)[:, :E0], INTER, axis=1), (3, 1))
    eye = np.eye(32)
    b["rows_d"] = np.tile(np.repeat(eye, HD, axis=1), (3, 1))
    b["rows_e"] = np.tile(np.tile(eye.reshape(32, 4, 1, HD), (1, 1, HD, 1)).reshape(32, -1), (3, 1))
    return c, b


def relative_buckets():
    rel = np.arange(1024) - (SEQ - 1)
    nb = 16
    out = (rel > 0).astype(np.int32) * nb
    rp = np.abs(rel)
    large = 8 + (np.log(np.maximum(rp, 1).astype(np.float32) / np.float32(8)) / np.float32(np.log(128 / 8)) * np.float32(8)).astype(np.int32)
    out = out + np.where(rp < 8, rp, np.minimum(large, nb - 1))
    return (np.arange(32)[:, None] == out[None]).astype(np.float32)


def kernel(**inputs):
    import ml_dtypes
    import concourse.bacc as _bacc
    from concourse.bass_utils import run_bass_kernel_spmd as _run

    g = {k: np.asarray(v) for k, v in inputs.items()}
    consts, consts_b = constants()
    cols, cols_b, lora_cols = {}, {}, {}

    def pack(items, index, rows, dtype=np.float32):
        at, parts = 0, []
        for name, a in items:
            a = np.asarray(a)
            a = a.reshape(a.shape[0], -1)
            full = np.zeros((rows, a.shape[1]), dtype)
            full[:a.shape[0]] = a
            index[name] = (at, a.shape[1])
            at += a.shape[1]
            parts.append(full)
        return np.ascontiguousarray(np.concatenate(parts, 1))

    def rows(v):
        return np.broadcast_to(v.reshape(1, -1), (P, v.size))

    def feat(v):
        return v.reshape(-1, P).T

    def down(w):
        return w.reshape(-1, P, w.shape[-1]).transpose(1, 0, 2)

    a, f, q, l, m, n_, t, k = ("L0_attn_", "L0_ffn_", "L1_attn_", "L1_ffn_", "L2_attn_", "L2_ffn_", "L3_attn_", "L3_ffn_")
    both = ("_f", "_b")
    first = list(consts.items())
    first += [
        ("norm_w", g[a + "norm_w"][:, None]), ("in_T", g[a + "in_proj_w"].T), ("out_T", down(g[a + "out_proj_w"].T)),
        ("conv_w", np.stack([g[a + "conv_w" + s].reshape(ND, P, KC) for s in both]).transpose(2, 0, 1, 3)),
        ("conv_b", np.stack([g[a + "conv_b" + s].reshape(ND, P) for s in both]).transpose(2, 0, 1)),
        ("xp_bc", np.stack([np.tile(g[a + "xproj_w" + s][DTR:].T.reshape(ND, P, 2 * NS), (1, 1, 3)) for s in both]).transpose(2, 0, 1, 3)),
        ("xp_dt", np.stack([g[a + "xproj_w" + s][:DTR].T.reshape(ND, P, DTR) for s in both]).transpose(2, 0, 1, 3)),
        ("dt_T", np.concatenate([np.concatenate([g[a + "dtproj_w" + s].T, g[a + "dtproj_b" + s][None]], 0) for s in both], 1)),
        ("D", np.stack([g[a + "D" + s].reshape(ND, P) for s in both]).transpose(2, 0, 1)),
        ("gate_T", g[f + "gate_w"].T), ("gate_b", rows(g[f + "gate_b"])),
        ("We1", np.concatenate([g[f + "We1"].transpose(1, 0, 2).reshape(D, -1), g[f + "ws1"]], 1)),
        ("We3", np.concatenate([g[f + "We3"].transpose(1, 0, 2).reshape(D, -1), g[f + "ws3"]], 1)),
        ("We2", down(np.concatenate([g[f + "We2"].reshape(-1, D), g[f + "ws2"]], 0))),
        ("be1", feat(np.concatenate([g[f + "be1"].ravel(), g[f + "bs1"]]))),
        ("be3", feat(np.concatenate([g[f + "be3"].ravel(), g[f + "bs3"]]))),
        ("be2", g[f + "be2"]), ("bs2", rows(g[f + "bs2"])),
    ]
    rest = [
        ("Wq", g[q + "Wq"]), ("Wk", g[q + "Wk"]), ("Wv", g[q + "Wv"]), ("Wo", down(g[q + "Wo"])),
        ("W_T", g[l + "W"].T), ("R_T", g[l + "R"].T), ("A1_T", g[l + "A"].reshape(-1, D).T),
        ("B1", g[l + "B"].transpose(0, 2, 1).reshape(-1, D)), ("b_1", rows(g[l + "b"])),
        ("qkv2", g[m + "W_qkv"].T), ("o2", g[m + "W_o"].T),
        ("qkv3", np.concatenate([g[n_ + "Wq"], g[n_ + "Wk"], g[n_ + "Wv"]], 1)),
        ("bqkv3", rows(np.concatenate([g[n_ + "bq"], g[n_ + "bk"], g[n_ + "bv"]]))),
        ("o3", g[n_ + "Wo"]), ("bo3", rows(g[n_ + "bo"])), ("Wg2", g[n_ + "Wg"]), ("bg2", rows(g[n_ + "bg"])),
        ("W1_2", g[n_ + "W1"].transpose(1, 0, 2)), ("b1_2", feat(g[n_ + "b1"].ravel())),
        ("W2_2", down(g[n_ + "W2"].reshape(-1, D))), ("b2_2", g[n_ + "b2"]),
        ("g1", rows(g[n_ + "g1"])), ("be1_2", rows(g[n_ + "be1"])), ("g2", rows(g[n_ + "g2"])), ("be2_2", rows(g[n_ + "be2"])),
        ("qkv4", g[t + "W_qkv"].T), ("o4", g[t + "W_o"].T), ("Wg3", g[k + "Wg"].T),
        ("b1_3", feat(g[k + "b1"].ravel())), ("b3_3", feat(g[k + "b3"].ravel())), ("b2_3", g[k + "b2"]),
    ]
    fold = [("W1_3", g[k + "W1"].transpose(2, 0, 1)), ("W3_3", g[k + "W3"].transpose(2, 0, 1)),
            ("W2_3", down(g[k + "W2"].transpose(0, 2, 1).reshape(-1, D))), ("LTM", feat(g[t + "W_LTM"].ravel())),
            ("A", np.stack([g[a + "A_log" + s].reshape(ND, P, NS) for s in both]).transpose(2, 0, 1, 3))]
    for name, key in (("Vgs", "V_gs"), ("VT0", "V_T0"), ("btau", "beta_tau"), ("bgm", "beta_gm"), ("Cch", "C_ch"), ("gam", "gamma")):
        fold.append((name, feat(np.repeat(g[t + key], HD * HD))))
    fold += [("ppd", rows(g[t + "alpha_ppd"])), ("ICt", rows(g[t + "IC_threshold"])),
              ("ret", np.zeros((P, NG))), ("coef", np.zeros((P, NG)))]
    wf = pack(fold + first + rest, cols, P)
    ends = cols[first[0][0]][0], cols[rest[0][0]][0], wf.shape[1]
    wb = pack(list(consts_b.items()), cols_b, P, ml_dtypes.bfloat16)
    lora = pack([("A1", g[k + "A1"].transpose(1, 0, 2)), ("B1T", g[k + "B1"].transpose(2, 0, 1)),
                 ("A3", g[k + "A3"].transpose(1, 0, 2)), ("B3T", g[k + "B3"].transpose(2, 0, 1)),
                 ("A2", g[k + "A2"].transpose(1, 0, 2)), ("B2T", g[k + "B2"].transpose(2, 0, 1))], lora_cols, R1)
    x = g[a + "x"]
    arrays = {"in_x": np.concatenate([x, np.zeros_like(x[:1])]), "in_wf": wf, "in_wb": wb, "in_lora": lora,
              "in_onehot": relative_buckets(), "in_table": np.ascontiguousarray(g[q + "rel_bias_table"])}
    nc = _bacc.Bacc("TRN2", target_bir_lowering=False, num_devices=1)
    d = {n: nc.dram_tensor(n, v.shape, mybir.dt.from_np(v.dtype), kind="ExternalInput").ap() for n, v in arrays.items()}
    out = nc.dram_tensor("out_0", x.shape, F32, kind="ExternalOutput").ap()
    bass_mk_seq(nc, d["in_x"], cols, cols_b, ends, d["in_wf"], d["in_wb"], d["in_lora"], lora_cols, d["in_onehot"], d["in_table"], out)
    r = _run(nc, [arrays], core_ids=[0])
    return r.results[0]["out_0"]
```
